# Optimizing a Trainium2 kernel written in Bass

```python
import numpy as np
import jax
import jax.numpy as jnp

def _softmax(x, axis=-1):
    return jax.nn.softmax(x, axis=axis)

def _gelu(x):
    return jax.nn.gelu(x, approximate=True)

def _silu(x):
    return jax.nn.silu(x)

def _sigmoid(x):
    return jax.nn.sigmoid(x)

def _layernorm(x, axis=-1, eps=1e-05):
    m = jnp.mean(x, axis=axis, keepdims=True)
    v = jnp.var(x, axis=axis, keepdims=True)
    return (x - m) / jnp.sqrt(v + eps)

def _scatter_add(tgt, idx, src, axis=0):
    return tgt.at[idx].add(src)

def _segment_sum(src, seg, n):
    return jax.ops.segment_sum(src, seg, n)
kernel_name = 'mk_gnn_preln_d4_gnn_r32_c21d67'

def setup_inputs(seed: int=0):
    np.random.seed(seed)
    _w = jnp.asarray

    def _rec_inputs():
        import jax
        import jax.numpy as jnp
        _gk = jax.random.key(seed)
        x = -0.0005121 + 1.001 * jax.random.normal(jax.random.fold_in(_gk, 1), (3125, 64), jnp.float32)
        src = jax.random.randint(jax.random.fold_in(_gk, 2), (100000,), 0, 3125, jnp.int32)
        dst = jax.random.randint(jax.random.fold_in(_gk, 3), (100000,), 0, 3125, jnp.int32)
        _o = jnp.argsort(dst, stable=True)
        src = src[_o]
        dst = dst[_o]
        edge_type_200 = jax.random.randint(jax.random.fold_in(_gk, 14), (100000,), 0, 200, jnp.int32)
        edge_type_8 = jax.random.randint(jax.random.fold_in(_gk, 15), (100000,), 0, 8, jnp.int32)
        edge_weight = jax.random.uniform(jax.random.fold_in(_gk, 16), (100000,), jnp.float32, 0.0, 0.999999)
        return (x, src, dst, edge_type_200, edge_type_8, edge_weight)
    x, src, dst, edge_type_200, edge_type_8, edge_weight = _rec_inputs()

    def _L0_gnn_setup():
        import jax, jax.numpy as jnp
        import numpy as np
        N = 50000
        E = 25000
        D_IN = 64
        D_OUT = 64
        key = jax.random.key(seed)
        k1, k2, k3, k4 = jax.random.split(key, 4)
        input_Z = jax.random.normal(k1, (N, D_IN), dtype=jnp.float32)
        edge_index = jax.random.randint(k2, (2, E), 0, N, dtype=jnp.int32)
        deg_inv = jax.random.uniform(k3, (N,), dtype=jnp.float32, minval=0.01, maxval=1.0)
        W = jax.random.uniform(k4, (D_IN, D_OUT), dtype=jnp.float32, minval=-0.05, maxval=0.05)
        return {'input_Z': input_Z, 'edge_index': edge_index, 'deg_inv': deg_inv, 'W': W}
    _L0_gnn_all = _L0_gnn_setup()
    _L0_gnn_in = {k: v for k, v in _L0_gnn_all.items() if k in ('W',)}
    del _L0_gnn_all

    def _L1_gnn_setup():
        import jax, jax.numpy as jnp
        import numpy as np
        N, E, D, RD, NUM_RELS = (3125, 31250, 64, 64, 200)
        NEG_SLOPE = 0.2
        key = jax.random.key(seed)
        ks = jax.random.split(key, 8)
        H = jax.random.normal(ks[0], (N, D), dtype=jnp.float32)
        src = jax.random.randint(ks[1], (E,), 0, N, dtype=jnp.int32)
        dst = jax.random.randint(ks[2], (E,), 0, N, dtype=jnp.int32)
        rel = jax.random.randint(ks[3], (E,), 0, NUM_RELS, dtype=jnp.int32)

        def xavier(k, shape):
            fan_in, fan_out = (shape[1], shape[0])
            lim = float(np.sqrt(6.0 / (fan_in + fan_out)))
            return jax.random.uniform(k, shape, jnp.float32, -lim, lim)
        W_node = xavier(ks[4], (D, D))
        W_rel = xavier(ks[5], (D, RD))
        attvec = xavier(ks[6], (1, 3 * D))
        rel_emb = xavier(ks[7], (NUM_RELS, RD))
        return {'H': H, 'W_node': W_node, 'W_rel': W_rel, 'attvec': attvec, 'rel_emb': rel_emb, 'src': src, 'dst': dst, 'rel': rel, 'num_nodes': N}
    _L1_gnn_all = _L1_gnn_setup()
    _L1_gnn_in = {k: v for k, v in _L1_gnn_all.items() if k in ('W_node', 'W_rel', 'attvec', 'rel_emb')}
    del _L1_gnn_all

    def _L2_gnn_setup():
        import jax, jax.numpy as jnp
        import numpy as np
        N_NODE = 50000
        N_EDGE = 31250
        IN_CH = 64
        HID_CH = 64
        NUM_REL = 8
        key = jax.random.key(seed)
        k1, k2, k3, k4 = jax.random.split(key, 4)
        x = jax.random.normal(k1, (N_NODE, IN_CH), dtype=jnp.float32)
        W = jax.random.normal(k2, (NUM_REL, IN_CH, HID_CH), dtype=jnp.float32)
        edge_index = jax.random.randint(k3, (2, N_EDGE), 0, N_NODE, dtype=jnp.int64)
        rel = jax.random.randint(k4, (N_EDGE,), 0, NUM_REL, dtype=jnp.int64)
        return {'x': x, 'W': W, 'edge_index': edge_index, 'rel': rel, 'num_node': N_NODE, 'num_edge': N_EDGE}
    _L2_gnn_all = _L2_gnn_setup()
    _L2_gnn_in = {k: v for k, v in _L2_gnn_all.items() if k in ('W',)}
    del _L2_gnn_all

    def _L3_gnn_setup():
        import jax, jax.numpy as jnp
        import numpy as np
        N = 3125
        E = 50000
        D = 64
        H1 = 32
        H2 = 64
        EH = 32

        def _lin(key, fan_in, fan_out, bias=True):
            k1, k2 = jax.random.split(key)
            bound = 1.0 / np.sqrt(fan_in)
            W = jax.random.uniform(k1, (fan_in, fan_out), jnp.float32, -bound, bound)
            if bias:
                b = jax.random.uniform(k2, (fan_out,), jnp.float32, -bound, bound)
                return (W, b)
            return W

        def _graph_conv(x, edge_index, edge_weight, Wrel, brel, Wroot):
            src, dst = (edge_index[0], edge_index[1])
            msg = x[src] * edge_weight[:, None]
            agg = jax.ops.segment_sum(msg, dst, num_segments=x.shape[0])
            return agg @ Wrel + brel + x @ Wroot

        def _edge_mlp(x, edge_index, edge_attr, Wf, bf, Wr, br):
            xi = x[edge_index[0]]
            xj = x[edge_index[1]]
            feat = jnp.concatenate([xi, xj, edge_attr[:, None]], axis=1)
            h = jax.nn.relu(feat @ Wf + bf)
            return (h @ Wr + br).ravel()
        key = jax.random.key(seed)
        ks = jax.random.split(key, 16)
        x = jax.random.normal(ks[0], (N, D), jnp.float32)
        edge_index = jax.random.randint(ks[1], (2, E), 0, N, jnp.int64)
        edge_attr = jax.random.uniform(ks[2], (E,), jnp.float32)
        Wrel1, brel1 = _lin(ks[3], D, H1)
        Wroot1 = _lin(ks[4], D, H1, bias=False)
        Wrel2, brel2 = _lin(ks[5], H1, H2)
        Wroot2 = _lin(ks[6], H1, H2, bias=False)
        Wrel3, brel3 = _lin(ks[7], H2, D)
        Wroot3 = _lin(ks[8], H2, D, bias=False)
        Wf1, bf1 = _lin(ks[9], 2 * D + 1, EH)
        Wr1, br1 = _lin(ks[10], EH, 1)
        Wf2, bf2 = _lin(ks[11], 2 * H1 + 1, EH)
        Wr2, br2 = _lin(ks[12], EH, 1)
        return {'x': x, 'edge_index': edge_index, 'edge_attr': edge_attr, 'Wrel1': Wrel1, 'brel1': brel1, 'Wroot1': Wroot1, 'Wrel2': Wrel2, 'brel2': brel2, 'Wroot2': Wroot2, 'Wrel3': Wrel3, 'brel3': brel3, 'Wroot3': Wroot3, 'Wf1': Wf1, 'bf1': bf1, 'Wr1': Wr1, 'br1': br1, 'Wf2': Wf2, 'bf2': bf2, 'Wr2': Wr2, 'br2': br2}
    _L3_gnn_all = _L3_gnn_setup()
    _L3_gnn_in = {k: v for k, v in _L3_gnn_all.items() if k in ('Wrel1', 'brel1', 'Wroot1', 'Wrel2', 'brel2', 'Wroot2', 'Wrel3', 'brel3', 'Wroot3', 'Wf1', 'bf1', 'Wr1', 'br1', 'Wf2', 'bf2', 'Wr2', 'br2')}
    del _L3_gnn_all
    return {'x': x, 'src': src, 'dst': dst, 'edge_type_200': edge_type_200, 'edge_type_8': edge_type_8, 'edge_weight': edge_weight, 'L0_gnn_W': _L0_gnn_in['W'], 'L1_gnn_W_node': _L1_gnn_in['W_node'], 'L1_gnn_W_rel': _L1_gnn_in['W_rel'], 'L1_gnn_attvec': _L1_gnn_in['attvec'], 'L1_gnn_rel_emb': _L1_gnn_in['rel_emb'], 'L2_gnn_W': _L2_gnn_in['W'], 'L3_gnn_Wrel1': _L3_gnn_in['Wrel1'], 'L3_gnn_brel1': _L3_gnn_in['brel1'], 'L3_gnn_Wroot1': _L3_gnn_in['Wroot1'], 'L3_gnn_Wrel2': _L3_gnn_in['Wrel2'], 'L3_gnn_brel2': _L3_gnn_in['brel2'], 'L3_gnn_Wroot2': _L3_gnn_in['Wroot2'], 'L3_gnn_Wrel3': _L3_gnn_in['Wrel3'], 'L3_gnn_brel3': _L3_gnn_in['brel3'], 'L3_gnn_Wroot3': _L3_gnn_in['Wroot3'], 'L3_gnn_Wf1': _L3_gnn_in['Wf1'], 'L3_gnn_bf1': _L3_gnn_in['bf1'], 'L3_gnn_Wr1': _L3_gnn_in['Wr1'], 'L3_gnn_br1': _L3_gnn_in['br1'], 'L3_gnn_Wf2': _L3_gnn_in['Wf2'], 'L3_gnn_bf2': _L3_gnn_in['bf2'], 'L3_gnn_Wr2': _L3_gnn_in['Wr2'], 'L3_gnn_br2': _L3_gnn_in['br2']}

def reference(x, src, dst, edge_type_200, edge_type_8, edge_weight, L0_gnn_W, L1_gnn_W_node, L1_gnn_W_rel, L1_gnn_attvec, L1_gnn_rel_emb, L2_gnn_W, L3_gnn_Wrel1, L3_gnn_brel1, L3_gnn_Wroot1, L3_gnn_Wrel2, L3_gnn_brel2, L3_gnn_Wroot2, L3_gnn_Wrel3, L3_gnn_brel3, L3_gnn_Wroot3, L3_gnn_Wf1, L3_gnn_bf1, L3_gnn_Wr1, L3_gnn_br1, L3_gnn_Wf2, L3_gnn_bf2, L3_gnn_Wr2, L3_gnn_br2):
    import jax
    import jax.numpy as jnp

    def _L0_gnn_ref(input_Z, edge_index, deg_inv, W):
        import jax, jax.numpy as jnp
        import numpy as np
        N = 50000
        E = 25000
        D_IN = 64
        D_OUT = 64
        src = edge_index[0]
        dst = edge_index[1]
        AZ = jax.ops.segment_sum(input_Z[src], dst, num_segments=input_Z.shape[0])
        AZ = AZ + input_Z
        AZW = AZ @ W
        DAZW = deg_inv[:, None] * AZW
        return jnp.tanh(DAZW)

    def _L1_gnn_ref(H, W_node, W_rel, attvec, rel_emb, src, dst, rel, num_nodes):
        import jax, jax.numpy as jnp
        import numpy as np
        N, E, D, RD, NUM_RELS = (3125, 31250, 64, 64, 200)
        NEG_SLOPE = 0.2
        Wh = H @ W_node.T
        Wr = rel_emb[rel] @ W_rel.T
        h_i = Wh[src]
        h_j = Wh[dst]
        a = attvec[0]
        e_ij = h_i @ a[:D] + h_j @ a[D:2 * D] + Wr @ a[2 * D:]
        e_ij = jax.nn.leaky_relu(e_ij, NEG_SLOPE)
        e_max = jax.ops.segment_max(e_ij, src, num_segments=num_nodes)
        alpha_num = jnp.exp(e_ij - e_max[src])
        denom = jax.ops.segment_sum(alpha_num, src, num_segments=num_nodes) + 1e-12
        alpha = alpha_num / denom[src]
        msg = h_j + Wr
        H_out = jax.ops.segment_sum(alpha[:, None] * msg, src, num_segments=num_nodes)
        return H_out

    def _L2_gnn_ref(x, W, edge_index, rel, num_node, num_edge):
        import jax, jax.numpy as jnp
        import numpy as np
        N_NODE = 50000
        N_EDGE = 31250
        IN_CH = 64
        HID_CH = 64
        NUM_REL = 8
        src = edge_index[0, :num_edge]
        dst = edge_index[1, :num_edge]
        r = rel[:num_edge]
        xw = jnp.einsum('ni,rih->rnh', x, W)
        transformed = xw[r, src]
        out = jax.ops.segment_sum(transformed, dst, num_segments=num_node)
        return out

    def _L3_gnn_ref(x, edge_index, edge_attr, Wrel1, brel1, Wroot1, Wrel2, brel2, Wroot2, Wrel3, brel3, Wroot3, Wf1, bf1, Wr1, br1, Wf2, bf2, Wr2, br2):
        import jax, jax.numpy as jnp
        import numpy as np
        N = 3125
        E = 50000
        D = 64
        H1 = 32
        H2 = 64
        EH = 32

        def _lin(key, fan_in, fan_out, bias=True):
            k1, k2 = jax.random.split(key)
            bound = 1.0 / np.sqrt(fan_in)
            W = jax.random.uniform(k1, (fan_in, fan_out), jnp.float32, -bound, bound)
            if bias:
                b = jax.random.uniform(k2, (fan_out,), jnp.float32, -bound, bound)
                return (W, b)
            return W

        def _graph_conv(x, edge_index, edge_weight, Wrel, brel, Wroot):
            src, dst = (edge_index[0], edge_index[1])
            msg = x[src] * edge_weight[:, None]
            agg = jax.ops.segment_sum(msg, dst, num_segments=x.shape[0])
            return agg @ Wrel + brel + x @ Wroot

        def _edge_mlp(x, edge_index, edge_attr, Wf, bf, Wr, br):
            xi = x[edge_index[0]]
            xj = x[edge_index[1]]
            feat = jnp.concatenate([xi, xj, edge_attr[:, None]], axis=1)
            h = jax.nn.relu(feat @ Wf + bf)
            return (h @ Wr + br).ravel()
        x1 = jax.nn.relu(_graph_conv(x, edge_index, edge_attr, Wrel1, brel1, Wroot1))
        ea1 = _edge_mlp(x, edge_index, edge_attr, Wf1, bf1, Wr1, br1)
        x2 = jax.nn.relu(_graph_conv(x1, edge_index, ea1, Wrel2, brel2, Wroot2))
        ea2 = _edge_mlp(x1, edge_index, ea1, Wf2, bf2, Wr2, br2)
        x3 = jax.nn.relu(_graph_conv(x2, edge_index, ea2, Wrel3, brel3, Wroot3))
        return x3
    edge_index = jnp.stack([src, dst])
    deg = jnp.maximum(jax.ops.segment_sum(jnp.ones(dst.shape, jnp.float32), dst, num_segments=3125), 1.0)
    deg_isqrt = deg ** (-0.5)
    h = jnp.maximum(_layernorm(x, axis=-1), 0.0)
    x = x + _L0_gnn_ref(h, edge_index, deg_isqrt, L0_gnn_W)
    h = jnp.maximum(_layernorm(x, axis=-1), 0.0)
    x = x + _L1_gnn_ref(h, L1_gnn_W_node, L1_gnn_W_rel, L1_gnn_attvec, L1_gnn_rel_emb, src, dst, edge_type_200, 3125)
    h = jnp.maximum(_layernorm(x, axis=-1), 0.0)
    x = x + _L2_gnn_ref(h, L2_gnn_W, edge_index, edge_type_8, 3125, 100000)
    h = jnp.maximum(_layernorm(x, axis=-1), 0.0)
    x = x + _L3_gnn_ref(h, edge_index, edge_weight, L3_gnn_Wrel1, L3_gnn_brel1, L3_gnn_Wroot1, L3_gnn_Wrel2, L3_gnn_brel2, L3_gnn_Wroot2, L3_gnn_Wrel3, L3_gnn_brel3, L3_gnn_Wroot3, L3_gnn_Wf1, L3_gnn_bf1, L3_gnn_Wr1, L3_gnn_br1, L3_gnn_Wf2, L3_gnn_bf2, L3_gnn_Wr2, L3_gnn_br2)
    return x

_drawn_inputs = setup_inputs


def setup_inputs(seed=0):
    import zlib

    import numpy as np

    out = dict(_drawn_inputs(seed))
    spreads = {}
    factors = {'L1_gnn_W_rel': 4.629,
     'L1_gnn_rel_emb': 8.0,
     'L3_gnn_brel1': 5.746,
     'L3_gnn_brel2': 4.105,
     'L3_gnn_brel3': 200.0,
     'L3_gnn_Wroot3': 5.201,
     'L3_gnn_bf2': 4.769}
    for name, (base, spread) in spreads.items():
        noise = np.random.default_rng([zlib.crc32(name.encode()), seed]).standard_normal(out[name].shape)
        drawn = base * np.exp(spread * noise) if base else spread * noise
        out[name] = jnp.asarray(drawn.astype(out[name].dtype))
    for name, factor in factors.items():
        out[name] = (out[name] * factor).astype(out[name].dtype)
    return out
```

```python
from contextlib import ExitStack

import concourse.bass as bass
from concourse import mybir

ALU = mybir.AluOpType
ACT = mybir.ActivationFunctionType
AX = mybir.AxisListType
F32 = mybir.dt.float32
F16 = mybir.dt.float16
BF16 = mybir.dt.bfloat16
I32 = mybir.dt.int32
U32 = mybir.dt.uint32

P = 128
N_NODES = 3125
N_EDGES = 100000
D = 64
N_REL = 200
N_TYPE = 8
H1 = 32
EH = 32
CH = -(-N_NODES // P)
NCH = CH + CH % 2
NP_ = NCH * P
FULL = N_NODES // P
TAIL = N_NODES - FULL * P
EP = 125
EC = N_EDGES // EP
RG = 8
NB = CH * CH
G = 8
MAX_TILES = (N_EDGES + (P - 1) * NB) // P
GROUPS = -(-MAX_TILES // (2 * G)) * 2
TILES = (GROUPS + 1) * G
TROWS = -(-TILES // P)
REC = 8
TW = 96
AW = 72
BANK = 512
APB = BANK // AW
NEG = -1.0e30
EPS = 1e-5
assert EP * EC == N_EDGES and EC % RG == 0 and GROUPS % 2 == 0 and EP <= P


def build(nc, i, out):
    with ExitStack() as ctx:
        program(nc, ctx, i, out)


def program(nc, ctx, i, out):
    names = iter(range(10**6))

    def sb(name, shape, dt, at=ctx):
        return at.enter_context(nc.sbuf_tensor(f"{name}_{next(names)}", shape, dt))

    def sem(name):
        return ctx.enter_context(nc.semaphore(f"{name}_{next(names)}"))

    past = sem("past")

    rec = nc.dram_tensor("rec", [P * TILES, REC], F32, kind="Internal").ap()
    rows = nc.dram_tensor("rows", [3, TILES, P], F16, kind="Internal").ap()
    offs_d = nc.dram_tensor("offs_d", [5 * TROWS, P], I32, kind="Internal").ap()
    xw = nc.dram_tensor("xw", [N_TYPE * NP_, D], F32, kind="Internal").ap()

    acc = ctx.enter_context(nc.psum_tensor("acc", [P, 4 * BANK], F32))
    work = ctx.enter_context(nc.psum_tensor("work", [P, 4 * BANK], F32))

    lane = sb("lane", [P, 1], F32)
    lane_hi = sb("lane_hi", [P, 1], F32)
    iota_n = sb("iota_n", [P, P], F32)
    ident = sb("ident", [P, P], F32)
    zeros = sb("zeros", [P, BANK], BF16)
    src_lo = sb("src_lo", [P, TILES], F32)
    dst_lo = sb("dst_lo", [P, TILES], F32)
    weight = sb("weight", [P, TILES], F32)
    typed_src = sb("typed_src", [P, TILES], U32)
    edge_a = sb("edge_a", [P, TILES], F32)
    edge_b = sb("edge_b", [P, TILES], F32)
    offs = sb("offs", [1, 5, TROWS * P], I32)
    OFF_GS, OFF_GD, OFF_AD, OFF_AS, OFF_RS = range(5)
    xs = sb("xs", [P, NCH, D], F32)
    hs = sb("hs", [P, NCH, D], F32)
    t_src = sb("t_src", [P, NCH, TW], F32)
    t_dst = sb("t_dst", [P, NCH, TW], F32)
    xt = sb("xt", [P, 2, 2, P], F32)
    cat = sb("cat", [P, NCH, P], F32)
    deg = sb("deg", [P, NCH], F32)

    t_src_f = t_src[:, :, :].rearrange("p c w -> p (c w)")
    t_dst_f = t_dst[:, :, :].rearrange("p c w -> p (c w)")
    cat_f = cat[:, :, :].rearrange("p c w -> p (c w)")

    def bank_chunks(b):
        lo, hi = b * APB, min((b + 1) * APB, NCH)
        n = hi - lo
        return lo, hi, acc[:, b * BANK:b * BANK + n * AW].rearrange("p (c w) -> p c w", w=AW)

    with ExitStack() as edges:
        bucket = sb("bucket", [EP, EC], F32, edges)
        record = sb("record", [EP, EC, REC], F32, edges)
        iota_b = sb("iota_b", [P, NB], F16, edges)
        onehot = sb("onehot", [EP, RG, NB], BF16, edges)
        ones = sb("ones", [P, P], BF16, edges)
        before = sb("before", [P, P], BF16, edges)
        notbefore = sb("notbefore", [P, P], BF16, edges)
        s_in, s_const, s_prep, s_pad, s_x = sem("s_in"), sem("s_const"), sem("s_prep"), sem("s_pad"), sem("s_x")
        with ExitStack() as tmp, nc.Block() as block:
            raw = sb("raw", [EP, 5, EC], I32, tmp)
            part = sb("part", [EP, 4, EC], I32, tmp)
            padrow = sb("padrow", [P, TILES // 8, REC], F32, tmp)

            @block.sync
            def _(sp):
                for n, name in enumerate(("src", "dst", "edge_type_200", "edge_type_8")):
                    sp.dma_start(raw[:, n, :], i[name].rearrange("(p c) -> p c", p=EP)).then_inc(s_in, 16)
                sp.dma_start(raw[:, 4, :].bitcast(F32), i["edge_weight"].rearrange("(p c) -> p c", p=EP)).then_inc(s_in, 16)
                sp.wait_ge(s_const, 3)
                sp.dma_start(xs[:, 0:FULL, :], i["x"][0:FULL * P, :].rearrange("(c p) d -> p c d", p=P)).then_inc(s_x, 16)
                sp.dma_start(xs[0:TAIL, FULL, :], i["x"][FULL * P:N_NODES, :]).then_inc(s_x, 16)
                sp.wait_ge(s_const, 5)
                rec_rows = rec.rearrange("(p t) r -> p (t r)", p=P)
                for n in range(8):
                    w = TILES // 8 * REC
                    sp.dma_start(rec_rows[:, n * w:(n + 1) * w], padrow[:, :, :].rearrange("p t r -> p (t r)")).then_inc(s_pad, 16)
                sp.wait_ge(s_pad, 16 * 8)
                sp.wait_ge(s_x, 32)

            @block.gpsimd
            def _(gp):
                gp.memset(record[:, :, 5:REC], 0.0)
                gp.memset(ones[:, :], 1.0).then_inc(s_const, 1)
                gp.memset(zeros[:, :], 0.0).then_inc(s_const, 1)
                gp.memset(xs[:, :, :], 0.0).then_inc(s_const, 1)
                gp.memset(padrow[:, :, :], 0.0).then_inc(s_const, 1)
                gp.wait_ge(s_const, 4)
                gp.memset(padrow[:, :, 0:3], -1.0).then_inc(s_const, 1)
                gp.iota(iota_n[:, :], pattern=[[1, P]], base=0, channel_multiplier=0, allow_small_or_imprecise_dtypes=True)
                gp.iota(lane[:, :], pattern=[[0, 1]], base=0, channel_multiplier=1, allow_small_or_imprecise_dtypes=True)
                gp.iota(lane_hi[:, :], pattern=[[0, 1]], base=P, channel_multiplier=1, allow_small_or_imprecise_dtypes=True)
                gp.iota(iota_b[:, :], pattern=[[1, NB]], base=0, channel_multiplier=0, allow_small_or_imprecise_dtypes=True)
                gp.memset(onehot[:, :, :], 0.0).then_inc(s_const, 1)

            @block.vector
            def _(ve):
                n = 0
                ve.wait_ge(s_in, 16 * 5)
                for j in range(2):
                    ve.tensor_scalar(part[:, j, :], raw[:, j, :], P - 1, None, ALU.bitwise_and).then_inc(s_prep, 1)
                    ve.tensor_scalar(part[:, 2 + j, :], raw[:, j, :], 7, None, ALU.arith_shift_right).then_inc(s_prep, 1)
                ve.wait_ge(s_prep, 4)
                for j in range(2):
                    ve.tensor_copy(record[:, :, j], part[:, j, :])
                ve.tensor_copy(record[:, :, 2], raw[:, 2, :])
                ve.tensor_copy(record[:, :, 3], raw[:, 4, :].bitcast(F32))
                ve.scalar_tensor_tensor(out=record[:, :, 4], in0=raw[:, 3, :], scalar=float(NP_), in1=raw[:, 0, :],
                                        op0=ALU.mult, op1=ALU.add)
                ve.scalar_tensor_tensor(out=bucket[:, :], in0=part[:, 2, :], scalar=float(CH), in1=part[:, 3, :],
                                        op0=ALU.mult, op1=ALU.add)
                ve.wait_ge(s_const, 6)
                ve.tensor_scalar(ident[:, :], iota_n[:, :], lane[:, 0:1], None, ALU.is_equal)
                ve.tensor_scalar(before[:, :], iota_n[:, :], lane[:, 0:1], None, ALU.is_gt)
                ve.tensor_scalar(notbefore[:, :], iota_n[:, :], lane[:, 0:1], None, ALU.is_le)
                ve.memset(hs[:, :, :], 0.0)
                ve.memset(xt[:, :, :, :], 0.0)
                ve.memset(cat[:, :, :], 0.0)
                ve.memset(t_src[:, :, :], 0.0)
                ve.memset(t_dst[:, :, :], 0.0)

        h_made = [sem(f"h_made{s}") for s in range(2)]
        h_used = [sem(f"h_used{s}") for s in range(2)]
        with nc.Block() as block:
            @block.vector
            def _(ve):
                with ve.Fori(0, EC // 2) as t:
                    for s in range(2):
                        ve.wait_ge(h_used[s], t)
                        ve.tensor_scalar(onehot[:, s, :], iota_b[0:EP, :], bucket[:, bass.ds(2 * t + s, 1)], None,
                                         ALU.is_equal).then_inc(h_made[s], 1)

            @block.tensor
            def _(pe):
                for b in range(2):
                    pe.matmul(work[:, b * BANK:(b + 1) * BANK], zeros[:, 0:P], zeros[:, :], start=True, stop=True)
                with pe.Fori(0, EC // 2) as t:
                    for s in range(2):
                        pe.wait_ge(h_made[s], t + 1)
                        pe.matmul(work[:, 0:BANK], ones[0:EP, :], onehot[:, s, 0:BANK], start=False, stop=False, skip_group_check=True)
                        pe.matmul(work[:, BANK:NB], ones[0:EP, :], onehot[:, s, BANK:NB], start=False, stop=False,
                                  skip_group_check=True).then_inc(h_used[s], 1)

        with ExitStack() as tmp:
            base_hi = sb("base_hi", [1, NB], BF16, edges)
            base_lo = sb("base_lo", [1, NB], BF16, edges)
            ni = sb("ni", [P, NB], I32, tmp)
            nt = sb("nt", [P, NB], F32, tmp)
            one_f = sb("one_f", [P, NB], F32, tmp)
            ends = sb("ends", [P, NB], F32, tmp)
            starts = sb("starts", [P, NB], I32, tmp)
            st_a = sb("st_a", [1, NB], I32, tmp)
            less = sb("less", [P, NB], F32, tmp)
            tile_no = sb("tile_no", [P, TROWS], F32, tmp)
            tb = sb("tb", [P, TROWS], F32, tmp)
            steps = sb("steps", [P, CH - 1], F32, tmp)
            ge = sb("ge", [P, TROWS, CH - 1], F32, tmp)
            tcs = sb("tcs", [P, 2, TROWS], F32, tmp)
            tbank = sb("tbank", [P, 2, TROWS], F32, tmp)
            fld = sb("fld", [P, 5, TROWS], F32, tmp)
            fld_t = sb("fld_t", [5 * TROWS, P], I32, tmp)
            s_i, s_v, s_t, s_c, s_o = sem("s_i"), sem("s_v"), sem("s_t"), sem("s_c"), sem("s_o")
            with nc.Block() as block:
                @block.gpsimd
                def _(gp):
                    gp.iota(tile_no[:, :], pattern=[[P, TROWS]], base=0, channel_multiplier=1, allow_small_or_imprecise_dtypes=True)
                    gp.iota(steps[:, :], pattern=[[1, CH - 1]], base=1, channel_multiplier=0, allow_small_or_imprecise_dtypes=True)
                    gp.memset(one_f[:, :], 1.0).then_inc(s_i, 1)

                @block.vector
                def _(ve):
                    n = 0

                    def step(op):
                        nonlocal n
                        op.then_inc(s_v, 1)
                        n += 1
                        ve.wait_ge(s_v, n)

                    ve.wait_ge(s_i, 1)
                    step(ve.tensor_scalar(ni[:, :], work[:, 0:NB], float(P - 1), None, ALU.add))
                    step(ve.tensor_scalar(starts[:, :], ni[:, :], 7, None, ALU.arith_shift_right))
                    step(ve.tensor_copy(nt[:, :], starts[:, :]))
                    step(ve.tensor_tensor_scan(ends[:, :], one_f[:, :], nt[:, :], 0.0, ALU.mult, ALU.add))
                    step(ve.tensor_tensor(starts[:, :], ends[:, :], nt[:, :], ALU.subtract))
                    step(ve.tensor_scalar(st_a[:, :], starts[0:1, :], 31, None, ALU.bitwise_and))
                    step(ve.tensor_scalar(base_lo[:, :], st_a[:, :], float(P), None, ALU.mult))
                    step(ve.tensor_scalar(st_a[:, :], starts[0:1, :], 5, None, ALU.arith_shift_right))
                    step(ve.tensor_scalar(base_hi[:, :], st_a[:, :], float(32 * P), None, ALU.mult))
                    for k in range(TROWS):
                        step(ve.tensor_scalar(less[:, :], ends[:, :], tile_no[:, k:k + 1], None, ALU.is_le))
                        step(ve.tensor_reduce(tb[:, k:k + 1], less[:, :], AX.X, ALU.add))
                    step(ve.tensor_scalar(tb[:, :], tb[:, :], float(NB - 1), None, ALU.min))
                    step(ve.tensor_scalar(less[:, 0:CH - 1], steps[:, :], float(CH), None, ALU.mult))
                    step(ve.tensor_tensor(ge[:, :, :], tb[:, :].unsqueeze(2).to_broadcast([P, TROWS, CH - 1]),
                                          less[:, 0:CH - 1].unsqueeze(1).to_broadcast([P, TROWS, CH - 1]), ALU.is_ge))
                    step(ve.tensor_reduce(tcs[:, 0, :], ge[:, :, :], AX.X, ALU.add))
                    step(ve.scalar_tensor_tensor(out=tcs[:, 1, :], in0=tcs[:, 0, :], scalar=-float(CH), in1=tb[:, :],
                                                 op0=ALU.mult, op1=ALU.add))
                    nb = CH // APB
                    step(ve.tensor_scalar(less[:, 0:nb], steps[:, 0:nb], float(APB), None, ALU.mult))
                    for j in range(2):
                        step(ve.tensor_tensor(ge[:, :, 0:nb], tcs[:, j, :].unsqueeze(2).to_broadcast([P, TROWS, nb]),
                                              less[:, 0:nb].unsqueeze(1).to_broadcast([P, TROWS, nb]), ALU.is_ge))
                        step(ve.tensor_reduce(tbank[:, j, :], ge[:, :, 0:nb], AX.X, ALU.add))
                    step(ve.tensor_scalar(tbank[:, :, :], tbank[:, :, :], float(BANK - APB * AW), None, ALU.mult))
                    for j, f in ((0, OFF_GS), (1, OFF_GD)):
                        step(ve.tensor_scalar(fld[:, f, :], tcs[:, j, :], float(TW), None, ALU.mult))
                    step(ve.tensor_scalar(fld[:, OFF_RS, :], tcs[:, 0, :], float(P), None, ALU.mult))
                    for j, f in ((0, OFF_AS), (1, OFF_AD)):
                        step(ve.scalar_tensor_tensor(out=fld[:, f, :], in0=tcs[:, j, :], scalar=float(AW), in1=tbank[:, j, :],
                                                     op0=ALU.mult, op1=ALU.add))
                    ve.sem_inc(s_t, 1)
                    ve.wait_ge(s_t, 2)
                    ve.tensor_copy(fld_t[:, :], work[0:5 * TROWS, 3 * BANK:3 * BANK + P]).then_inc(s_c, 1)

                @block.tensor
                def _(pe):
                    pe.wait_ge(s_t, 1)
                    pe.transpose(work[0:5 * TROWS, 3 * BANK:3 * BANK + P], fld[:, :, :].rearrange("p f t -> p (f t)"),
                                 ident[:, :]).then_inc(s_t, 1)

                @block.sync
                def _(sp):
                    sp.wait_ge(s_c, 1)
                    sp.dma_start(offs_d, fld_t[:, :]).then_inc(s_o, 16)
                    sp.wait_ge(s_o, 16)
                    sp.dma_start(offs[:, :, :], offs_d.rearrange("(o f t) p -> o f (t p)", o=1, f=5)).then_inc(s_o, 16)
                    sp.wait_ge(s_o, 32)

        with ExitStack() as tmp:
            junk = sb("junk", [EP, NB], BF16, tmp)
            place = sb("place", [EP, RG], F32, tmp)
            place_i = sb("place_i", [EP, RG], I32, tmp)
            place_lane = sb("place_lane", [EP, RG], I32, tmp)
            place_tile = sb("place_tile", [EP, RG], I32, tmp)
            address = sb("address", [EP, RG], U32, tmp)
            staged = sb("staged", [EP, RG, REC], F32, tmp)
            r_made, r_ready, r_read, r_step = sem("r_made"), sem("r_ready"), sem("r_read"), sem("r_step")
            r_staged, r_sent = sem("r_staged"), sem("r_sent")
            with nc.Block() as block:
                @block.vector
                def _(ve):
                    with ve.Fori(0, EC // RG) as t:
                        def mark(k):
                            ve.tensor_scalar(onehot[:, k, :], iota_b[0:EP, :], bucket[:, bass.ds(RG * t + k, 1)], None,
                                             ALU.is_equal).then_inc(r_made, 1)

                        mark(0)
                        for k in range(RG):
                            if k + 1 < RG:
                                mark(k + 1)
                            ve.wait_ge(r_ready, RG * t + k + 1)
                            if k == 0:
                                ve.wait_ge(r_made, RG * t + 1)
                            ve.tensor_tensor_reduce(junk[:, :], onehot[:, k, :], work[0:EP, 0:NB], 1.0, 0.0, ALU.mult,
                                                    ALU.add, place[:, k:k + 1]).then_inc(r_read, 1)
                            ve.wait_ge(r_made, RG * t + min(k + 2, RG))
                        ve.wait_ge(r_read, RG * t + RG)
                        ve.tensor_copy(place_i[:, :], place[:, :]).then_inc(r_step, 1)
                        ve.wait_ge(r_step, 3 * t + 1)
                        ve.tensor_scalar(place_lane[:, :], place_i[:, :], P - 1, None, ALU.bitwise_and).then_inc(r_step, 1)
                        ve.tensor_scalar(place_tile[:, :], place_i[:, :], 7, None, ALU.arith_shift_right).then_inc(r_step, 1)
                        ve.wait_ge(r_step, 3 * t + 3)
                        ve.wait_ge(r_sent, 16 * RG * t)
                        ve.scalar_tensor_tensor(out=address[:, :], in0=place_lane[:, :], scalar=float(TILES), in1=place_tile[:, :],
                                                op0=ALU.mult, op1=ALU.add)
                        ve.tensor_copy(staged[:, :, :], record[:, bass.ds(RG * t, RG), :]).then_inc(r_staged, 1)

                @block.tensor
                def _(pe):
                    def add(which, k):
                        pe.matmul(work[:, 0:BANK], which, onehot[:, k, 0:BANK], start=False, stop=False, skip_group_check=True)
                        return pe.matmul(work[:, BANK:NB], which, onehot[:, k, BANK:NB], start=False, stop=False, skip_group_check=True)

                    for b in range(2):
                        lo, hi = b * BANK, min((b + 1) * BANK, NB)
                        pe.matmul(work[:, b * BANK:(b + 1) * BANK], zeros[:, 0:P], zeros[:, :], start=True, stop=True)
                        for part in (base_hi, base_lo):
                            pe.matmul(work[:, lo:hi], ones[0:1, :], part[0:1, lo:hi], start=False, stop=False, skip_group_check=True)
                    with pe.Fori(0, EC // RG) as t:
                        for k in range(RG):
                            pe.wait_ge(r_read, RG * t + k)
                            add(notbefore[0:EP, :], (k - 1) % RG)
                            pe.wait_ge(r_made, RG * t + k + 1)
                            add(before[0:EP, :], k).then_inc(r_ready, 1)

                @block.gpsimd
                def _(gp):
                    with gp.Fori(0, EC // RG) as t:
                        gp.wait_ge(r_staged, t + 1)
                        gp.sem_inc(past, 1)
                        for k in range(RG):
                            gp.indirect_dma_start(out=rec, out_offset=bass.IndirectOffsetOnAxis(ap=address[:, k:k + 1], axis=0),
                                                  in_=staged[:, k, :], in_offset=None).then_inc(r_sent, 16)
                        gp.wait_ge(r_sent, 16 * RG * t + 16 * RG)

    with ExitStack() as tmp:
        allrec = sb("allrec", [P, TILES, REC], F32, tmp)
        row_sb = sb("row_sb", [P, 2, 3 * P], F16, tmp)
        s_l, s_u, s_w = sem("s_l"), sem("s_u"), sem("s_w")
        s_tp = [sem(f"s_tp{s}") for s in range(2)]
        s_cp = [sem(f"s_cp{s}") for s in range(2)]
        s_wr = [sem(f"s_wr{s}") for s in range(2)]
        spans = [(a, min(a + P, TILES)) for a in range(0, TILES, P)]
        with nc.Block() as block:
            @block.sync
            def _(sp):
                sp.dma_start(allrec[:, :, :], rec.rearrange("(p t) r -> p t r", p=P)).then_inc(s_l, 16)
                for n, (a, b) in enumerate(spans):
                    sp.wait_ge(s_cp[n % 2], n // 2 + 1)
                    sp.dma_start(rows[:, a:b, :].rearrange("f t e -> t f e"),
                                 row_sb[0:b - a, n % 2, :].rearrange("t (f e) -> t f e", f=3)).then_inc(s_wr[n % 2], 16)
                for s in range(2):
                    sp.wait_ge(s_wr[s], 16 * ((len(spans) + 1 - s) // 2))

            @block.tensor
            def _(pe):
                pe.wait_ge(s_l, 16)
                for n, (a, b) in enumerate(spans):
                    pe.wait_ge(s_cp[n % 2], n // 2)
                    for f in range(3):
                        mm = pe.transpose(work[0:b - a, (n % 2) * BANK + f * P:(n % 2) * BANK + (f + 1) * P],
                                          allrec[:, a:b, f], ident[:, :])
                    mm.then_inc(s_tp[n % 2], 1)

            @block.scalar
            def _(ac):
                for n, (a, b) in enumerate(spans):
                    ac.wait_ge(s_tp[n % 2], n // 2 + 1)
                    if n >= 2:
                        ac.wait_ge(s_wr[n % 2], 16 * (n // 2))
                    ac.copy(row_sb[0:b - a, n % 2, :], work[0:b - a, (n % 2) * BANK:(n % 2) * BANK + 3 * P]).then_inc(s_cp[n % 2], 1)

            @block.vector
            def _(ve):
                ve.wait_ge(s_l, 16)
                ve.tensor_copy(src_lo[:, :], allrec[:, :, 0])
                ve.tensor_copy(dst_lo[:, :], allrec[:, :, 1])
                ve.tensor_copy(weight[:, :], allrec[:, :, 3])
                ve.tensor_copy(typed_src[:, :], allrec[:, :, 4])

    marks = sb("marks", [P, 2, 4, G * P], F32)
    bcast = sb("bcast", [P, 2, 3, G * P], F16)
    pick = sb("pick", [P, 2, G, P], F32)
    msg = sb("msg", [P, 2, G, AW], F32)
    small = sb("small", [P, 2, 4, G], F32)
    wide = sb("wide", [P, 2, BANK], F32)
    biases = sb("biases", [P, 8, D], F32)
    w_sb = sb("w_sb", [P, BANK], F32)
    gath = [work[:, 2 * s * BANK:2 * (s + 1) * BANK].rearrange("p (t w) -> p t w", w=P) for s in range(2)]
    column = {"src": src_lo, "dst": dst_lo}
    acc_off = {"src": OFF_AS, "dst": OFF_AD}
    ACC_MAX = (CH - 1) * AW + (CH - 1) // APB * (BANK - APB * AW)

    def offsets(eng, field, group, regs, most):
        eng.load(regs, offs[0:1, field, bass.ds(G * group, G)])
        return [eng.snap(r, min_val=0, max_val=most) for r in regs]

    def clear_acc(pe):
        for b in range(4):
            pe.matmul(acc[:, b * BANK:(b + 1) * BANK], zeros[:, 0:P], zeros[:, :], start=True, stop=True)

    m_loaded, m_marked, m_gathered, m_msg, m_picked, m_added, m_part, m_diff, m_kept = (
        [sem(f"m_{what}{s}") for s in range(2)]
        for what in ("loaded", "marked", "gathered", "msg", "picked", "added", "part", "diff", "kept"))
    m_step = sem("m_step")
    pass_sems = [m for pair in (m_loaded, m_marked, m_gathered, m_msg, m_picked, m_added, m_part, m_diff, m_kept) for m in pair]
    pass_sems.append(m_step)
    counted = {"pass": 0, "linear": 0, "sent": 0, "load": 0, "ve": 0, "ac": 0}

    def edge_pass(name, fields, into, width, gathers, kind, w=None, mlp=None):
        need_rows = sorted({f[0] for f in fields})
        if counted["pass"]:
            with nc.Block() as block:
                @block.gpsimd
                def _(gp):
                    for m in pass_sems:
                        gp.sem_clear(m)
        counted["pass"] += 1

        with nc.Block() as block:
            @block.sync
            def _(sp):
                def load(g, s, k):
                    sp.wait_ge(m_marked[s], k)
                    for f in need_rows:
                        sp.dma_start(bcast[:, s, f, :], rows[f, bass.ds(G * g, G), :].rearrange("(o t) e -> o (t e)", o=1)
                                     .to_broadcast([P, G * P])).then_inc(m_loaded[s], 16)

                load(0, 0, 0)
                with sp.Fori(0, GROUPS // 2) as t:
                    load(2 * t + 1, 1, t)
                    load(2 * t + 2, 0, t + 1)

            @block.vector
            def _(ve):
                def mark(s, k):
                    ve.wait_ge(m_loaded[s], 16 * len(need_rows) * (k + 1))
                    ve.wait_ge(m_gathered[s], k)
                    for n, (f, high) in enumerate(fields):
                        op = ve.tensor_scalar(marks[:, s, n, :], bcast[:, s, f, :], (lane_hi if high else lane)[:, 0:1], None,
                                              ALU.is_equal)
                    op.then_inc(m_marked[s], 1)

                def message(g, s, k):
                    ve.wait_ge(m_gathered[s], k + 1)
                    if kind == "weighted":
                        ve.wait_ge(m_added[s], k)
                        op = ve.tensor_tensor(msg[:, s, :, 0:width], gath[s][:, :, 0:width],
                                              w[:, bass.ds(G * g, G)].unsqueeze(2).to_broadcast([P, G, width]), ALU.mult)
                        if mlp is None:
                            op.then_inc(m_msg[s], 1)
                            return
                        w_row, w_out, b_out, dest = mlp
                        n0 = 4 * g
                        hid = wide[:, s, 0:G * EH].rearrange("p (t h) -> p t h", h=EH)
                        ve.wait_ge(m_part[s], k + 1)
                        ve.tensor_tensor(hid, hid, gath[s][:, :, width:width + EH], ALU.add).then_inc(m_step, 1)
                        ve.wait_ge(m_step, n0 + 1)
                        ve.scalar_tensor_tensor(out=hid, in0=hid, scalar=0.0, in1=w_out.unsqueeze(1).to_broadcast([P, G, EH]),
                                                op0=ALU.max, op1=ALU.mult).then_inc(m_step, 1)
                        ve.wait_ge(m_step, n0 + 2)
                        ve.tensor_reduce(small[:, s, 0, :], hid, AX.X, ALU.add).then_inc(m_step, 1)
                        ve.wait_ge(m_step, n0 + 3)
                        ve.tensor_scalar(dest[:, bass.ds(G * g, G)], small[:, s, 0, :], b_out, None, ALU.add).then_inc(m_msg[s], 1)
                        ve.sem_inc(m_step, 1)
                    elif kind == "maximum":
                        regs = offsets(ve, OFF_RS, g, max_regs, (CH - 1) * P)
                        ve.wait_ge(m_kept[s], k)
                        ve.tensor_copy(small[:, s, 1, :], gath[s][:, :, 0]).then_inc(m_step, 1)
                        ve.wait_ge(m_step, (G + 2) * g + 1)
                        ve.scalar_tensor_tensor(out=small[:, s, 0, :], in0=small[:, s, 1, :], scalar=0.2,
                                                in1=small[:, s, 1, :], op0=ALU.mult, op1=ALU.max).then_inc(m_step, 1)
                        ve.wait_ge(m_step, (G + 2) * g + 2)
                        ve.sem_inc(m_part[s], 1)
                        ve.wait_ge(m_picked[s], k + 1)
                        for j in range(G):
                            top = cat_f[:, bass.ds(regs[j], P)]
                            op = ve.scalar_tensor_tensor(out=top, in0=pick[:, s, j, :], scalar=small[:, s, 0, j:j + 1], in1=top,
                                                         op0=ALU.add, op1=ALU.max)
                            op.then_inc(m_step, 1)
                            ve.wait_ge(m_step, (G + 2) * g + 3 + j)
                        ve.sem_inc(m_msg[s], 1)
                    elif kind == "softmax":
                        ve.wait_ge(m_msg[s], k)
                        ve.tensor_tensor(small[:, s, 0, :], edge_a[:, bass.ds(G * g, G)], gath[s][:, :, D + 1],
                                         ALU.subtract).then_inc(m_part[s], 1)

                if kind == "maximum":
                    max_regs = [ve.alloc_register(f"{name}_off{j}") for j in range(G)]
                    ve.memset(cat[:, :, :], NEG)
                mark(0, 0)
                with ve.Fori(0, GROUPS // 2) as t:
                    mark(1, t)
                    message(2 * t, 0, t)
                    mark(0, t + 1)
                    message(2 * t + 1, 1, t)

            @block.gpsimd
            def _(gp):
                def choose(g, s, k):
                    gp.wait_ge(m_msg[s] if kind == "maximum" else m_added[s], k)
                    gp.tensor_tensor(pick[:, s, :, :], iota_n[:, :].unsqueeze(1).to_broadcast([P, G, P]),
                                     column[into][:, bass.ds(G * g, G)].unsqueeze(2).to_broadcast([P, G, P]),
                                     ALU.subtract).then_inc(m_diff[s], 1)
                    gp.wait_ge(m_diff[s], k + 1)
                    gp.sem_inc(past, 1)
                    if kind == "maximum":
                        gp.tensor_scalar(pick[:, s, :, :], pick[:, s, :, :], 0.0, -1.0, ALU.is_equal, ALU.add).then_inc(m_added[s], 1)
                        gp.wait_ge(m_added[s], k + 1)
                        gp.sem_inc(past, 1)
                        op = gp.tensor_scalar(pick[:, s, :, :], pick[:, s, :, :], -NEG, None, ALU.mult)
                    else:
                        op = gp.tensor_scalar(pick[:, s, :, :], pick[:, s, :, :], 0.0, None, ALU.is_equal)
                    op.then_inc(m_picked[s], 1)
                    if kind == "maximum":
                        gp.wait_ge(m_part[s], k + 1)
                        gp.tensor_copy(edge_a[:, bass.ds(G * g, G)], small[:, s, 0, :]).then_inc(m_kept[s], 1)
                    if mlp is not None:
                        gp.wait_ge(m_msg[s], k)
                        gp.tensor_tensor(wide[:, s, 0:G * EH].rearrange("p (t h) -> p t h", h=EH),
                                         w[:, bass.ds(G * g, G)].unsqueeze(2).to_broadcast([P, G, EH]),
                                         mlp[0].unsqueeze(1).to_broadcast([P, G, EH]), ALU.mult).then_inc(m_part[s], 1)

                with gp.Fori(0, GROUPS // 2) as t:
                    for s in range(2):
                        choose(2 * t + s, s, t)

            @block.scalar
            def _(ac):
                if kind not in ("plain", "softmax"):
                    return
                with ac.Fori(0, GROUPS // 2) as t:
                    for s in range(2):
                        if kind == "plain":
                            ac.wait_ge(m_gathered[s], t + 1)
                            ac.wait_ge(m_added[s], t)
                            ac.copy(msg[:, s, :, 0:width], gath[s][:, :, 0:width]).then_inc(m_msg[s], 1)
                        else:
                            ac.wait_ge(m_part[s], t + 1)
                            ac.activation(small[:, s, 1, :], small[:, s, 0, :], ACT.Exp).then_inc(m_kept[s], 1)
                            ac.wait_ge(m_kept[s], t + 1)
                            ac.wait_ge(m_added[s], t)
                            for j in range(G):
                                op = ac.activation(msg[:, s, j, 0:width], gath[s][:, j, 0:width], ACT.Copy, scale=small[:, s, 1, j:j + 1])
                            op.then_inc(m_msg[s], 1)

            @block.tensor
            def _(pe):
                regs = [pe.alloc_register(f"{name}_r{j}") for j in range(G)]
                regs2 = [pe.alloc_register(f"{name}_q{j}") for j in range(G)]
                kinds = sorted({gt[1] for gt in gathers if gt[1] is not None})

                def gather(g, s, k):
                    pe.wait_ge(m_marked[s], k + 1)
                    pe.wait_ge(m_msg[s], k)
                    at = {f: offsets(pe, f, g, r, (CH - 1) * TW) for f, r in zip(kinds, (regs, regs2))}
                    for j in range(G):
                        for mark_n, field, table, first, n, col, start, stop in gathers:
                            rhs = table[:, first:first + n] if field is None else table[:, bass.ds(at[field][j] + first, n)]
                            mm = pe.matmul(gath[s][:, j, col:col + n], marks[:, s, mark_n, j * P:(j + 1) * P], rhs,
                                           start=start, stop=stop)
                    mm.then_inc(m_gathered[s], 1)

                def add(g, s, k):
                    if kind == "maximum":
                        return
                    pe.wait_ge(m_msg[s], k + 1)
                    pe.wait_ge(m_picked[s], k + 1)
                    at = offsets(pe, acc_off[into], g, regs, ACC_MAX)
                    for j in range(G):
                        mm = pe.matmul(acc[:, bass.ds(at[j], width)], pick[:, s, j, :], msg[:, s, j, 0:width],
                                       start=False, stop=False, skip_group_check=True)
                    mm.then_inc(m_added[s], 1)

                if kind != "maximum":
                    clear_acc(pe)
                gather(0, 0, 0)
                with pe.Fori(0, GROUPS // 2) as t:
                    gather(2 * t + 1, 1, t)
                    add(2 * t, 0, t)
                    gather(2 * t + 2, 0, t + 1)
                    add(2 * t + 1, 1, t)
                for r in regs + regs2:
                    pe.free_register(r)

    l_in, l_tp, l_xt, l_mm, l_out, l_sent = ([sem(f"l_{what}{s}") for s in range(2)]
                                             for what in ("in", "tp", "xt", "mm", "out", "sent"))
    s_ld, s_ve, s_ac = sem("s_ld"), sem("s_ve"), sem("s_ac")

    def linear(name, x, k_dim, m, finish, store=None, chunks=NCH):
        c0 = counted["linear"]
        counted["linear"] += chunks // 2
        sent0 = counted["sent"]
        if store is not None:
            counted["sent"] += 16 * (chunks // 2)
        turned = [work[:, s * BANK:s * BANK + P] for s in range(2)]
        product = [work[:, (2 + s) * BANK:(2 + s) * BANK + m] for s in range(2)]
        with nc.Block() as block:
            @block.scalar
            def _(ac):
                with ac.Fori(0, chunks // 2) as t:
                    for s in range(2):
                        ac.wait_ge(l_tp[s], t + c0)
                        ac.copy(xt[:, s, 0, 0:k_dim], x(2 * t + s)).then_inc(l_in[s], 1)
                    for s in range(2):
                        ac.wait_ge(l_tp[s], t + c0 + 1)
                        ac.wait_ge(l_mm[s], t + c0)
                        ac.copy(xt[0:k_dim, s, 1, :], turned[s][0:k_dim, :]).then_inc(l_xt[s], 1)

            @block.tensor
            def _(pe):
                with pe.Fori(0, chunks // 2) as t:
                    for s in range(2):
                        pe.wait_ge(l_in[s], t + c0 + 1)
                        pe.wait_ge(l_xt[s], t + c0)
                        pe.transpose(turned[s], xt[:, s, 0, :], ident[:, :]).then_inc(l_tp[s], 1)
                    for s in range(2):
                        pe.wait_ge(l_xt[s], t + c0 + 1)
                        pe.wait_ge(l_out[s], t + c0)
                        pe.matmul(product[s], xt[0:k_dim, s, 1, :], w_sb[0:k_dim, 0:m], start=True, stop=True).then_inc(l_mm[s], 1)

            @block.vector
            def _(ve):
                with ve.Fori(0, chunks // 2) as t:
                    for s in range(2):
                        ve.wait_ge(l_mm[s], t + c0 + 1)
                        if store is not None:
                            ve.wait_ge(l_sent[s], 16 * t + sent0)
                        finish(ve, 2 * t + s, s, product[s]).then_inc(l_out[s], 1)

            if store is not None:
                @block.sync
                def _(sp):
                    with sp.Fori(0, chunks // 2) as t:
                        for s in range(2):
                            sp.wait_ge(l_out[s], t + c0 + 1)
                            store(sp, 2 * t + s, s).then_inc(l_sent[s], 16)
                    for s in range(2):
                        sp.wait_ge(l_sent[s], 16 * (chunks // 2) + sent0)

    def load_block(name, loads):
        counted["load"] += 16 * len(loads)
        with nc.Block() as block:
            @block.sync
            def _(sp):
                for dest, what in loads:
                    sp.dma_start(dest, what).then_inc(s_ld, 16)
                sp.wait_ge(s_ld, counted["load"])

    def node_block(name, body, act=None):
        ve0, ac1 = counted["ve"], counted["ac"] + 1
        counted["ac"] += act is not None
        with nc.Block() as block:
            @block.vector
            def _(ve):
                n = ve0
                for op in body(ve):
                    if op is None:
                        ve.wait_ge(s_ac, ac1)
                        continue
                    op.then_inc(s_ve, 1)
                    n += 1
                    ve.wait_ge(s_ve, n)
                counted["ve"] = n

            if act is not None:
                after, op = act
                @block.scalar
                def _(ac):
                    ac.wait_ge(s_ve, ve0 + after)
                    op(ac).then_inc(s_ac, 1)

    def layernorm(name, before=()):
        mean, ssq = stat[:, 0, :], stat[:, 1, :]

        def body(ve):
            for f in before:
                yield f(ve)
            yield ve.tensor_reduce(mean, xs[:, :, :], AX.X, ALU.add)
            yield ve.tensor_scalar(mean, mean, 1.0 / D, None, ALU.mult)
            yield ve.tensor_tensor(hs[:, :, :], xs[:, :, :], mean.unsqueeze(2).to_broadcast([P, NCH, D]), ALU.subtract)
            yield ve.tensor_tensor(cat[:, :, 0:D], hs[:, :, :], hs[:, :, :], ALU.mult)
            yield ve.tensor_reduce(ssq, cat[:, :, 0:D], AX.X, ALU.add)
            yield ve.tensor_scalar(ssq, ssq, 1.0 / D, EPS, ALU.mult, ALU.add)
            yield None
            yield ve.reciprocal(ssq, mean)
            yield ve.tensor_tensor(hs[:, :, :], hs[:, :, :], ssq.unsqueeze(2).to_broadcast([P, NCH, D]), ALU.mult)
            yield ve.tensor_scalar(hs[:, :, :], hs[:, :, :], 0.0, None, ALU.max)

        node_block(name, body, (len(before) + 6, lambda ac: ac.activation(mean, ssq, ACT.Sqrt)))

    stat = sb("stat", [P, 2, NCH], F32)
    all_nodes = lambda ap, w: ap.unsqueeze(1).to_broadcast([P, NCH, w])

    w0 = i["L0_gnn_W"]
    layernorm("ln0")

    def tables0(ve):
        yield ve.tensor_copy(t_src[:, :, 0:D], hs[:, :, :])
        yield ve.memset(t_src[:, :, D:D + 1], 1.0)
    node_block("tables0", tables0)
    edge_pass("l0", [(0, False)], "dst", D + 1, [(0, OFF_GS, t_src_f, 0, D + 1, 0, True, True)], "plain")
    load_block("w0", [(w_sb[0:D, 0:D], w0)])

    def after0(ve):
        for b in range(4):
            lo, hi, a = bank_chunks(b)
            if lo < hi:
                yield ve.tensor_tensor(hs[:, lo:hi, :], hs[:, lo:hi, :], a[:, :, 0:D], ALU.add)
                yield ve.tensor_scalar(deg[:, lo:hi], a[:, :, D], 1.0, None, ALU.max)
        yield None
        yield ve.reciprocal(deg[:, :], stat[:, 0, :])
    banks = sum(bank_chunks(b)[0] < bank_chunks(b)[1] for b in range(4))
    node_block("after0", after0, (2 * banks, lambda ac: ac.activation(stat[:, 0, :], deg[:, :], ACT.Sqrt)))
    linear("lin0", lambda c: hs[:, bass.ds(c, 1), :].rearrange("p a d -> p (a d)"), D, D,
           lambda ve, c, s, y: ve.tensor_scalar(cat[:, bass.ds(c, 1), 0:D].rearrange("p a d -> p (a d)"), y,
                                                deg[:, bass.ds(c, 1)], None, ALU.mult))
    s_tanh = sem("s_tanh")
    with nc.Block() as block:
        @block.scalar
        def _(ac):
            ac.activation(hs[:, :, :], cat[:, :, 0:D], ACT.Tanh).then_inc(s_tanh, 1)

    layernorm("ln1", [lambda ve: ve.tensor_tensor(xs[:, :, :], xs[:, :, :], hs[:, :, :], ALU.add)])
    rel_in = cat[:, 0:2, 0:D]
    rel_t = sb("rel_t", [P, 2, D + 2], F32)
    node_block("relzero", lambda ve: iter([ve.memset(cat[:, 0:2, 0:D], 0.0)]))
    load_block("w1", [
        (w_sb[0:D, 0:D], i["W_node_T"]), (w_sb[0:D, D:2 * D], i["W_rel_T"]),
        (rel_in[:, 0, :], i["L1_gnn_rel_emb"][0:P, :]), (rel_in[0:N_REL - P, 1, :], i["L1_gnn_rel_emb"][P:N_REL, :]),
    ] + [(biases[:, j, :], i["L1_gnn_attvec"][0:1, j * D:(j + 1) * D].to_broadcast([P, D])) for j in range(3)])
    linear("lin1", lambda c: hs[:, bass.ds(c, 1), :].rearrange("p a d -> p (a d)"), D, D,
           lambda ve, c, s, y: ve.tensor_copy(t_dst[:, bass.ds(c, 1), 0:D].rearrange("p a d -> p (a d)"), y))
    node_block("relw", lambda ve: iter([ve.tensor_copy(w_sb[0:D, 0:D], w_sb[0:D, D:2 * D])]))
    linear("linr", lambda c: cat[:, bass.ds(c, 1), 0:D].rearrange("p a d -> p (a d)"), D, D,
           lambda ve, c, s, y: ve.tensor_copy(rel_t[:, bass.ds(c, 1), 0:D].rearrange("p a d -> p (a d)"), y), chunks=2)

    def tables1(ve):
        for j, (col, table, first) in enumerate(((0, t_src, 0), (1, t_dst, D + 1))):
            yield ve.tensor_tensor(cat[:, :, 0:D], t_dst[:, :, 0:D], all_nodes(biases[:, j, :], D), ALU.mult)
            yield ve.tensor_reduce(table[:, :, first:first + 1].rearrange("p c o -> p (c o)"), cat[:, :, 0:D], AX.X, ALU.add)
        yield ve.tensor_tensor(cat[:, 0:2, 0:D], rel_t[:, :, 0:D], biases[:, 2, :].unsqueeze(1).to_broadcast([P, 2, D]), ALU.mult)
        yield ve.tensor_reduce(rel_t[:, :, D + 1:D + 2].rearrange("p c o -> p (c o)"), cat[:, 0:2, 0:D], AX.X, ALU.add)
        yield ve.memset(rel_t[:, :, D:D + 1], 0.0)
        yield ve.memset(t_dst[:, :, D:D + 1], 1.0)
    node_block("tables1", tables1)
    rel_f = rel_t[:, :, :].rearrange("p c d -> p (c d)")
    W2 = D + 2
    edge_pass("l1max", [(0, False), (1, False), (2, False), (2, True)], "src", 0, [
        (0, OFF_GS, t_src_f, 0, 1, 0, True, False), (1, OFF_GD, t_dst_f, D + 1, 1, 0, False, False),
        (2, None, rel_f, D + 1, 1, 0, False, False), (3, None, rel_f, W2 + D + 1, 1, 0, False, True)], "maximum")

    x_in = [sem(f"x_in{s}") for s in range(2)]
    x_tp = [sem(f"x_tp{s}") for s in range(2)]
    x_out = [sem(f"x_out{s}") for s in range(2)]
    with nc.Block() as block:
        @block.scalar
        def _(ac):
            with ac.Fori(0, NCH // 2) as t:
                for s in range(2):
                    ac.wait_ge(x_tp[s], t)
                    ac.copy(xt[:, s, 0, :], cat[:, bass.ds(2 * t + s, 1), :].rearrange("p a d -> p (a d)")).then_inc(x_in[s], 1)

        @block.tensor
        def _(pe):
            with pe.Fori(0, NCH // 2) as t:
                for s in range(2):
                    pe.wait_ge(x_in[s], t + 1)
                    pe.wait_ge(x_out[s], t)
                    pe.transpose(work[:, s * BANK:s * BANK + P], xt[:, s, 0, :], ident[:, :]).then_inc(x_tp[s], 1)

        @block.vector
        def _(ve):
            with ve.Fori(0, NCH // 2) as t:
                for s in range(2):
                    ve.wait_ge(x_tp[s], t + 1)
                    ve.tensor_reduce(stat[:, 0, bass.ds(2 * t + s, 1)], work[:, s * BANK:s * BANK + P], AX.X, ALU.max).then_inc(x_out[s], 1)
    node_block("tables1b", lambda ve: iter([ve.tensor_copy(t_src[:, :, 0], stat[:, 0, :])]))
    edge_pass("l1sum", [(0, False), (1, False), (2, False), (2, True)], "src", D + 1, [
        (1, OFF_GD, t_dst_f, 0, D + 1, 0, True, False),
        (2, None, rel_f, 0, D + 1, 0, False, False), (3, None, rel_f, W2, D + 1, 0, False, True),
        (0, OFF_GS, t_src_f, 0, 1, D + 1, True, True)], "softmax")

    def after1(ve):
        for b in range(4):
            lo, hi, a = bank_chunks(b)
            if lo < hi:
                yield ve.tensor_copy(hs[:, lo:hi, :], a[:, :, 0:D])
                yield ve.tensor_scalar(deg[:, lo:hi], a[:, :, D], 1e-12, None, ALU.add)
        yield ve.reciprocal(deg[:, :], deg[:, :])
        yield ve.tensor_tensor(hs[:, :, :], hs[:, :, :], deg[:, :].unsqueeze(2).to_broadcast([P, NCH, D]), ALU.mult)
    node_block("after1", after1)

    layernorm("ln2", [lambda ve: ve.tensor_tensor(xs[:, :, :], xs[:, :, :], hs[:, :, :], ALU.add)])
    load_block("w2", [(w_sb[0:D, :].rearrange("i (r h) -> i r h", r=N_TYPE), i["L2_gnn_W"].rearrange("r i h -> i r h"))])
    xw_rows = xw.rearrange("(r n) d -> n r d", r=N_TYPE)
    linear("lin2", lambda c: hs[:, bass.ds(c, 1), :].rearrange("p a d -> p (a d)"), D, N_TYPE * D,
           lambda ve, c, s, y: ve.tensor_copy(wide[:, s, :], y),
           store=lambda sp, c, s: sp.dma_start(xw_rows[bass.ds(P * c, P), :, :], wide[:, s, :].rearrange("p (r d) -> p r d", r=N_TYPE)))

    ty_idx = sb("ty_idx", [P, 2, G], U32)
    ty_chosen = [sem(f"ty_chosen{s}") for s in range(2)]
    ty_rows = [sem(f"ty_rows{s}") for s in range(2)]
    ty_picked = [sem(f"ty_picked{s}") for s in range(2)]
    ty_added = [sem(f"ty_added{s}") for s in range(2)]
    with nc.Block() as block:
        @block.vector
        def _(ve):
            with ve.Fori(0, GROUPS // 2) as t:
                for s in range(2):
                    g = 2 * t + s
                    ve.wait_ge(ty_added[s], t)
                    ve.tensor_tensor(pick[:, s, :, :], iota_n[:, :].unsqueeze(1).to_broadcast([P, G, P]),
                                     dst_lo[:, bass.ds(G * g, G)].unsqueeze(2).to_broadcast([P, G, P]),
                                     ALU.is_equal).then_inc(ty_picked[s], 1)

        @block.scalar
        def _(ac):
            with ac.Fori(0, GROUPS // 2) as t:
                for s in range(2):
                    ac.wait_ge(ty_rows[s], 16 * G * t)
                    ac.copy(ty_idx[:, s, :], typed_src[:, bass.ds(G * (2 * t + s), G)]).then_inc(ty_chosen[s], 1)

        @block.gpsimd
        def _(gp):
            with gp.Fori(0, GROUPS // 2) as t:
                for s in range(2):
                    gp.wait_ge(ty_chosen[s], t + 1)
                    gp.wait_ge(ty_added[s], t)
                    gp.sem_inc(past, 1)
                    for j in range(G):
                        gp.indirect_dma_start(out=msg[:, s, j, 0:D], out_offset=None, in_=xw,
                                              in_offset=bass.IndirectOffsetOnAxis(ap=ty_idx[:, s, j:j + 1], axis=0)).then_inc(ty_rows[s], 16)

        @block.tensor
        def _(pe):
            regs = [pe.alloc_register(f"ty_r{j}") for j in range(G)]
            clear_acc(pe)
            with pe.Fori(0, GROUPS // 2) as t:
                for s in range(2):
                    at = offsets(pe, OFF_AD, 2 * t + s, regs, ACC_MAX)
                    pe.wait_ge(ty_picked[s], t + 1)
                    pe.wait_ge(ty_rows[s], 16 * G * t + 16 * G)
                    for j in range(G):
                        mm = pe.matmul(acc[:, bass.ds(at[j], D)], pick[:, s, j, :], msg[:, s, j, 0:D], start=False, stop=False,
                                       skip_group_check=True)
                    mm.then_inc(ty_added[s], 1)
            for r in regs:
                pe.free_register(r)

    def add_acc(b):
        lo, hi, a = bank_chunks(b)
        return lambda ve: ve.tensor_tensor(xs[:, lo:hi, :], xs[:, lo:hi, :], a[:, :, 0:D], ALU.add)
    layernorm("ln3", [add_acc(b) for b in range(banks)])

    def conv_loads(n, k_dim, m):
        return [(w_sb[0:k_dim, 0:m], i[f"L3_gnn_Wrel{n}"]), (w_sb[k_dim:2 * k_dim, 0:m], i[f"L3_gnn_Wroot{n}"]),
                (biases[:, 0, 0:m], i[f"L3_gnn_brel{n}"].rearrange("(o m) -> o m", o=1).to_broadcast([P, m]))]

    def mlp_loads(n, k_dim):
        wf = i[f"L3_gnn_Wf{n}"]
        return [(w_sb[0:k_dim, 0:EH], wf[0:k_dim, :]), (w_sb[0:k_dim, EH:2 * EH], wf[k_dim:2 * k_dim, :]),
                (biases[:, 1, 0:EH], i[f"L3_gnn_bf{n}"].rearrange("(o m) -> o m", o=1).to_broadcast([P, EH])),
                (biases[:, 2, 0:EH], wf[2 * k_dim:2 * k_dim + 1, :].to_broadcast([P, EH])),
                (biases[:, 3, 0:EH], i[f"L3_gnn_Wr{n}"].rearrange("h o -> o h").to_broadcast([P, EH])),
                (biases[:, 3, EH:EH + 1], i[f"L3_gnn_br{n}"].rearrange("(o m) -> o m", o=1).to_broadcast([P, 1]))]

    def flat(ap):
        return ap.rearrange("p a d -> p (a d)")

    def edge_net_tables(n, k_dim):
        load_block(f"mw{n}", mlp_loads(n, k_dim))
        linear(f"mlp{n}", lambda c: flat(hs[:, bass.ds(c, 1), 0:k_dim]), k_dim, 2 * EH,
               lambda ve, c, s, y: ve.tensor_copy(flat(cat[:, bass.ds(c, 1), 0:2 * EH]), y))

        def body(ve):
            yield ve.tensor_copy(t_src[:, :, 0:k_dim], hs[:, :, 0:k_dim])
            yield ve.tensor_copy(t_src[:, :, k_dim:k_dim + EH], cat[:, :, 0:EH])
            yield ve.tensor_tensor(t_dst[:, :, 0:EH], cat[:, :, EH:2 * EH], all_nodes(biases[:, 1, 0:EH], EH), ALU.add)
        node_block(f"mt{n}", body)

    def conv(n, k_dim, m):
        load_block(f"cw{n}", conv_loads(n, k_dim, m))

        def body(ve):
            for b in range(banks):
                lo, hi, a = bank_chunks(b)
                yield ve.tensor_copy(cat[:, lo:hi, 0:k_dim], a[:, :, 0:k_dim])
            yield ve.tensor_copy(cat[:, :, k_dim:2 * k_dim], hs[:, :, 0:k_dim])
        node_block(f"cc{n}", body)
        linear(f"conv{n}", lambda c: flat(cat[:, bass.ds(c, 1), 0:2 * k_dim]), 2 * k_dim, m,
               lambda ve, c, s, y: ve.tensor_tensor(flat(hs[:, bass.ds(c, 1), 0:m]), y, biases[:, 0, 0:m], ALU.add))
        node_block(f"cr{n}", lambda ve: iter([ve.tensor_scalar(hs[:, :, 0:m], hs[:, :, 0:m], 0.0, None, ALU.max)]))

    for n, k_dim, m, w, dest in ((1, D, H1, weight, edge_a), (2, H1, D, edge_a, edge_b)):
        edge_net_tables(n, k_dim)
        edge_pass(f"l3_{n}", [(0, False), (1, False)], "dst", k_dim, [
            (0, OFF_GS, t_src_f, 0, k_dim + EH, 0, True, False), (1, OFF_GD, t_dst_f, 0, EH, k_dim, False, True)],
            "weighted", w=w, mlp=(biases[:, 2, 0:EH], biases[:, 3, 0:EH], biases[:, 3, EH:EH + 1], dest))
        conv(n, k_dim, m)
    node_block("t3", lambda ve: iter([ve.tensor_copy(t_src[:, :, 0:D], hs[:, :, :])]))
    edge_pass("l3_3", [(0, False)], "dst", D, [(0, OFF_GS, t_src_f, 0, D, 0, True, True)], "weighted", w=edge_b)
    conv(3, D, D)
    node_block("last", lambda ve: iter([ve.tensor_tensor(xs[:, :, :], xs[:, :, :], hs[:, :, :], ALU.add)]))
    s_out = sem("s_out")
    with nc.Block() as block:
        @block.sync
        def _(sp):
            sp.dma_start(out[0:FULL * P, :].rearrange("(c p) d -> p c d", p=P), xs[:, 0:FULL, :]).then_inc(s_out, 16)
            sp.dma_start(out[FULL * P:N_NODES, :], xs[0:TAIL, FULL, :]).then_inc(s_out, 16)
            sp.wait_ge(s_out, 32)


def kernel(**inputs):
    import numpy as np
    import concourse.bacc as bacc
    from concourse import mybir
    from concourse.bass_utils import run_bass_kernel_spmd

    host = {name: np.ascontiguousarray(a) for name, a in inputs.items()}
    host["W_node_T"] = np.ascontiguousarray(host.pop("L1_gnn_W_node").T)
    host["W_rel_T"] = np.ascontiguousarray(host.pop("L1_gnn_W_rel").T)
    nc = bacc.Bacc("TRN2", target_bir_lowering=False, num_devices=1)
    arrays, aps = {}, {}
    for name, a in host.items():
        arrays[f"in_{name}"] = a
        aps[name] = nc.dram_tensor(f"in_{name}", a.shape, mybir.dt.from_np(a.dtype), kind="ExternalInput").ap()
    out = nc.dram_tensor("out", (N_NODES, D), mybir.dt.float32, kind="ExternalOutput").ap()
    build(nc, aps, out)
    return run_bass_kernel_spmd(nc, [arrays], core_ids=[0]).results[0]["out"]
```

```python
from contextlib import ExitStack

import concourse.bass as bass
from concourse import mybir

ALU = mybir.AluOpType
ACT = mybir.ActivationFunctionType
AX = mybir.AxisListType
F32 = mybir.dt.float32
F16 = mybir.dt.float16
BF16 = mybir.dt.bfloat16
I32 = mybir.dt.int32
U32 = mybir.dt.uint32

P = 128
N_NODES = 3125
N_EDGES = 100000
D = 64
N_REL = 200
N_TYPE = 8
H1 = 32
EH = 32
CH = -(-N_NODES // P)
NCH = CH + CH % 2
NP_ = NCH * P
FULL = N_NODES // P
TAIL = N_NODES - FULL * P
EP = 125
EC = N_EDGES // EP
RG = 8
NB = CH * CH
G = 4
MAX_TILES = (N_EDGES + (P - 1) * NB) // P
GROUPS = -(-MAX_TILES // (2 * G)) * 2
TILES = (GROUPS + 1) * G
TROWS = -(-TILES // P)
PADS = 192
REC = 8
TW = 288
TD = 200
GW = 256
AW = 72
BANK = 512
APB = BANK // AW
NEG = -1.0e30
EPS = 1e-5
assert EP * EC == N_EDGES and EC % RG == 0 and GROUPS % 2 == 0 and EP <= P


def build(nc, i, out):
    with ExitStack() as ctx:
        program(nc, ctx, i, out)


def program(nc, ctx, i, out):
    names = iter(range(10**6))

    def sb(name, shape, dt, at=ctx):
        return at.enter_context(nc.sbuf_tensor(f"{name}_{next(names)}", shape, dt))

    def sem(name):
        return ctx.enter_context(nc.semaphore(f"{name}_{next(names)}"))

    past = sem("past")

    rec = nc.dram_tensor("rec", [P * TILES, REC], F32, kind="Internal").ap()
    rows = nc.dram_tensor("rows", [3, TILES, P], F16, kind="Internal").ap()
    offs_d = nc.dram_tensor("offs_d", [5 * TROWS, P], I32, kind="Internal").ap()
    xw = nc.dram_tensor("xw", [N_TYPE * NP_, D], F32, kind="Internal").ap()

    acc = ctx.enter_context(nc.psum_tensor("acc", [P, 4 * BANK], F32))
    work = ctx.enter_context(nc.psum_tensor("work", [P, 4 * BANK], F32))

    lane = sb("lane", [P, 1], F32)
    lane_hi = sb("lane_hi", [P, 1], F32)
    iota_n = sb("iota_n", [P, P], F32)
    ident = sb("ident", [P, P], F32)
    zeros = sb("zeros", [P, BANK], BF16)
    src_lo = sb("src_lo", [P, 1, TILES], F32)
    dst_lo = sb("dst_lo", [P, 4, TILES], F32)
    weight = sb("weight", [P, TILES], F32)
    typed_src = sb("typed_src", [P, TILES], U32)
    offs = sb("offs", [1, 5, TROWS * P], I32)
    OFF_GS, OFF_GD, OFF_AD, OFF_AS, OFF_RS = range(5)
    xs = sb("xs", [P, NCH, D], F32)
    hs = sb("hs", [P, NCH, D], F32)
    xt = sb("xt", [P, 2, 2, P], F32)
    deg = sb("deg", [P, NCH], F32)

    def bank_chunks(b):
        lo, hi = b * APB, min((b + 1) * APB, NCH)
        n = hi - lo
        return lo, hi, acc[:, b * BANK:b * BANK + n * AW].rearrange("p (c w) -> p c w", w=AW)

    with ExitStack() as edges:
        bucket = sb("bucket", [EP, EC], F32, edges)
        record = sb("record", [EP, EC, REC], F32, edges)
        iota_b = sb("iota_b", [P, NB], F16, edges)
        onehot = sb("onehot", [EP, RG, NB], BF16, edges)
        ones = sb("ones", [P, P], BF16, edges)
        before = sb("before", [P, P], BF16, edges)
        notbefore = sb("notbefore", [P, P], BF16, edges)
        h_made = [sem(f"h_made{s}") for s in range(2)]
        h_used = [sem(f"h_used{s}") for s in range(2)]
        r_made, r_ready, r_read, r_step = sem("r_made"), sem("r_ready"), sem("r_read"), sem("r_step")
        r_staged, r_sent, r_free = sem("r_staged"), sem("r_sent"), sem("r_free")
        s_in, s_const, s_prep, s_pad, s_x = sem("s_in"), sem("s_const"), sem("s_prep"), sem("s_pad"), sem("s_x")
        with ExitStack() as tmp, nc.Block() as block:
            raw = sb("raw", [EP, 5, EC], I32, tmp)
            part = sb("part", [EP, 4, EC], I32, tmp)
            padrow = sb("padrow", [P, PADS, REC], F32, tmp)

            @block.sync
            def _(sp):
                for n, name in enumerate(("src", "dst", "edge_type_200", "edge_type_8")):
                    sp.dma_start(raw[:, n, :], i[name].rearrange("(p c) -> p c", p=EP)).then_inc(s_in, 16)
                sp.dma_start(raw[:, 4, :].bitcast(F32), i["edge_weight"].rearrange("(p c) -> p c", p=EP)).then_inc(s_in, 16)
                sp.wait_ge(s_const, 3)
                sp.dma_start(xs[:, 0:FULL, :], i["x"][0:FULL * P, :].rearrange("(c p) d -> p c d", p=P)).then_inc(s_x, 16)
                sp.dma_start(xs[0:TAIL, FULL, :], i["x"][FULL * P:N_NODES, :]).then_inc(s_x, 16)
                sp.wait_ge(s_const, 5)
                rec_rows = rec.rearrange("(p t) r -> p (t r)", p=P)
                for a in range(0, TILES, PADS):
                    n = min(PADS, TILES - a)
                    sp.dma_start(rec_rows[:, a * REC:(a + n) * REC],
                                 padrow[:, 0:n, :].rearrange("p t r -> p (t r)")).then_inc(s_pad, 16)
                sp.wait_ge(s_pad, 16 * -(-TILES // PADS))
                sp.wait_ge(s_x, 32)

            @block.gpsimd
            def _(gp):
                for m in h_used + [r_read, r_free]:
                    gp.sem_inc(m, 1)
                gp.memset(record[:, :, 5:REC], 0.0)
                gp.memset(ones[:, :], 1.0).then_inc(s_const, 1)
                gp.memset(zeros[:, :], 0.0).then_inc(s_const, 1)
                gp.memset(xs[:, :, :], 0.0).then_inc(s_const, 1)
                gp.memset(padrow[:, :, :], 0.0).then_inc(s_const, 1)
                gp.wait_ge(s_const, 4)
                gp.memset(padrow[:, :, 0:3], -1.0).then_inc(s_const, 1)
                gp.iota(iota_n[:, :], pattern=[[1, P]], base=0, channel_multiplier=0, allow_small_or_imprecise_dtypes=True)
                gp.iota(lane[:, :], pattern=[[0, 1]], base=0, channel_multiplier=1, allow_small_or_imprecise_dtypes=True)
                gp.iota(lane_hi[:, :], pattern=[[0, 1]], base=P, channel_multiplier=1, allow_small_or_imprecise_dtypes=True)
                gp.iota(iota_b[:, :], pattern=[[1, NB]], base=0, channel_multiplier=0, allow_small_or_imprecise_dtypes=True)
                gp.memset(onehot[:, :, :], 0.0).then_inc(s_const, 1)

            @block.vector
            def _(ve):
                n = 0
                ve.wait_ge(s_in, 16 * 5)
                for j in range(2):
                    ve.tensor_scalar(part[:, j, :], raw[:, j, :], P - 1, None, ALU.bitwise_and).then_inc(s_prep, 1)
                    ve.tensor_scalar(part[:, 2 + j, :], raw[:, j, :], 7, None, ALU.arith_shift_right).then_inc(s_prep, 1)
                ve.wait_ge(s_prep, 4)
                for j in range(2):
                    ve.tensor_copy(record[:, :, j], part[:, j, :])
                ve.tensor_copy(record[:, :, 2], raw[:, 2, :])
                ve.tensor_copy(record[:, :, 3], raw[:, 4, :].bitcast(F32))
                ve.scalar_tensor_tensor(out=record[:, :, 4], in0=raw[:, 3, :], scalar=float(NP_), in1=raw[:, 0, :],
                                        op0=ALU.mult, op1=ALU.add)
                ve.scalar_tensor_tensor(out=bucket[:, :], in0=part[:, 2, :], scalar=float(CH), in1=part[:, 3, :],
                                        op0=ALU.mult, op1=ALU.add)
                ve.wait_ge(s_const, 6)
                ve.tensor_scalar(ident[:, :], iota_n[:, :], lane[:, 0:1], None, ALU.is_equal)
                ve.tensor_scalar(before[:, :], iota_n[:, :], lane[:, 0:1], None, ALU.is_gt)
                ve.tensor_scalar(notbefore[:, :], iota_n[:, :], lane[:, 0:1], None, ALU.is_le)
                ve.memset(hs[:, :, :], 0.0)
                ve.memset(xt[:, :, :, :], 0.0)

        with nc.Block() as block:
            @block.vector
            def _(ve):
                with ve.Fori(0, EC // 2) as t:
                    for s in range(2):
                        ve.wait_ge(h_used[s], t + 1)
                        ve.tensor_scalar(onehot[:, s, :], iota_b[0:EP, :], bucket[:, bass.ds(2 * t + s, 1)], None,
                                         ALU.is_equal).then_inc(h_made[s], 1)

            @block.tensor
            def _(pe):
                for b in range(2):
                    pe.matmul(work[:, b * BANK:(b + 1) * BANK], zeros[:, 0:P], zeros[:, :], start=True, stop=True)
                with pe.Fori(0, EC // 2) as t:
                    for s in range(2):
                        pe.wait_ge(h_made[s], t + 1)
                        pe.matmul(work[:, 0:BANK], ones[0:EP, :], onehot[:, s, 0:BANK], start=False, stop=False, skip_group_check=True)
                        pe.matmul(work[:, BANK:NB], ones[0:EP, :], onehot[:, s, BANK:NB], start=False, stop=False,
                                  skip_group_check=True).then_inc(h_used[s], 1)

        with ExitStack() as tmp:
            base_hi = sb("base_hi", [1, NB], BF16, edges)
            base_lo = sb("base_lo", [1, NB], BF16, edges)
            ni = sb("ni", [P, NB], I32, tmp)
            nt = sb("nt", [P, NB], F32, tmp)
            one_f = sb("one_f", [P, NB], F32, tmp)
            ends = sb("ends", [P, NB], F32, tmp)
            starts = sb("starts", [P, NB], I32, tmp)
            st_a = sb("st_a", [1, NB], I32, tmp)
            less = sb("less", [P, NB], F32, tmp)
            tile_no = sb("tile_no", [P, TROWS], F32, tmp)
            tb = sb("tb", [P, TROWS], F32, tmp)
            steps = sb("steps", [P, CH - 1], F32, tmp)
            ge = sb("ge", [P, TROWS, CH - 1], F32, tmp)
            tcs = sb("tcs", [P, 2, TROWS], F32, tmp)
            tbank = sb("tbank", [P, 2, TROWS], F32, tmp)
            fld = sb("fld", [P, 5, TROWS], F32, tmp)
            fld_t = sb("fld_t", [5 * TROWS, P], I32, tmp)
            s_i, s_v, s_t, s_c, s_o = sem("s_i"), sem("s_v"), sem("s_t"), sem("s_c"), sem("s_o")
            with nc.Block() as block:
                @block.gpsimd
                def _(gp):
                    gp.iota(tile_no[:, :], pattern=[[P, TROWS]], base=0, channel_multiplier=1, allow_small_or_imprecise_dtypes=True)
                    gp.iota(steps[:, :], pattern=[[1, CH - 1]], base=1, channel_multiplier=0, allow_small_or_imprecise_dtypes=True)
                    gp.memset(one_f[:, :], 1.0).then_inc(s_i, 1)

                @block.vector
                def _(ve):
                    n = 0

                    def step(op):
                        nonlocal n
                        op.then_inc(s_v, 1)
                        n += 1
                        ve.wait_ge(s_v, n)

                    ve.wait_ge(s_i, 1)
                    step(ve.tensor_scalar(ni[:, :], work[:, 0:NB], float(P - 1), None, ALU.add))
                    step(ve.tensor_scalar(starts[:, :], ni[:, :], 7, None, ALU.arith_shift_right))
                    step(ve.tensor_copy(nt[:, :], starts[:, :]))
                    step(ve.tensor_tensor_scan(ends[:, :], one_f[:, :], nt[:, :], 0.0, ALU.mult, ALU.add))
                    step(ve.tensor_tensor(starts[:, :], ends[:, :], nt[:, :], ALU.subtract))
                    step(ve.tensor_scalar(st_a[:, :], starts[0:1, :], 31, None, ALU.bitwise_and))
                    step(ve.tensor_scalar(base_lo[:, :], st_a[:, :], float(P), None, ALU.mult))
                    step(ve.tensor_scalar(st_a[:, :], starts[0:1, :], 5, None, ALU.arith_shift_right))
                    step(ve.tensor_scalar(base_hi[:, :], st_a[:, :], float(32 * P), None, ALU.mult))
                    for k in range(TROWS):
                        step(ve.tensor_scalar(less[:, :], ends[:, :], tile_no[:, k:k + 1], None, ALU.is_le))
                        step(ve.tensor_reduce(tb[:, k:k + 1], less[:, :], AX.X, ALU.add))
                    step(ve.tensor_scalar(tb[:, :], tb[:, :], float(NB - 1), None, ALU.min))
                    step(ve.tensor_scalar(less[:, 0:CH - 1], steps[:, :], float(CH), None, ALU.mult))
                    step(ve.tensor_tensor(ge[:, :, :], tb[:, :].unsqueeze(2).to_broadcast([P, TROWS, CH - 1]),
                                          less[:, 0:CH - 1].unsqueeze(1).to_broadcast([P, TROWS, CH - 1]), ALU.is_ge))
                    step(ve.tensor_reduce(tcs[:, 0, :], ge[:, :, :], AX.X, ALU.add))
                    step(ve.scalar_tensor_tensor(out=tcs[:, 1, :], in0=tcs[:, 0, :], scalar=-float(CH), in1=tb[:, :],
                                                 op0=ALU.mult, op1=ALU.add))
                    nb = CH // APB
                    step(ve.tensor_scalar(less[:, 0:nb], steps[:, 0:nb], float(APB), None, ALU.mult))
                    for j in range(2):
                        step(ve.tensor_tensor(ge[:, :, 0:nb], tcs[:, j, :].unsqueeze(2).to_broadcast([P, TROWS, nb]),
                                              less[:, 0:nb].unsqueeze(1).to_broadcast([P, TROWS, nb]), ALU.is_ge))
                        step(ve.tensor_reduce(tbank[:, j, :], ge[:, :, 0:nb], AX.X, ALU.add))
                    step(ve.tensor_scalar(tbank[:, :, :], tbank[:, :, :], float(BANK - APB * AW), None, ALU.mult))
                    for j, f, w in ((0, OFF_GS, TW), (1, OFF_GD, TD)):
                        step(ve.tensor_scalar(fld[:, f, :], tcs[:, j, :], float(w), None, ALU.mult))
                    step(ve.tensor_scalar(fld[:, OFF_RS, :], tcs[:, 0, :], float(P), None, ALU.mult))
                    for j, f in ((0, OFF_AS), (1, OFF_AD)):
                        step(ve.scalar_tensor_tensor(out=fld[:, f, :], in0=tcs[:, j, :], scalar=float(AW), in1=tbank[:, j, :],
                                                     op0=ALU.mult, op1=ALU.add))
                    ve.sem_inc(s_t, 1)
                    ve.wait_ge(s_t, 2)
                    ve.tensor_copy(fld_t[:, :], work[0:5 * TROWS, 3 * BANK:3 * BANK + P]).then_inc(s_c, 1)

                @block.tensor
                def _(pe):
                    pe.wait_ge(s_t, 1)
                    pe.transpose(work[0:5 * TROWS, 3 * BANK:3 * BANK + P], fld[:, :, :].rearrange("p f t -> p (f t)"),
                                 ident[:, :]).then_inc(s_t, 1)

                @block.sync
                def _(sp):
                    sp.wait_ge(s_c, 1)
                    sp.dma_start(offs_d, fld_t[:, :]).then_inc(s_o, 16)
                    sp.wait_ge(s_o, 16)
                    sp.dma_start(offs[:, :, :], offs_d.rearrange("(o f t) p -> o f (t p)", o=1, f=5)).then_inc(s_o, 16)
                    sp.wait_ge(s_o, 32)

        with ExitStack() as tmp:
            junk = sb("junk", [EP, NB], BF16, tmp)
            place = sb("place", [EP, RG], F32, tmp)
            place_i = sb("place_i", [EP, RG], I32, tmp)
            place_lane = sb("place_lane", [EP, RG], I32, tmp)
            place_tile = sb("place_tile", [EP, RG], I32, tmp)
            address = sb("address", [EP, RG], U32, tmp)
            staged = sb("staged", [EP, RG, REC], F32, tmp)
            with nc.Block() as block:
                @block.vector
                def _(ve):
                    with ve.Fori(0, EC // RG) as t:
                        def mark(k):
                            ve.tensor_scalar(onehot[:, k, :], iota_b[0:EP, :], bucket[:, bass.ds(RG * t + k, 1)], None,
                                             ALU.is_equal).then_inc(r_made, 1)

                        mark(0)
                        for k in range(RG):
                            if k + 1 < RG:
                                mark(k + 1)
                            ve.wait_ge(r_ready, RG * t + k + 1)
                            if k == 0:
                                ve.wait_ge(r_made, RG * t + 1)
                            ve.tensor_tensor_reduce(junk[:, :], onehot[:, k, :], work[0:EP, 0:NB], 1.0, 0.0, ALU.mult,
                                                    ALU.add, place[:, k:k + 1]).then_inc(r_read, 1)
                            ve.wait_ge(r_made, RG * t + min(k + 2, RG))
                        ve.wait_ge(r_read, RG * t + RG + 1)
                        ve.tensor_copy(place_i[:, :], place[:, :]).then_inc(r_step, 1)
                        ve.wait_ge(r_step, 3 * t + 1)
                        ve.tensor_scalar(place_lane[:, :], place_i[:, :], P - 1, None, ALU.bitwise_and).then_inc(r_step, 1)
                        ve.tensor_scalar(place_tile[:, :], place_i[:, :], 7, None, ALU.arith_shift_right).then_inc(r_step, 1)
                        ve.wait_ge(r_step, 3 * t + 3)
                        ve.wait_ge(r_free, t + 1)
                        ve.scalar_tensor_tensor(out=address[:, :], in0=place_lane[:, :], scalar=float(TILES), in1=place_tile[:, :],
                                                op0=ALU.mult, op1=ALU.add)
                        ve.tensor_copy(staged[:, :, :], record[:, bass.ds(RG * t, RG), :]).then_inc(r_staged, 1)

                @block.tensor
                def _(pe):
                    def add(which, k):
                        pe.matmul(work[:, 0:BANK], which, onehot[:, k, 0:BANK], start=False, stop=False, skip_group_check=True)
                        return pe.matmul(work[:, BANK:NB], which, onehot[:, k, BANK:NB], start=False, stop=False, skip_group_check=True)

                    for b in range(2):
                        lo, hi = b * BANK, min((b + 1) * BANK, NB)
                        pe.matmul(work[:, b * BANK:(b + 1) * BANK], zeros[:, 0:P], zeros[:, :], start=True, stop=True)
                        for part in (base_hi, base_lo):
                            pe.matmul(work[:, lo:hi], ones[0:1, :], part[0:1, lo:hi], start=False, stop=False, skip_group_check=True)
                    with pe.Fori(0, EC // RG) as t:
                        for k in range(RG):
                            pe.wait_ge(r_read, RG * t + k + 1)
                            add(notbefore[0:EP, :], (k - 1) % RG)
                            pe.wait_ge(r_made, RG * t + k + 1)
                            add(before[0:EP, :], k).then_inc(r_ready, 1)

                @block.gpsimd
                def _(gp):
                    with gp.Fori(0, EC // RG) as t:
                        gp.wait_ge(r_staged, t + 1)
                        gp.sem_inc(past, 1)
                        for k in range(RG):
                            gp.indirect_dma_start(out=rec, out_offset=bass.IndirectOffsetOnAxis(ap=address[:, k:k + 1], axis=0),
                                                  in_=staged[:, k, :], in_offset=None).then_inc(r_sent, 16)
                        gp.wait_ge(r_sent, 16 * RG * t + 16 * RG)
                        gp.sem_inc(r_free, 1)

    with ExitStack() as tmp:
        allrec = sb("allrec", [P, TILES, REC], F32, tmp)
        row_sb = sb("row_sb", [P, 2, 3 * P], F16, tmp)
        s_l, s_u, s_w = sem("s_l"), sem("s_u"), sem("s_w")
        s_tp = [sem(f"s_tp{s}") for s in range(2)]
        s_cp = [sem(f"s_cp{s}") for s in range(2)]
        s_wr = [sem(f"s_wr{s}") for s in range(2)]
        spans = [(a, min(a + P, TILES)) for a in range(0, TILES, P)]
        with nc.Block() as block:
            @block.sync
            def _(sp):
                sp.dma_start(allrec[:, :, :], rec.rearrange("(p t) r -> p t r", p=P)).then_inc(s_l, 16)
                for n, (a, b) in enumerate(spans):
                    sp.wait_ge(s_cp[n % 2], n // 2 + 1)
                    sp.dma_start(rows[:, a:b, :].rearrange("f t e -> t f e"),
                                 row_sb[0:b - a, n % 2, :].rearrange("t (f e) -> t f e", f=3)).then_inc(s_wr[n % 2], 16)
                for s in range(2):
                    sp.wait_ge(s_wr[s], 16 * ((len(spans) + 1 - s) // 2))

            @block.tensor
            def _(pe):
                pe.wait_ge(s_l, 16)
                for n, (a, b) in enumerate(spans):
                    pe.wait_ge(s_cp[n % 2], n // 2)
                    for f in range(3):
                        mm = pe.transpose(work[0:b - a, (n % 2) * BANK + f * P:(n % 2) * BANK + (f + 1) * P],
                                          allrec[:, a:b, f], ident[:, :])
                    mm.then_inc(s_tp[n % 2], 1)

            @block.scalar
            def _(ac):
                for n, (a, b) in enumerate(spans):
                    ac.wait_ge(s_tp[n % 2], n // 2 + 1)
                    if n >= 2:
                        ac.wait_ge(s_wr[n % 2], 16 * (n // 2))
                    ac.copy(row_sb[0:b - a, n % 2, :], work[0:b - a, (n % 2) * BANK:(n % 2) * BANK + 3 * P]).then_inc(s_cp[n % 2], 1)

            @block.vector
            def _(ve):
                ve.wait_ge(s_l, 16)
                ve.tensor_copy(src_lo[:, 0, :], allrec[:, :, 0])
                ve.tensor_copy(dst_lo[:, 0, :], allrec[:, :, 1])
                ve.tensor_copy(weight[:, :], allrec[:, :, 3])
                ve.tensor_copy(typed_src[:, :], allrec[:, :, 4])

    edge_a = sb("edge_a", [P, TILES], F32)
    edge_b = sb("edge_b", [P, TILES], F32)
    t_src = sb("t_src", [P, NCH, TW], BF16)
    t_dst = sb("t_dst", [P, NCH, TD], BF16)
    cat = sb("cat", [P, NCH, P], F32)
    cat2 = sb("cat2", [P, NCH, P], F32)
    t_src_f = t_src[:, :, :].rearrange("p c w -> p (c w)")
    t_dst_f = t_dst[:, :, :].rearrange("p c w -> p (c w)")
    cat_f = [c[:, :, :].rearrange("p c w -> p (c w)") for c in (cat, cat2)]

    marks = sb("marks", [P, 2, 4, G * P], BF16)
    bcast = sb("bcast", [P, 2, 3, G * P], F16)
    pick = sb("pick", [P, 2, G, 3, P], BF16)
    pick_f = sb("pick_f", [P, 2, G, P], F32)
    near = sb("near", [P, 2, 4, G], F32)
    msg = sb("msg", [P, 2, G, 3 * (D + 1)], BF16)
    msg_f = sb("msg_f", [P, 2, G, D + 1], F32)
    small = sb("small", [P, 2, 4, G], F32)
    wide = sb("wide", [P, 2, BANK], F32)
    iota_bf = sb("iota_bf", [P, P], BF16)
    biases = sb("biases", [P, 8, D], F32)
    w_sb = sb("w_sb", [P, BANK], F32)
    stat = sb("stat", [P, 2, NCH], F32)
    rel_f = sb("rel_f", [P, 2, D + 2], F32)
    rel_t = sb("rel_t", [P, 2, TD], BF16)
    gath = [work[:, 2 * s * BANK:2 * (s + 1) * BANK].rearrange("p (t w) -> p t w", w=GW) for s in range(2)]
    column = {"src": src_lo, "dst": dst_lo}
    acc_off = {"src": OFF_AS, "dst": OFF_AD}
    table_most = {OFF_GS: (CH - 1) * TW, OFF_GD: (CH - 1) * TD}
    ACC_MAX = (CH - 1) * AW + (CH - 1) // APB * (BANK - APB * AW)

    def offsets(eng, field, tile, regs, most):
        eng.load(regs, offs[0:1, field, bass.ds(tile, len(regs))])
        return [eng.snap(r, min_val=0, max_val=most) for r in regs]

    def clear_acc(pe):
        for b in range(4):
            pe.matmul(acc[:, b * BANK:(b + 1) * BANK], zeros[:, 0:P], zeros[:, :], start=True, stop=True)

    m_loaded, m_marked, m_gathered, m_msg, m_picked, m_added, m_part, m_near, m_kept, m_sum = (
        [sem(f"m_{what}{s}") for s in range(2)]
        for what in ("loaded", "marked", "gathered", "msg", "picked", "added", "part", "near", "kept", "sum"))
    m_step = sem("m_step")
    first_ones = m_marked + m_gathered + m_msg + m_picked + m_added + m_kept
    pass_sems = first_ones + m_loaded + m_part + m_near + m_sum + [m_step]
    x_in, x_tp, x_out = ([sem(f"x_{what}{s}") for s in range(2)] for what in ("in", "tp", "out"))
    counted = {"pass": 0, "linear": 0, "sent": 0, "load": 0, "ve": 0, "ac": 0}

    def edge_pass(name, fields, into, width, gathers, kind, share=None, mlp=None):
        need_rows = sorted({f[0] for f in fields})
        kinds = sorted({gt[1] for gt in gathers if gt[1] is not None})
        with nc.Block() as block:
            @block.gpsimd
            def _(gp):
                if counted["pass"]:
                    for m in pass_sems:
                        gp.sem_clear(m)
                for m in first_ones:
                    gp.sem_inc(m, 1)

            if kind == "maximum":
                @block.vector
                def _(ve):
                    ve.memset(cat[:, :, :], NEG)
                    ve.memset(cat2[:, :, :], NEG)
        counted["pass"] += 1

        with nc.Block() as block:
            @block.sync
            def _(sp):
                def load(g, s, k):
                    sp.wait_ge(m_marked[s], k + 1)
                    for f in need_rows:
                        sp.dma_start(bcast[:, s, f, :], rows[f, bass.ds(G * g, G), :].rearrange("(o t) e -> o (t e)", o=1)
                                     .to_broadcast([P, G * P])).then_inc(m_loaded[s], 16)

                load(0, 0, 0)
                with sp.Fori(0, GROUPS // 2) as t:
                    load(2 * t + 1, 1, t)
                    load(2 * t + 2, 0, t + 1)

            @block.vector
            def _(ve):
                def mark(s, k):
                    ve.wait_ge(m_loaded[s], 16 * len(need_rows) * (k + 1))
                    ve.wait_ge(m_gathered[s], k + 1)
                    for n, (f, high) in enumerate(fields):
                        op = ve.tensor_scalar(marks[:, s, n, :], bcast[:, s, f, :], (lane_hi if high else lane)[:, 0:1], None,
                                              ALU.is_equal)
                    op.then_inc(m_marked[s], 1)

                def choose(s, k):
                    ve.wait_ge(m_near[s], k + 1)
                    ve.wait_ge(m_added[s], k + 1)
                    for j in range(G):
                        lo = near[:, s, 0, j:j + 1]
                        if kind == "plain":
                            op = ve.tensor_scalar(pick[:, s, j, 0, :], iota_bf[:, :], lo, None, ALU.is_equal)
                        elif kind == "softmax":
                            op = ve.tensor_scalar(pick_f[:, s, j, :], iota_n[:, :], lo, None, ALU.is_equal)
                        elif kind == "maximum":
                            op = ve.tensor_scalar(pick[:, s, j, 0, :], iota_bf[:, :], lo, NEG, ALU.not_equal, ALU.mult)
                        else:
                            for q in range(3):
                                op = ve.tensor_scalar(pick[:, s, j, q, :], iota_bf[:, :], lo, near[:, s, 1 + q, j:j + 1],
                                                      ALU.is_equal, ALU.mult)
                    op.then_inc(m_picked[s], 1)

                def message(g, s, k):
                    if kind == "plain":
                        return
                    ve.wait_ge(m_gathered[s], k + 2)
                    if mlp is not None:
                        w_row, w_out, b_out, dest = mlp
                        n0 = 4 * g
                        hid = wide[:, s, 0:G * EH].rearrange("p (t h) -> p t h", h=EH)
                        add = wide[:, s, G * EH:2 * G * EH].rearrange("p (t h) -> p t h", h=EH)
                        ve.tensor_reduce(add, gath[s][:, :, 3 * width:3 * width + 2 * EH].rearrange("p t (q h) -> p t h q", q=2),
                                         AX.X, ALU.add).then_inc(m_sum[s], 1)
                        ve.wait_ge(m_sum[s], k + 1)
                        ve.wait_ge(m_part[s], k + 1)
                        ve.tensor_tensor(hid, hid, add, ALU.add).then_inc(m_step, 1)
                        ve.wait_ge(m_step, n0 + 1)
                        ve.scalar_tensor_tensor(out=hid, in0=hid, scalar=0.0, in1=w_out.unsqueeze(1).to_broadcast([P, G, EH]),
                                                op0=ALU.max, op1=ALU.mult).then_inc(m_step, 1)
                        ve.wait_ge(m_step, n0 + 2)
                        ve.tensor_reduce(small[:, s, 0, :], hid, AX.X, ALU.add).then_inc(m_step, 1)
                        ve.wait_ge(m_step, n0 + 3)
                        ve.tensor_scalar(dest[:, bass.ds(G * g, G)], small[:, s, 0, :], b_out, None, ALU.add).then_inc(m_step, 1)
                        ve.sem_inc(m_kept[s], 1)
                    elif kind == "maximum":
                        n0 = (G + 2) * g
                        ve.wait_ge(m_kept[s], k + 1)
                        ve.tensor_reduce(small[:, s, 1, :], gath[s][:, :, 0:3], AX.X, ALU.add).then_inc(m_step, 1)
                        ve.wait_ge(m_step, n0 + 1)
                        ve.scalar_tensor_tensor(out=small[:, s, 0, :], in0=small[:, s, 1, :], scalar=0.2,
                                                in1=small[:, s, 1, :], op0=ALU.mult, op1=ALU.max).then_inc(m_step, 1)
                        ve.wait_ge(m_step, n0 + 2)
                        ve.sem_inc(m_part[s], 1)
                        ve.wait_ge(m_picked[s], k + 2)
                        for j in range(G):
                            ve.wait_ge(m_step, n0 + 1 + j)
                            top = cat_f[j % 2][:, bass.ds(top_at[G * s + j], P)]
                            op = ve.scalar_tensor_tensor(out=top, in0=pick[:, s, j, 0, :], scalar=small[:, s, 0, j:j + 1], in1=top,
                                                         op0=ALU.add, op1=ALU.max)
                            op.then_inc(m_step, 1)
                        ve.sem_inc(m_msg[s], 1)
                        ve.sem_inc(m_added[s], 1)
                    elif kind == "softmax":
                        ve.wait_ge(m_msg[s], k + 1)
                        n0 = 2 * g
                        ve.tensor_reduce(small[:, s, 2, :], gath[s][:, :, 3 * width:3 * width + 3], AX.X, ALU.add).then_inc(m_step, 1)
                        ve.wait_ge(m_step, n0 + 1)
                        ve.tensor_tensor(small[:, s, 0, :], edge_a[:, bass.ds(G * g, G)], small[:, s, 2, :],
                                         ALU.subtract).then_inc(m_part[s], 1)
                        ve.tensor_reduce(wide[:, s, 0:G * width].rearrange("p (t w) -> p t w", w=width),
                                         gath[s][:, :, 0:3 * width].rearrange("p t (q w) -> p t w q", q=3),
                                         AX.X, ALU.add).then_inc(m_sum[s], 1)
                        ve.sem_inc(m_step, 1)

                if kind == "maximum":
                    max_regs = [ve.alloc_register(f"{name}_off{j}") for j in range(2 * G)]
                mark(0, 0)
                with ve.Fori(0, GROUPS // 2) as t:
                    if kind == "maximum":
                        top_at = offsets(ve, OFF_RS, 2 * G * t, max_regs, (CH - 1) * P)
                    mark(1, t)
                    choose(0, t)
                    message(2 * t, 0, t)
                    mark(0, t + 1)
                    choose(1, t)
                    message(2 * t + 1, 1, t)
                if kind == "maximum":
                    for r in max_regs:
                        ve.free_register(r)

            if kind == "maximum" or mlp is not None:
                @block.gpsimd
                def _(gp):
                    with gp.Fori(0, GROUPS // 2) as t:
                        for s in range(2):
                            g = 2 * t + s
                            if kind == "maximum":
                                gp.wait_ge(m_part[s], t + 1)
                                gp.tensor_copy(edge_a[:, bass.ds(G * g, G)], small[:, s, 0, :]).then_inc(m_kept[s], 1)
                            else:
                                gp.wait_ge(m_kept[s], t + 1)
                                gp.tensor_tensor(wide[:, s, 0:G * EH].rearrange("p (t h) -> p t h", h=EH),
                                                 share[:, bass.ds(G * g, G)].unsqueeze(2).to_broadcast([P, G, EH]),
                                                 mlp[0].unsqueeze(1).to_broadcast([P, G, EH]), ALU.mult).then_inc(m_part[s], 1)

            @block.scalar
            def _(ac):
                n_near = 4 if kind == "weighted" else 1

                def beside(g, s, k):
                    ac.wait_ge(m_picked[s], k + 1)
                    ac.copy(near[:, s, 0:n_near, :], column[into][:, 0:n_near, bass.ds(G * g, G)]).then_inc(m_near[s], 1)

                beside(0, 0, 0)
                with ac.Fori(0, GROUPS // 2) as t:
                    for s in range(2):
                        if s == 0:
                            beside(2 * t + 1, 1, t)
                        if kind in ("plain", "weighted"):
                            ac.wait_ge(m_gathered[s], t + 2)
                            if mlp is not None:
                                ac.wait_ge(m_sum[s], t + 1)
                            ac.wait_ge(m_added[s], t + 1)
                            ac.copy(msg[:, s, :, 0:3 * width], gath[s][:, :, 0:3 * width]).then_inc(m_msg[s], 1)
                        elif kind == "softmax":
                            ac.wait_ge(m_part[s], t + 1)
                            ac.activation(small[:, s, 1, :], small[:, s, 0, :], ACT.Exp).then_inc(m_kept[s], 1)
                            ac.wait_ge(m_kept[s], t + 2)
                            ac.wait_ge(m_sum[s], t + 1)
                            ac.wait_ge(m_added[s], t + 1)
                            for j in range(G):
                                op = ac.activation(msg_f[:, s, j, :], wide[:, s, j * width:(j + 1) * width], ACT.Copy,
                                                   scale=small[:, s, 1, j:j + 1])
                            op.then_inc(m_msg[s], 1)
                        if s == 1:
                            beside(2 * t + 2, 0, t + 1)

            @block.tensor
            def _(pe):
                regs = {f: [pe.alloc_register(f"{name}_{f}_{j}") for j in range(2 * G)] for f in kinds + [acc_off[into]]}

                def gather(at, s, k):
                    pe.wait_ge(m_marked[s], k + 2)
                    pe.wait_ge(m_msg[s], k + 1)
                    if mlp is not None:
                        pe.wait_ge(m_kept[s], k + 1)
                    for j in range(G):
                        for mark_n, field, table, first, n, col, start, stop in gathers:
                            if field is None:
                                rhs = table[:, first:first + n]
                            else:
                                most = TW if field == OFF_GS else TD
                                rhs = table[:, bass.ds(at[field][j], most)][:, first:first + n]
                            mm = pe.matmul(gath[s][:, j, col:col + n], marks[:, s, mark_n, j * P:(j + 1) * P], rhs,
                                           start=start, stop=stop)
                    mm.then_inc(m_gathered[s], 1)

                def add(at, s, k):
                    if kind == "maximum":
                        return
                    pe.wait_ge(m_msg[s], k + 2)
                    pe.wait_ge(m_picked[s], k + 2)
                    for j in range(G):
                        sums = acc[:, bass.ds(at[j], width)]
                        if kind == "softmax":
                            mm = pe.matmul(sums, pick_f[:, s, j, :], msg_f[:, s, j, :], start=False, stop=False, skip_group_check=True)
                            continue
                        for q in range(3 if kind == "weighted" else 1):
                            for r in range(3):
                                mm = pe.matmul(sums, pick[:, s, j, q, :], msg[:, s, j, r * width:(r + 1) * width],
                                               start=False, stop=False, skip_group_check=True)
                    mm.then_inc(m_added[s], 1)

                if kind != "maximum":
                    clear_acc(pe)
                gather({f: offsets(pe, f, 0, regs[f][0:G], table_most[f]) for f in kinds}, 0, 0)
                with pe.Fori(0, GROUPS // 2) as t:
                    here = {f: offsets(pe, f, 2 * G * t + G, regs[f], table_most[f]) for f in kinds}
                    if kind != "maximum":
                        to = offsets(pe, acc_off[into], 2 * G * t, regs[acc_off[into]], ACC_MAX)
                    else:
                        to = [0] * 2 * G
                    gather({f: here[f][0:G] for f in kinds}, 1, t)
                    add(to[0:G], 0, t)
                    gather({f: here[f][G:2 * G] for f in kinds}, 0, t + 1)
                    add(to[G:2 * G], 1, t)
                for rs in regs.values():
                    for r in rs:
                        pe.free_register(r)

    l_in, l_tp, l_xt, l_mm, l_out, l_sent, l_back = (
        [sem(f"l_{what}{s}") for s in range(2)] for what in ("in", "tp", "xt", "mm", "out", "sent", "back"))
    s_ld, s_ve, s_ac = sem("s_ld"), sem("s_ve"), sem("s_ac")
    with nc.Block() as block:
        @block.gpsimd
        def _(gp):
            for m in l_tp + l_in + l_xt + l_mm + l_out + l_back:
                gp.sem_inc(m, 1)
            gp.memset(edge_a[:, :], 0.0)
            gp.memset(edge_b[:, :], 0.0)
            gp.memset(cat[:, :, :], 0.0)
            gp.memset(cat2[:, :, :], 0.0)
            gp.memset(t_src[:, :, :], 0.0)
            gp.memset(t_dst[:, :, :], 0.0)

    def linear(name, x, k_dim, m, finish, store=None, chunks=NCH):
        c0 = counted["linear"] + 1
        counted["linear"] += chunks // 2
        sent0 = counted["sent"]
        if store is not None:
            counted["sent"] += chunks // 2
        turned = [work[:, s * BANK:s * BANK + P] for s in range(2)]
        product = [work[:, (2 + s) * BANK:(2 + s) * BANK + m] for s in range(2)]
        with nc.Block() as block:
            @block.scalar
            def _(ac):
                with ac.Fori(0, chunks // 2) as t:
                    for s in range(2):
                        ac.wait_ge(l_tp[s], t + c0)
                        ac.copy(xt[:, s, 0, 0:k_dim], x(2 * t + s)).then_inc(l_in[s], 1)
                    for s in range(2):
                        ac.wait_ge(l_tp[s], t + c0 + 1)
                        ac.wait_ge(l_mm[s], t + c0)
                        ac.copy(xt[0:k_dim, s, 1, :], turned[s][0:k_dim, :]).then_inc(l_xt[s], 1)

            @block.tensor
            def _(pe):
                with pe.Fori(0, chunks // 2) as t:
                    for s in range(2):
                        pe.wait_ge(l_in[s], t + c0 + 1)
                        pe.wait_ge(l_xt[s], t + c0)
                        pe.transpose(turned[s], xt[:, s, 0, :], ident[:, :]).then_inc(l_tp[s], 1)
                    for s in range(2):
                        pe.wait_ge(l_xt[s], t + c0 + 1)
                        pe.wait_ge(l_out[s], t + c0)
                        pe.matmul(product[s], xt[0:k_dim, s, 1, :], w_sb[0:k_dim, 0:m], start=True, stop=True).then_inc(l_mm[s], 1)

            @block.vector
            def _(ve):
                with ve.Fori(0, chunks // 2) as t:
                    for s in range(2):
                        ve.wait_ge(l_mm[s], t + c0 + 1)
                        if store is not None:
                            ve.wait_ge(l_back[s], t + sent0 + 1)
                        finish(ve, 2 * t + s, s, product[s]).then_inc(l_out[s], 1)

            if store is not None:
                @block.sync
                def _(sp):
                    with sp.Fori(0, chunks // 2) as t:
                        for s in range(2):
                            sp.wait_ge(l_out[s], t + c0 + 1)
                            store(sp, 2 * t + s, s).then_inc(l_sent[s], 16)
                        for s in range(2):
                            sp.wait_ge(l_sent[s], 16 * (t + sent0 + 1))
                            sp.sem_inc(l_back[s], 1)

    def flat(ap):
        return ap.rearrange("p a d -> p (a d)")

    def chunk(buf, c, n):
        return flat(buf[:, bass.ds(c, 1), 0:n])

    def stepper(ve):
        def step(op):
            op.then_inc(s_ve, 1)
            counted["ve"] += 1
            ve.wait_ge(s_ve, counted["ve"])
        return step

    def split(ve, step, x, hi, mid, lo, rest):
        step(ve.tensor_copy(hi, x))
        step(ve.tensor_tensor(rest, x, hi, ALU.subtract))
        step(ve.tensor_copy(mid, rest))
        step(ve.tensor_tensor(lo, rest, mid, ALU.subtract))

    def layernorm(before):
        mean, var = stat[:, 0, :], stat[:, 1, :]
        counted["ac"] += 1
        with nc.Block() as block:
            @block.vector
            def _(ve):
                step = stepper(ve)
                before(ve, step)
                step(ve.tensor_reduce(mean, xs[:, :, :], AX.X, ALU.add))
                step(ve.tensor_scalar(mean, mean, 1.0 / D, None, ALU.mult))
                step(ve.tensor_tensor(hs[:, :, :], xs[:, :, :], mean.unsqueeze(2).to_broadcast([P, NCH, D]), ALU.subtract))
                step(ve.tensor_tensor(cat[:, :, 0:D], hs[:, :, :], hs[:, :, :], ALU.mult))
                step(ve.tensor_reduce(var, cat[:, :, 0:D], AX.X, ALU.add))
                step(ve.tensor_scalar(var, var, 1.0 / D, EPS, ALU.mult, ALU.add))
                counted["sqrt"] = counted["ve"]
                ve.wait_ge(s_ac, counted["ac"])
                step(ve.reciprocal(var, mean))
                step(ve.tensor_tensor(hs[:, :, :], hs[:, :, :], var.unsqueeze(2).to_broadcast([P, NCH, D]), ALU.mult))
                step(ve.tensor_scalar(hs[:, :, :], hs[:, :, :], 0.0, None, ALU.max))

            @block.scalar
            def _(ac):
                ac.wait_ge(s_ve, counted["sqrt"])
                ac.activation(mean, var, ACT.Sqrt).then_inc(s_ac, 1)

    def weights(loads):
        counted["load"] += 16 * len(loads)
        with nc.Block() as block:
            @block.sync
            def _(sp):
                for dest, what in loads:
                    sp.dma_start(dest, what).then_inc(s_ld, 16)
                sp.wait_ge(s_ld, counted["load"])

    banks = [b for b in range(4) if b * APB < NCH]

    W0 = D + 1
    layernorm(lambda ve, step: None)
    with nc.Block() as block:
        @block.vector
        def _(ve):
            step = stepper(ve)
            step(ve.memset(t_src[:, :, 0:3 * W0], 0.0))
            step(ve.memset(t_src[:, :, D:W0], 1.0))
            split(ve, step, hs[:, :, :], t_src[:, :, 0:D], t_src[:, :, W0:W0 + D], t_src[:, :, 2 * W0:2 * W0 + D], cat[:, :, 0:D])
            step(ve.tensor_copy(iota_bf[:, :], iota_n[:, :]))
    edge_pass("l0", [(0, False)], "dst", W0, [(0, OFF_GS, t_src_f, 0, 3 * W0, 0, True, True)], "plain")
    weights([(w_sb[0:D, 0:D], i["L0_gnn_W"])])
    counted["ac"] += 1
    with nc.Block() as block:
        @block.vector
        def _(ve):
            step = stepper(ve)
            for b in banks:
                lo, hi, a = bank_chunks(b)
                step(ve.tensor_tensor(hs[:, lo:hi, :], hs[:, lo:hi, :], a[:, :, 0:D], ALU.add))
                step(ve.tensor_scalar(deg[:, lo:hi], a[:, :, D], 1.0, None, ALU.max))
            counted["sqrt"] = counted["ve"]
            ve.wait_ge(s_ac, counted["ac"])
            step(ve.reciprocal(deg[:, :], stat[:, 0, :]))

        @block.scalar
        def _(ac):
            ac.wait_ge(s_ve, counted["sqrt"])
            ac.activation(stat[:, 0, :], deg[:, :], ACT.Sqrt).then_inc(s_ac, 1)
    linear("lin0", lambda c: chunk(hs, c, D), D, D,
           lambda ve, c, s, y: ve.tensor_scalar(chunk(cat, c, D), y, deg[:, bass.ds(c, 1)], None, ALU.mult))
    with nc.Block() as block:
        @block.scalar
        def _(ac):
            ac.activation(hs[:, :, :], cat[:, :, 0:D], ACT.Tanh)

    layernorm(lambda ve, step: step(ve.tensor_tensor(xs[:, :, :], xs[:, :, :], hs[:, :, :], ALU.add)))
    with nc.Block() as block:
        @block.vector
        def _(ve):
            ve.memset(cat2[:, 0:2, 0:D], 0.0)
    weights([(w_sb[0:D, 0:D], i["W_node_T"]), (w_sb[0:D, D:2 * D], i["W_rel_T"]),
             (cat2[:, 0, 0:D], i["L1_gnn_rel_emb"][0:P, :]), (cat2[0:N_REL - P, 1, 0:D], i["L1_gnn_rel_emb"][P:N_REL, :])]
            + [(biases[:, j, :], i["L1_gnn_attvec"][0:1, j * D:(j + 1) * D].to_broadcast([P, D])) for j in range(3)])
    linear("lin1", lambda c: chunk(hs, c, D), D, D, lambda ve, c, s, y: ve.tensor_copy(chunk(cat, c, D), y))
    with nc.Block() as block:
        @block.vector
        def _(ve):
            ve.tensor_copy(w_sb[0:D, 0:D], w_sb[0:D, D:2 * D])
    linear("linr", lambda c: chunk(cat2, c, D), D, D, lambda ve, c, s, y: ve.tensor_copy(chunk(rel_f, c, D), y), chunks=2)

    SP3 = 3 * W0
    with nc.Block() as block:
        @block.vector
        def _(ve):
            step = stepper(ve)
            tmp, tmp2 = cat2[:, :, 0:D], cat2[:, :, D:2 * D]
            step(ve.memset(t_dst[:, :, :], 0.0))
            step(ve.memset(t_dst[:, :, D:W0], 1.0))
            step(ve.memset(rel_t[:, :, :], 0.0))
            split(ve, step, cat[:, :, 0:D], t_dst[:, :, 0:D], t_dst[:, :, W0:W0 + D], t_dst[:, :, 2 * W0:2 * W0 + D], tmp)
            split(ve, step, rel_f[:, :, 0:D], rel_t[:, :, 0:D], rel_t[:, :, W0:W0 + D], rel_t[:, :, 2 * W0:2 * W0 + D], tmp[:, 0:2, :])
            for j, (rows_in, n, table, first) in enumerate(((cat, NCH, t_src, 0), (cat, NCH, t_dst, SP3), (rel_f, 2, rel_t, SP3))):
                step(ve.tensor_tensor(tmp[:, 0:n, :], rows_in[:, 0:n, 0:D], biases[:, j, :].unsqueeze(1).to_broadcast([P, n, D]), ALU.mult))
                step(ve.tensor_reduce(stat[:, 0, 0:n], tmp[:, 0:n, :], AX.X, ALU.add))
                split(ve, step, stat[:, 0, 0:n], table[:, 0:n, first], table[:, 0:n, first + 1], table[:, 0:n, first + 2], stat[:, 1, 0:n])
    rel_tf = flat(rel_t[:, :, :])
    edge_pass("l1max", [(0, False), (1, False), (2, False), (2, True)], "src", 0, [
        (0, OFF_GS, t_src_f, 0, 3, 0, True, False), (1, OFF_GD, t_dst_f, SP3, 3, 0, False, False),
        (2, None, rel_tf, SP3, 3, 0, False, False), (3, None, rel_tf, TD + SP3, 3, 0, False, True)], "maximum")

    with nc.Block() as block:
        @block.vector
        def _(ve):
            ve.tensor_tensor(cat[:, :, :], cat[:, :, :], cat2[:, :, :], ALU.max)

        @block.gpsimd
        def _(gp):
            for m in x_tp + x_out:
                gp.sem_inc(m, 1)
    with nc.Block() as block:
        @block.scalar
        def _(ac):
            with ac.Fori(0, NCH // 2) as t:
                for s in range(2):
                    ac.wait_ge(x_tp[s], t + 1)
                    ac.copy(xt[:, s, 0, :], chunk(cat, 2 * t + s, P)).then_inc(x_in[s], 1)

        @block.tensor
        def _(pe):
            with pe.Fori(0, NCH // 2) as t:
                for s in range(2):
                    pe.wait_ge(x_in[s], t + 1)
                    pe.wait_ge(x_out[s], t + 1)
                    pe.transpose(work[:, s * BANK:s * BANK + P], xt[:, s, 0, :], ident[:, :]).then_inc(x_tp[s], 1)

        @block.vector
        def _(ve):
            with ve.Fori(0, NCH // 2) as t:
                for s in range(2):
                    ve.wait_ge(x_tp[s], t + 2)
                    ve.tensor_reduce(stat[:, 0, bass.ds(2 * t + s, 1)], work[:, s * BANK:s * BANK + P], AX.X, ALU.max).then_inc(x_out[s], 1)
    with nc.Block() as block:
        @block.vector
        def _(ve):
            split(ve, stepper(ve), stat[:, 0, :], t_src[:, :, 0], t_src[:, :, 1], t_src[:, :, 2], stat[:, 1, :])
    edge_pass("l1sum", [(0, False), (1, False), (2, False), (2, True)], "src", W0, [
        (1, OFF_GD, t_dst_f, 0, 3 * W0, 0, True, False),
        (2, None, rel_tf, 0, 3 * W0, 0, False, False), (3, None, rel_tf, TD, 3 * W0, 0, False, True),
        (0, OFF_GS, t_src_f, 0, 3, SP3, True, True)], "softmax")
    with nc.Block() as block:
        @block.vector
        def _(ve):
            step = stepper(ve)
            for b in banks:
                lo, hi, a = bank_chunks(b)
                step(ve.tensor_copy(hs[:, lo:hi, :], a[:, :, 0:D]))
                step(ve.tensor_scalar(deg[:, lo:hi], a[:, :, D], 1e-12, None, ALU.add))
            step(ve.reciprocal(deg[:, :], deg[:, :]))
            step(ve.tensor_tensor(hs[:, :, :], hs[:, :, :], deg[:, :].unsqueeze(2).to_broadcast([P, NCH, D]), ALU.mult))

    layernorm(lambda ve, step: step(ve.tensor_tensor(xs[:, :, :], xs[:, :, :], hs[:, :, :], ALU.add)))
    weights([(w_sb[0:D, :].rearrange("i (r h) -> i r h", r=N_TYPE), i["L2_gnn_W"].rearrange("r i h -> i r h"))])
    xw_rows = xw.rearrange("(r n) d -> n r d", r=N_TYPE)
    linear("lin2", lambda c: chunk(hs, c, D), D, N_TYPE * D, lambda ve, c, s, y: ve.tensor_copy(wide[:, s, :], y),
           store=lambda sp, c, s: sp.dma_start(xw_rows[bass.ds(P * c, P), :, :], wide[:, s, :].rearrange("p (r d) -> p r d", r=N_TYPE)))

    ty_idx = sb("ty_idx", [P, 2, G], U32)
    ty_msg = sb("ty_msg", [P, 2, G, D], F32)
    ty_chosen, ty_rows, ty_picked, ty_added = ([sem(f"ty_{what}{s}") for s in range(2)]
                                               for what in ("chosen", "rows", "picked", "added"))
    with nc.Block() as block:
        @block.gpsimd
        def _(gp):
            for m in ty_added:
                gp.sem_inc(m, 1)
    with nc.Block() as block:
        @block.vector
        def _(ve):
            with ve.Fori(0, GROUPS // 2) as t:
                for s in range(2):
                    g = 2 * t + s
                    ve.wait_ge(ty_added[s], t + 1)
                    ve.tensor_tensor(pick_f[:, s, :, :], iota_n[:, :].unsqueeze(1).to_broadcast([P, G, P]),
                                     dst_lo[:, 0, bass.ds(G * g, G)].unsqueeze(2).to_broadcast([P, G, P]),
                                     ALU.is_equal).then_inc(ty_picked[s], 1)

        @block.scalar
        def _(ac):
            with ac.Fori(0, GROUPS // 2) as t:
                for s in range(2):
                    ac.wait_ge(ty_added[s], t + 1)
                    ac.copy(ty_idx[:, s, :], typed_src[:, bass.ds(G * (2 * t + s), G)]).then_inc(ty_chosen[s], 1)

        @block.gpsimd
        def _(gp):
            with gp.Fori(0, GROUPS // 2) as t:
                for s in range(2):
                    gp.wait_ge(ty_chosen[s], t + 1)
                    gp.sem_inc(past, 1)
                    for j in range(G):
                        gp.indirect_dma_start(out=ty_msg[:, s, j, :], out_offset=None, in_=xw,
                                              in_offset=bass.IndirectOffsetOnAxis(ap=ty_idx[:, s, j:j + 1], axis=0)).then_inc(ty_rows[s], 16)

        @block.tensor
        def _(pe):
            regs = [pe.alloc_register(f"ty_r{j}") for j in range(G)]
            clear_acc(pe)
            with pe.Fori(0, GROUPS // 2) as t:
                for s in range(2):
                    at = offsets(pe, OFF_AD, G * (2 * t + s), regs, ACC_MAX)
                    pe.wait_ge(ty_picked[s], t + 1)
                    pe.wait_ge(ty_rows[s], 16 * G * t + 16 * G)
                    for j in range(G):
                        mm = pe.matmul(acc[:, bass.ds(at[j], D)], pick_f[:, s, j, :], ty_msg[:, s, j, :], start=False, stop=False,
                                       skip_group_check=True)
                    mm.then_inc(ty_added[s], 1)
            for r in regs:
                pe.free_register(r)

    def add_sums(ve, step):
        for b in banks:
            lo, hi, a = bank_chunks(b)
            step(ve.tensor_tensor(xs[:, lo:hi, :], xs[:, lo:hi, :], a[:, :, 0:D], ALU.add))
    layernorm(add_sums)

    def conv_loads(n, k_dim, m):
        return [(w_sb[0:k_dim, 0:m], i[f"L3_gnn_Wrel{n}"]), (w_sb[k_dim:2 * k_dim, 0:m], i[f"L3_gnn_Wroot{n}"]),
                (biases[:, 0, 0:m], i[f"L3_gnn_brel{n}"].rearrange("(o m) -> o m", o=1).to_broadcast([P, m]))]

    def mlp_loads(n, k_dim):
        wf = i[f"L3_gnn_Wf{n}"]
        return [(w_sb[0:k_dim, 0:EH], wf[0:k_dim, :]), (w_sb[0:k_dim, EH:2 * EH], wf[k_dim:2 * k_dim, :]),
                (biases[:, 1, 0:EH], i[f"L3_gnn_bf{n}"].rearrange("(o m) -> o m", o=1).to_broadcast([P, EH])),
                (biases[:, 2, 0:EH], wf[2 * k_dim:2 * k_dim + 1, :].to_broadcast([P, EH])),
                (biases[:, 3, 0:EH], i[f"L3_gnn_Wr{n}"].rearrange("h o -> o h").to_broadcast([P, EH])),
                (biases[:, 3, EH:EH + 1], i[f"L3_gnn_br{n}"].rearrange("(o m) -> o m", o=1).to_broadcast([P, 1]))]

    parts = sb("parts", [P, 3, TILES], BF16)

    def conv_tables(n, k_dim, w, net):
        if net:
            weights(mlp_loads(n, k_dim))
            linear(f"mlp{n}", lambda c: chunk(hs, c, k_dim), k_dim, 2 * EH,
                   lambda ve, c, s, y: ve.tensor_copy(chunk(cat, c, 2 * EH), y))
        with nc.Block() as block:
            @block.vector
            def _(ve):
                step = stepper(ve)
                rest = cat2[:, :, 0:k_dim]
                split(ve, step, hs[:, :, 0:k_dim], *(t_src[:, :, q * k_dim:(q + 1) * k_dim] for q in range(3)), rest)
                split(ve, step, w[:, :], *(parts[:, q, :] for q in range(3)), flat(cat2[:, :, :])[:, 0:TILES])
                step(ve.tensor_copy(dst_lo[:, 1:4, :], parts[:, :, :]))
                if net:
                    k3 = 3 * k_dim
                    rest = cat2[:, :, 0:EH]
                    split(ve, step, cat[:, :, 0:EH], *(t_src[:, :, k3 + q * EH:k3 + (q + 1) * EH] for q in range(3)), rest)
                    step(ve.tensor_tensor(cat[:, :, EH:2 * EH], cat[:, :, EH:2 * EH],
                                          biases[:, 1, 0:EH].unsqueeze(1).to_broadcast([P, NCH, EH]), ALU.add))
                    split(ve, step, cat[:, :, EH:2 * EH], *(t_dst[:, :, q * EH:(q + 1) * EH] for q in range(3)), rest)

    def conv(n, k_dim, m):
        weights(conv_loads(n, k_dim, m))
        with nc.Block() as block:
            @block.vector
            def _(ve):
                step = stepper(ve)
                for b in banks:
                    lo, hi, a = bank_chunks(b)
                    step(ve.tensor_copy(cat[:, lo:hi, 0:k_dim], a[:, :, 0:k_dim]))
                step(ve.tensor_copy(cat[:, :, k_dim:2 * k_dim], hs[:, :, 0:k_dim]))
        linear(f"conv{n}", lambda c: chunk(cat, c, 2 * k_dim), 2 * k_dim, m,
               lambda ve, c, s, y: ve.tensor_tensor(chunk(hs, c, m), y, biases[:, 0, 0:m], ALU.add))
        with nc.Block() as block:
            @block.vector
            def _(ve):
                ve.tensor_scalar(hs[:, :, 0:m], hs[:, :, 0:m], 0.0, None, ALU.max)

    for n, k_dim, m, w, dest in ((1, D, H1, weight, edge_a), (2, H1, D, edge_a, edge_b)):
        conv_tables(n, k_dim, w, True)
        k3 = 3 * k_dim
        edge_pass(f"l3_{n}", [(0, False), (1, False)], "dst", k_dim, [
            (0, OFF_GS, t_src_f, 0, k3 + 2 * EH, 0, True, False), (0, OFF_GS, t_src_f, k3 + 2 * EH, EH, k3 + EH, False, False),
            (1, OFF_GD, t_dst_f, 0, 2 * EH, k3, False, False), (1, OFF_GD, t_dst_f, 2 * EH, EH, k3 + EH, False, True)],
            "weighted", share=w, mlp=(biases[:, 2, 0:EH], biases[:, 3, 0:EH], biases[:, 3, EH:EH + 1], dest))
        conv(n, k_dim, m)
    conv_tables(3, D, edge_b, False)
    edge_pass("l3_3", [(0, False)], "dst", D, [(0, OFF_GS, t_src_f, 0, 3 * D, 0, True, True)], "weighted")
    conv(3, D, D)
    with nc.Block() as block:
        @block.vector
        def _(ve):
            ve.tensor_tensor(xs[:, :, :], xs[:, :, :], hs[:, :, :], ALU.add)
    s_out = sem("s_out")
    with nc.Block() as block:
        @block.sync
        def _(sp):
            sp.dma_start(out[0:FULL * P, :].rearrange("(c p) d -> p c d", p=P), xs[:, 0:FULL, :]).then_inc(s_out, 16)
            sp.dma_start(out[FULL * P:N_NODES, :], xs[0:TAIL, FULL, :]).then_inc(s_out, 16)
            sp.wait_ge(s_out, 32)


def kernel(**inputs):
    import numpy as np
    import concourse.bacc as bacc
    from concourse import mybir
    from concourse.bass_utils import run_bass_kernel_spmd

    host = {name: np.ascontiguousarray(a) for name, a in inputs.items()}
    host["W_node_T"] = np.ascontiguousarray(host.pop("L1_gnn_W_node").T)
    host["W_rel_T"] = np.ascontiguousarray(host.pop("L1_gnn_W_rel").T)
    nc = bacc.Bacc("TRN2", target_bir_lowering=False, num_devices=1)
    arrays, aps = {}, {}
    for name, a in host.items():
        arrays[f"in_{name}"] = a
        aps[name] = nc.dram_tensor(f"in_{name}", a.shape, mybir.dt.from_np(a.dtype), kind="ExternalInput").ap()
    out = nc.dram_tensor("out", (N_NODES, D), mybir.dt.float32, kind="ExternalOutput").ap()
    build(nc, aps, out)
    return run_bass_kernel_spmd(nc, [arrays], core_ids=[0]).results[0]["out"]
```

```python
from contextlib import ExitStack

import concourse.bass as bass
from concourse import mybir

ALU = mybir.AluOpType
ACT = mybir.ActivationFunctionType
AX = mybir.AxisListType
F32 = mybir.dt.float32
F16 = mybir.dt.float16
BF16 = mybir.dt.bfloat16
I32 = mybir.dt.int32
U32 = mybir.dt.uint32

P = 128
N_NODES = 3125
N_EDGES = 100000
D = 64
N_REL = 200
N_TYPE = 8
H1 = 32
EH = 32
CH = -(-N_NODES // P)
NCH = CH + CH % 2
NP_ = NCH * P
FULL = N_NODES // P
TAIL = N_NODES - FULL * P
EP = 125
EC = N_EDGES // EP
HALF = EC // 2
RG = 4
SLOTS = 2 * RG
NB = CH * CH
G = 4
MAX_TILES = (N_EDGES + (P - 1) * NB) // P
U = 4
TURNS = -(-MAX_TILES // (U * G))
GROUPS = U * TURNS
TILES = (GROUPS + 2) * G
TROWS = -(-TILES // P)
TURNS2 = -(-((N_EDGES + (P - 1) * CH) // P) // (U * G))
TILES2 = TURNS2 * U * G
PAIR = 4
PADS = 192
REC = 8
TW = 200
TD = 200
GW = 256
AW = 72
BANK = 512
APB = BANK // AW
FAR = 2.0 ** 100
EPS = 1e-5
assert EP * EC == N_EDGES and EC % (4 * RG) == 0 and EP <= P


def build(nc, i, out):
    with ExitStack() as ctx:
        program(nc, ctx, i, out)


def program(nc, ctx, i, out):
    names = iter(range(10**6))

    def sb(name, shape, dt, at=ctx):
        return at.enter_context(nc.sbuf_tensor(f"{name}_{next(names)}", shape, dt))

    def sem(name):
        return ctx.enter_context(nc.semaphore(f"{name}_{next(names)}"))

    past = sem("past")

    rec = nc.dram_tensor("rec", [P * TILES, REC], F32, kind="Internal").ap()
    rows = nc.dram_tensor("rows", [3, TILES, P], F16, kind="Internal").ap()
    offs_d = nc.dram_tensor("offs_d", [8 * TROWS, P], I32, kind="Internal").ap()
    rec2 = nc.dram_tensor("rec2", [P * (TILES2 + TILES), PAIR], F32, kind="Internal").ap()
    rows2 = nc.dram_tensor("rows2", [TILES2, P], F16, kind="Internal").ap()
    node_rows = {w: nc.dram_tensor(f"node_rows{w}", [NP_, w], F32, kind="Internal").ap() for w in sorted({D + EH, D, H1 + EH})}
    xw = nc.dram_tensor("xw", [N_TYPE * NP_, D], F32, kind="Internal").ap()

    acc = ctx.enter_context(nc.psum_tensor("acc", [P, 4 * BANK], F32))
    work = ctx.enter_context(nc.psum_tensor("work", [P, 4 * BANK], F32))

    lane = sb("lane", [P, 1], F32)
    lane_hi = sb("lane_hi", [P, 1], F32)
    iota_n = sb("iota_n", [P, P], F32)
    ident = sb("ident", [P, P], F32)
    zeros = sb("zeros", [P, BANK], BF16)
    src_lo = sb("src_lo", [P, TILES], F32)
    dst_lo = sb("dst_lo", [P, TILES], F32)
    pair = sb("pair", [P, TILES, PAIR], F32)
    address2 = sb("address2", [P, TILES], U32)
    pair2 = sb("pair2", [P, TILES2, PAIR], F32)
    offs = sb("offs", [1, 7, TROWS * P], I32)
    OFF_GS, OFF_GD, OFF_AD, OFF_AS, OFF_RS, OFF_AD2, OFF_GD2, MOVED = range(8)
    xs = sb("xs", [P, NCH, D], F32)
    hs = sb("hs", [P, NCH, D], F32)
    xt = sb("xt", [P, 2, 2, P], F32)
    deg = sb("deg", [P, NCH], F32)

    def bank_chunks(b):
        lo, hi = b * APB, min((b + 1) * APB, NCH)
        n = hi - lo
        return lo, hi, acc[:, b * BANK:b * BANK + n * AW].rearrange("p (c w) -> p c w", w=AW)

    with ExitStack() as edges:
        bucket = sb("bucket", [EP, EC + 1], F32, edges)
        record = sb("record", [EP, EC, REC], F32, edges)
        iota_b = sb("iota_b", [P, NB], F16, edges)
        onehot = sb("onehot", [EP, SLOTS, NB], BF16, edges)
        ones = sb("ones", [P, P], BF16, edges)
        before = sb("before", [P, P], BF16, edges)
        notbefore = sb("notbefore", [P, P], BF16, edges)
        counts = [work[:, 2 * half * BANK:2 * (half + 1) * BANK] for half in range(2)]
        h_made, h_used = sem("h_made"), sem("h_used")
        r_made, r_ready, r_read, r_step = sem("r_made"), sem("r_ready"), sem("r_read"), sem("r_step")
        r_staged, r_sent, r_free = ([sem(f"r_{what}{g}") for g in range(2)] for what in ("staged", "sent", "free"))
        s_in, s_const, s_prep, s_pad, s_x = sem("s_in"), sem("s_const"), sem("s_prep"), sem("s_pad"), sem("s_x")
        with ExitStack() as tmp, nc.Block() as block:
            raw = sb("raw", [EP, 5, EC], I32, tmp)
            part = sb("part", [EP, 4, EC], I32, tmp)
            padrow = sb("padrow", [P, PADS, REC], F32, tmp)

            @block.sync
            def _(sp):
                for n, name in enumerate(("src", "dst", "edge_type_200", "edge_type_8")):
                    sp.dma_start(raw[:, n, :], i[name].rearrange("(p c) -> p c", p=EP)).then_inc(s_in, 16)
                sp.dma_start(raw[:, 4, :].bitcast(F32), i["edge_weight"].rearrange("(p c) -> p c", p=EP)).then_inc(s_in, 16)
                sp.wait_ge(s_const, 3)
                sp.dma_start(xs[:, 0:FULL, :], i["x"][0:FULL * P, :].rearrange("(c p) d -> p c d", p=P)).then_inc(s_x, 16)
                sp.dma_start(xs[0:TAIL, FULL, :], i["x"][FULL * P:N_NODES, :]).then_inc(s_x, 16)
                sp.wait_ge(s_const, 5)
                rec_rows = rec.rearrange("(p t) r -> p (t r)", p=P)
                for a in range(0, TILES, PADS):
                    n = min(PADS, TILES - a)
                    sp.dma_start(rec_rows[:, a * REC:(a + n) * REC],
                                 padrow[:, 0:n, :].rearrange("p t r -> p (t r)")).then_inc(s_pad, 16)
                sp.dma_start(rec2[0:P * TILES2, :].rearrange("(p t) r -> p t r", p=P), pair2[:, :, :]).then_inc(s_pad, 16)
                sp.wait_ge(s_pad, 16 * -(-TILES // PADS) + 16)
                sp.wait_ge(s_x, 32)

            @block.gpsimd
            def _(gp):
                for m in r_free:
                    gp.sem_inc(m, 1)
                gp.sem_inc(r_read, 2)
                gp.sem_inc(h_used, SLOTS)
                gp.memset(record[:, :, 6:REC], 0.0)
                gp.memset(bucket[:, EC:EC + 1], -1.0)
                gp.memset(ones[:, :], 1.0).then_inc(s_const, 1)
                gp.memset(zeros[:, :], 0.0).then_inc(s_const, 1)
                gp.memset(xs[:, :, :], 0.0).then_inc(s_const, 1)
                gp.memset(padrow[:, :, :], 0.0).then_inc(s_const, 1)
                gp.wait_ge(s_const, 4)
                gp.memset(pair2[:, :, 0], -1.0)
                gp.memset(pair2[:, :, 1:PAIR], 0.0)
                gp.memset(padrow[:, :, 0:3], -1.0).then_inc(s_const, 1)
                gp.iota(iota_n[:, :], pattern=[[1, P]], base=0, channel_multiplier=0, allow_small_or_imprecise_dtypes=True)
                gp.iota(lane[:, :], pattern=[[0, 1]], base=0, channel_multiplier=1, allow_small_or_imprecise_dtypes=True)
                gp.iota(lane_hi[:, :], pattern=[[0, 1]], base=P, channel_multiplier=1, allow_small_or_imprecise_dtypes=True)
                gp.iota(iota_b[:, :], pattern=[[1, NB]], base=0, channel_multiplier=0, allow_small_or_imprecise_dtypes=True)
                gp.memset(onehot[:, :, :], 0.0).then_inc(s_const, 1)

            @block.vector
            def _(ve):
                n = 0
                ve.wait_ge(s_in, 16 * 5)
                for j in range(2):
                    ve.tensor_scalar(part[:, j, :], raw[:, j, :], P - 1, None, ALU.bitwise_and).then_inc(s_prep, 1)
                    ve.tensor_scalar(part[:, 2 + j, :], raw[:, j, :], 7, None, ALU.arith_shift_right).then_inc(s_prep, 1)
                ve.wait_ge(s_prep, 4)
                for j in range(2):
                    ve.tensor_copy(record[:, :, j], part[:, j, :])
                ve.tensor_copy(record[:, :, 2], raw[:, 2, :])
                ve.tensor_copy(record[:, :, 5], raw[:, 0, :])
                ve.tensor_copy(record[:, :, 3], raw[:, 4, :].bitcast(F32))
                ve.scalar_tensor_tensor(out=record[:, :, 4], in0=raw[:, 3, :], scalar=float(NP_), in1=raw[:, 0, :],
                                        op0=ALU.mult, op1=ALU.add)
                ve.scalar_tensor_tensor(out=bucket[:, 0:EC], in0=part[:, 2, :], scalar=float(CH), in1=part[:, 3, :],
                                        op0=ALU.mult, op1=ALU.add)
                ve.wait_ge(s_const, 6)
                ve.tensor_scalar(ident[:, :], iota_n[:, :], lane[:, 0:1], None, ALU.is_equal)
                ve.tensor_scalar(before[:, :], iota_n[:, :], lane[:, 0:1], None, ALU.is_gt)
                ve.tensor_scalar(notbefore[:, :], iota_n[:, :], lane[:, 0:1], None, ALU.is_le)
                ve.memset(hs[:, :, :], 0.0)
                ve.memset(xt[:, :, :, :], 0.0)

        with nc.Block() as block:
            @block.vector
            def _(ve):
                with ve.Fori(0, HALF // RG) as t:
                    for k in range(RG):
                        for half in range(2):
                            ve.wait_ge(h_used, SLOTS * t + 2 * k + half + 1)
                            ve.tensor_scalar(onehot[:, 2 * k + half, :], iota_b[0:EP, :],
                                             bucket[:, bass.ds(RG * t + (half * HALF + k), 1)], None, ALU.is_equal).then_inc(h_made, 1)

            @block.tensor
            def _(pe):
                for b in range(4):
                    pe.matmul(work[:, b * BANK:(b + 1) * BANK], zeros[:, 0:P], zeros[:, :], start=True, stop=True)
                with pe.Fori(0, HALF // RG) as t:
                    for k in range(SLOTS):
                        pe.wait_ge(h_made, SLOTS * t + k + 1)
                        to = counts[k % 2]
                        pe.matmul(to[:, 0:BANK], ones[0:EP, :], onehot[:, k, 0:BANK], start=False, stop=False, skip_group_check=True)
                        pe.matmul(to[:, BANK:NB], ones[0:EP, :], onehot[:, k, BANK:NB], start=False, stop=False,
                                  skip_group_check=True).then_inc(h_used, 1)

        with ExitStack() as tmp:
            base_hi = sb("base_hi", [1, NB], BF16, edges)
            base_lo = sb("base_lo", [1, NB], BF16, edges)
            ni = sb("ni", [P, NB], I32, tmp)
            nt = sb("nt", [P, NB], F32, tmp)
            one_f = sb("one_f", [P, NB], F32, tmp)
            ends = sb("ends", [P, NB], F32, tmp)
            starts = sb("starts", [P, NB], I32, tmp)
            st_a = sb("st_a", [1, NB], I32, tmp)
            less = sb("less", [P, NB], F32, tmp)
            tile_no = sb("tile_no", [P, TROWS], F32, tmp)
            tb = sb("tb", [P, TROWS], F32, tmp)
            steps = sb("steps", [P, CH - 1], F32, tmp)
            ge = sb("ge", [P, TROWS, CH], F32, tmp)
            tcs = sb("tcs", [P, 2, TROWS], F32, tmp)
            tbank = sb("tbank", [P, 2, TROWS], F32, tmp)
            fld = sb("fld", [P, 8, TROWS], F32, tmp)
            fld_t = sb("fld_t", [8 * TROWS, P], I32, tmp)
            count = sb("count", [P, NB], F32, tmp)
            before_src = sb("before_src", [P, CH + 1, CH], F32, tmp)
            moved = sb("moved", [P, NB], F32, tmp)
            n2 = sb("n2", [P, 4, CH], F32, tmp)
            n2_i = sb("n2_i", [P, 2, CH], I32, tmp)
            chunk2 = sb("chunk2", [P, 2, TROWS], F32, tmp)
            s_i, s_v, s_t, s_c, s_o = sem("s_i"), sem("s_v"), sem("s_t"), sem("s_c"), sem("s_o")
            with nc.Block() as block:
                @block.gpsimd
                def _(gp):
                    gp.iota(tile_no[:, :], pattern=[[P, TROWS]], base=0, channel_multiplier=1, allow_small_or_imprecise_dtypes=True)
                    gp.iota(steps[:, :], pattern=[[1, CH - 1]], base=1, channel_multiplier=0, allow_small_or_imprecise_dtypes=True)
                    gp.memset(onehot[:, SLOTS - 2:SLOTS, :], 0.0)
                    gp.memset(one_f[:, :], 1.0).then_inc(s_i, 1)

                @block.vector
                def _(ve):
                    n = 0

                    def step(op):
                        nonlocal n
                        op.then_inc(s_v, 1)
                        n += 1
                        ve.wait_ge(s_v, n)

                    ve.wait_ge(s_i, 1)
                    step(ve.tensor_copy(nt[:, :], counts[0][:, 0:NB]))
                    step(ve.scalar_tensor_tensor(out=ni[:, :], in0=counts[1][:, 0:NB], scalar=float(P - 1), in1=nt[:, :],
                                                 op0=ALU.add, op1=ALU.add))
                    step(ve.tensor_scalar(starts[:, :], ni[:, :], 7, None, ALU.arith_shift_right))
                    step(ve.tensor_copy(nt[:, :], starts[:, :]))
                    step(ve.tensor_tensor_scan(ends[:, :], one_f[:, :], nt[:, :], 0.0, ALU.mult, ALU.add))
                    step(ve.tensor_tensor(starts[:, :], ends[:, :], nt[:, :], ALU.subtract))
                    step(ve.tensor_scalar(st_a[:, :], starts[0:1, :], 31, None, ALU.bitwise_and))
                    step(ve.tensor_scalar(base_lo[:, :], st_a[:, :], float(P), None, ALU.mult))
                    step(ve.tensor_scalar(st_a[:, :], starts[0:1, :], 5, None, ALU.arith_shift_right))
                    step(ve.tensor_scalar(base_hi[:, :], st_a[:, :], float(32 * P), None, ALU.mult))
                    for k in range(TROWS):
                        step(ve.tensor_scalar(less[:, :], ends[:, :], tile_no[:, k:k + 1], None, ALU.is_le))
                        step(ve.tensor_reduce(tb[:, k:k + 1], less[:, :], AX.X, ALU.add))
                    step(ve.tensor_scalar(tb[:, :], tb[:, :], float(NB - 1), None, ALU.min))
                    step(ve.tensor_scalar(less[:, 0:CH - 1], steps[:, :], float(CH), None, ALU.mult))
                    step(ve.tensor_tensor(ge[:, :, 0:CH - 1], tb[:, :].unsqueeze(2).to_broadcast([P, TROWS, CH - 1]),
                                          less[:, 0:CH - 1].unsqueeze(1).to_broadcast([P, TROWS, CH - 1]), ALU.is_ge))
                    step(ve.tensor_reduce(tcs[:, 0, :], ge[:, :, 0:CH - 1], AX.X, ALU.add))
                    step(ve.scalar_tensor_tensor(out=tcs[:, 1, :], in0=tcs[:, 0, :], scalar=-float(CH), in1=tb[:, :],
                                                 op0=ALU.mult, op1=ALU.add))
                    nb = CH // APB
                    step(ve.tensor_scalar(less[:, 0:nb], steps[:, 0:nb], float(APB), None, ALU.mult))
                    for j in range(2):
                        step(ve.tensor_tensor(ge[:, :, 0:nb], tcs[:, j, :].unsqueeze(2).to_broadcast([P, TROWS, nb]),
                                              less[:, 0:nb].unsqueeze(1).to_broadcast([P, TROWS, nb]), ALU.is_ge))
                        step(ve.tensor_reduce(tbank[:, j, :], ge[:, :, 0:nb], AX.X, ALU.add))
                    step(ve.tensor_scalar(tbank[:, :, :], tbank[:, :, :], float(BANK - APB * AW), None, ALU.mult))
                    for j, f, w in ((0, OFF_GS, TW), (1, OFF_GD, TD)):
                        step(ve.tensor_scalar(fld[:, f, :], tcs[:, j, :], float(w), None, ALU.mult))
                    step(ve.tensor_scalar(fld[:, OFF_RS, :], tcs[:, 0, :], float(P), None, ALU.mult))
                    for j, f in ((0, OFF_AS), (1, OFF_AD)):
                        step(ve.scalar_tensor_tensor(out=fld[:, f, :], in0=tcs[:, j, :], scalar=float(AW), in1=tbank[:, j, :],
                                                     op0=ALU.mult, op1=ALU.add))
                    step(ve.tensor_scalar(count[:, :], ni[:, :], -float(P - 1), None, ALU.add))
                    step(ve.memset(before_src[:, 0, :], 0.0))
                    for c in range(CH):
                        step(ve.tensor_tensor(before_src[:, c + 1, :], before_src[:, c, :], count[:, c * CH:(c + 1) * CH], ALU.add))
                    step(ve.tensor_scalar(n2_i[:, 0, :], before_src[:, CH, :], float(P - 1), None, ALU.add))
                    step(ve.tensor_scalar(n2_i[:, 1, :], n2_i[:, 0, :], 7, None, ALU.arith_shift_right))
                    step(ve.tensor_copy(n2[:, 0, :], n2_i[:, 1, :]))
                    step(ve.tensor_tensor_scan(n2[:, 1, :], one_f[:, 0:CH], n2[:, 0, :], 0.0, ALU.mult, ALU.add))
                    step(ve.tensor_tensor(n2[:, 2, :], n2[:, 1, :], n2[:, 0, :], ALU.subtract))
                    step(ve.tensor_scalar(n2[:, 3, :], n2[:, 2, :], float(P), None, ALU.mult))
                    step(ve.tensor_tensor(before_src[:, 0:CH, :], before_src[:, 0:CH, :],
                                          n2[:, 3, :].unsqueeze(1).to_broadcast([P, CH, CH]), ALU.add))
                    step(ve.scalar_tensor_tensor(out=moved[:, :], in0=starts[:, :], scalar=-float(P),
                                                 in1=before_src[:, 0:CH, :].rearrange("p s d -> p (s d)"), op0=ALU.mult, op1=ALU.add))
                    for k in range(TROWS):
                        step(ve.scalar_tensor_tensor(out=less[:, :], in0=iota_b[:, :], scalar=tb[:, k:k + 1], in1=moved[:, :],
                                                     op0=ALU.is_equal, op1=ALU.mult))
                        step(ve.tensor_reduce(fld[:, MOVED, k:k + 1], less[:, :], AX.X, ALU.add))
                    step(ve.tensor_tensor(ge[:, :, :], tile_no[:, :].unsqueeze(2).to_broadcast([P, TROWS, CH]),
                                          n2[:, 1, :].unsqueeze(1).to_broadcast([P, TROWS, CH]), ALU.is_ge))
                    step(ve.tensor_reduce(chunk2[:, 0, :], ge[:, :, :], AX.X, ALU.add))
                    step(ve.tensor_scalar(chunk2[:, 0, :], chunk2[:, 0, :], float(CH - 1), None, ALU.min))
                    step(ve.tensor_scalar(less[:, 0:nb], steps[:, 0:nb], float(APB), None, ALU.mult))
                    step(ve.tensor_tensor(ge[:, :, 0:nb], chunk2[:, 0, :].unsqueeze(2).to_broadcast([P, TROWS, nb]),
                                          less[:, 0:nb].unsqueeze(1).to_broadcast([P, TROWS, nb]), ALU.is_ge))
                    step(ve.tensor_reduce(chunk2[:, 1, :], ge[:, :, 0:nb], AX.X, ALU.add))
                    step(ve.tensor_scalar(chunk2[:, 1, :], chunk2[:, 1, :], float(BANK - APB * AW), None, ALU.mult))
                    step(ve.tensor_scalar(fld[:, OFF_GD2, :], chunk2[:, 0, :], float(TD), None, ALU.mult))
                    step(ve.scalar_tensor_tensor(out=fld[:, OFF_AD2, :], in0=chunk2[:, 0, :], scalar=float(AW), in1=chunk2[:, 1, :],
                                                 op0=ALU.mult, op1=ALU.add))
                    ve.sem_inc(s_t, 1)
                    ve.wait_ge(s_t, 2)
                    ve.tensor_copy(fld_t[:, :], work[0:8 * TROWS, 3 * BANK:3 * BANK + P]).then_inc(s_c, 1)

                @block.tensor
                def _(pe):
                    pe.wait_ge(s_t, 1)
                    pe.transpose(work[0:8 * TROWS, 3 * BANK:3 * BANK + P], fld[:, :, :].rearrange("p f t -> p (f t)"),
                                 ident[:, :]).then_inc(s_t, 1)

                @block.sync
                def _(sp):
                    sp.wait_ge(s_c, 1)
                    sp.dma_start(offs_d, fld_t[:, :]).then_inc(s_o, 16)
                    sp.wait_ge(s_o, 16)
                    sp.dma_start(offs[:, :, :], offs_d[0:7 * TROWS, :].rearrange("(o f t) p -> o f (t p)", o=1, f=7)).then_inc(s_o, 16)
                    sp.wait_ge(s_o, 32)

        with ExitStack() as tmp:
            junk = sb("junk", [EP, 4, NB], BF16, tmp)
            place = sb("place", [EP, 2, SLOTS], F32, tmp)
            place_i = sb("place_i", [EP, SLOTS], I32, tmp)
            place_lane = sb("place_lane", [EP, SLOTS], I32, tmp)
            place_tile = sb("place_tile", [EP, SLOTS], I32, tmp)
            address = sb("address", [EP, 2, SLOTS], U32, tmp)
            staged = sb("staged", [EP, 2, SLOTS, REC], F32, tmp)
            halves = record[:, :, :].rearrange("p (h c) r -> p h c r", h=2)
            running = [counts[1], counts[0]]
            CELLS = 2 * SLOTS
            with nc.Block() as block:
                @block.vector
                def _(ve):
                    def mark(t, n):
                        ve.tensor_scalar(onehot[:, n % SLOTS, :], iota_b[0:EP, :],
                                         bucket[:, bass.ds(2 * RG * t + (n % 2 * HALF + n // 2), 1)], None,
                                         ALU.is_equal).then_inc(r_made, 1)

                    mark(0, 0)
                    mark(0, 1)
                    with ve.Fori(0, EC // CELLS) as t:
                        for n in range(CELLS):
                            mark(t, n + 2)
                            g, k = n // SLOTS, n % SLOTS
                            at = (k % 2) * RG + k // 2
                            ve.wait_ge(r_ready, CELLS * t + n + 1)
                            ve.wait_ge(r_made, CELLS * t + n + 1)
                            ve.tensor_tensor_reduce(junk[:, n % 4, :], onehot[:, k, :], running[k % 2][0:EP, 0:NB], 1.0, 0.0, ALU.mult,
                                                    ALU.add, place[:, g, at:at + 1]).then_inc(r_read, 1)
                            if k < SLOTS - 1:
                                continue
                            ve.wait_ge(r_read, CELLS * t + (g + 1) * SLOTS + 2)
                            ve.tensor_copy(place_i[:, :], place[:, g, :]).then_inc(r_step, 1)
                            ve.wait_ge(r_step, 6 * t + 3 * g + 1)
                            ve.tensor_scalar(place_lane[:, :], place_i[:, :], P - 1, None, ALU.bitwise_and).then_inc(r_step, 1)
                            ve.tensor_scalar(place_tile[:, :], place_i[:, :], 7, None, ALU.arith_shift_right).then_inc(r_step, 1)
                            ve.wait_ge(r_step, 6 * t + 3 * g + 3)
                            ve.wait_ge(r_free[g], t + 1)
                            ve.scalar_tensor_tensor(out=address[:, g, :], in0=place_lane[:, :], scalar=float(TILES),
                                                    in1=place_tile[:, :], op0=ALU.mult, op1=ALU.add)
                            ve.tensor_copy(staged[:, g, :, :].rearrange("p (h c) r -> p h c r", h=2),
                                           halves[:, :, bass.ds(2 * RG * t + RG * g, RG), :]).then_inc(r_staged[g], 1)

                @block.tensor
                def _(pe):
                    def add(which, n):
                        to, ones_of = running[n % 2], onehot[:, n % SLOTS, :]
                        pe.matmul(to[:, 0:BANK], which, ones_of[:, 0:BANK], start=False, stop=False, skip_group_check=True)
                        return pe.matmul(to[:, BANK:NB], which, ones_of[:, BANK:NB], start=False, stop=False, skip_group_check=True)

                    for half, to in enumerate(running):
                        for b in range(2):
                            lo, hi = b * BANK, min((b + 1) * BANK, NB)
                            if half == 0:
                                pe.matmul(to[:, b * BANK:(b + 1) * BANK], zeros[:, 0:P], zeros[:, :], start=True, stop=True)
                            for part in (base_hi, base_lo):
                                pe.matmul(to[:, lo:hi], ones[0:1, :], part[0:1, lo:hi], start=False, stop=False, skip_group_check=True)
                    with pe.Fori(0, EC // CELLS) as t:
                        for n in range(CELLS):
                            pe.wait_ge(r_read, CELLS * t + n + 1)
                            add(notbefore[0:EP, :], n - 2)
                            pe.wait_ge(r_made, CELLS * t + n + 1)
                            add(before[0:EP, :], n).then_inc(r_ready, 1)

                @block.gpsimd
                def _(gp):
                    with gp.Fori(0, EC // CELLS) as t:
                        for g in range(2):
                            gp.wait_ge(r_staged[g], t + 1)
                            gp.sem_inc(past, 1)
                            for k in range(SLOTS):
                                gp.indirect_dma_start(out=rec, out_offset=bass.IndirectOffsetOnAxis(ap=address[:, g, k:k + 1], axis=0),
                                                      in_=staged[:, g, k, :], in_offset=None).then_inc(r_sent[g], 16)

                @block.scalar
                def _(ac):
                    with ac.Fori(0, EC // CELLS) as t:
                        for g in range(2):
                            ac.wait_ge(r_sent[g], 16 * SLOTS * t + 16 * SLOTS)
                            ac.sem_inc(r_free[g], 1)

    with ExitStack() as tmp:
        allrec = sb("allrec", [P, TILES, REC], F32, tmp)
        row_sb = sb("row_sb", [P, 2, 3 * P], F16, tmp)
        moved_by = sb("moved_by", [P, TILES], I32, tmp)
        own_place = sb("own_place", [P, TILES], F32, tmp)
        past_end = sb("past_end", [P, TILES], F32, tmp)
        place2 = sb("place2", [P, 3, TILES], I32, tmp)
        s_l, s_m, s_p, s_v2 = sem("s_l"), sem("s_m"), sem("s_p"), sem("s_v2")
        s_tp = [sem(f"s_tp{s}") for s in range(2)]
        s_cp = [sem(f"s_cp{s}") for s in range(2)]
        s_wr = [sem(f"s_wr{s}") for s in range(2)]
        spans = [(a, min(a + P, TILES)) for a in range(0, TILES, P)]
        with nc.Block() as block:
            @block.sync
            def _(sp):
                sp.dma_start(moved_by[:, :], offs_d[MOVED * TROWS:(MOVED + 1) * TROWS, :].rearrange("(o t) p -> o (t p)", o=1)[:, 0:TILES]
                             .to_broadcast([P, TILES])).then_inc(s_m, 16)
                sp.dma_start(allrec[:, :, :], rec.rearrange("(p t) r -> p t r", p=P)).then_inc(s_l, 16)
                for n, (a, b) in enumerate(spans):
                    sp.wait_ge(s_cp[n % 2], n // 2 + 1)
                    sp.dma_start(rows[:, a:b, :].rearrange("f t e -> t f e"),
                                 row_sb[0:b - a, n % 2, :].rearrange("t (f e) -> t f e", f=3)).then_inc(s_wr[n % 2], 16)
                for s in range(2):
                    sp.wait_ge(s_wr[s], 16 * ((len(spans) + 1 - s) // 2))

            @block.tensor
            def _(pe):
                pe.wait_ge(s_l, 16)
                for n, (a, b) in enumerate(spans):
                    if n >= 2:
                        pe.wait_ge(s_cp[n % 2], n // 2)
                    for f in range(3):
                        mm = pe.transpose(work[0:b - a, (n % 2) * BANK + f * P:(n % 2) * BANK + (f + 1) * P],
                                          allrec[:, a:b, f], ident[:, :])
                    mm.then_inc(s_tp[n % 2], 1)

            @block.scalar
            def _(ac):
                for n, (a, b) in enumerate(spans):
                    ac.wait_ge(s_tp[n % 2], n // 2 + 1)
                    if n >= 2:
                        ac.wait_ge(s_wr[n % 2], 16 * (n // 2))
                    ac.copy(row_sb[0:b - a, n % 2, :], work[0:b - a, (n % 2) * BANK:(n % 2) * BANK + 3 * P]).then_inc(s_cp[n % 2], 1)

            @block.vector
            def _(ve):
                ve.wait_ge(s_l, 16)
                ve.tensor_copy(src_lo[:, :], allrec[:, :, 0])
                ve.tensor_copy(dst_lo[:, :], allrec[:, :, 1])
                ve.tensor_copy(pair[:, :, 0], allrec[:, :, 1])
                ve.tensor_copy(pair[:, :, 1], allrec[:, :, 4])
                ve.tensor_copy(pair[:, :, 2], allrec[:, :, 5])
                ve.tensor_copy(pair[:, :, 3], allrec[:, :, 3])
                n = 0

                def step(op):
                    nonlocal n
                    op.then_inc(s_v2, 1)
                    n += 1
                    ve.wait_ge(s_v2, n)

                ve.wait_ge(s_m, 16)
                ve.wait_ge(s_p, 1)
                step(ve.tensor_tensor(place2[:, 0, :], moved_by[:, :], own_place[:, :], ALU.add))
                step(ve.tensor_scalar(place2[:, 0, :], place2[:, 0, :], 0.0, None, ALU.max))
                step(ve.tensor_scalar(place2[:, 1, :], place2[:, 0, :], P - 1, None, ALU.bitwise_and))
                step(ve.tensor_scalar(place2[:, 2, :], place2[:, 0, :], 7, None, ALU.arith_shift_right))
                step(ve.scalar_tensor_tensor(out=own_place[:, :], in0=place2[:, 1, :], scalar=float(TILES2), in1=place2[:, 2, :],
                                             op0=ALU.mult, op1=ALU.add))
                step(ve.tensor_tensor(own_place[:, :], own_place[:, :], past_end[:, :], ALU.subtract))
                step(ve.scalar_tensor_tensor(out=own_place[:, :], in0=allrec[:, :, 1], scalar=0.0, in1=own_place[:, :],
                                             op0=ALU.is_ge, op1=ALU.mult))
                step(ve.tensor_tensor(address2[:, :], own_place[:, :], past_end[:, :], ALU.add))

            @block.gpsimd
            def _(gp):
                gp.iota(past_end[:, :], pattern=[[P, TILES]], base=P * TILES2, channel_multiplier=1, allow_small_or_imprecise_dtypes=True)
                gp.iota(own_place[:, :], pattern=[[P, TILES]], base=0, channel_multiplier=1,
                        allow_small_or_imprecise_dtypes=True).then_inc(s_p, 1)

    edge_a = sb("edge_a", [P, TILES], F32)
    edge_b = sb("edge_b", [P, TILES2], F32)
    t_src = sb("t_src", [P, NCH, TW], BF16)
    t_dst = sb("t_dst", [P, NCH, TD], BF16)
    cat = sb("cat", [P, NCH, P], F32)
    cat2 = sb("cat2", [P, NCH, P], F32)
    t_src_f = t_src[:, :, :].rearrange("p c w -> p (c w)")
    t_dst_f = t_dst[:, :, :].rearrange("p c w -> p (c w)")
    cat_f = [c[:, :, :].rearrange("p c w -> p (c w)") for c in (cat, cat2)]

    marks = sb("marks", [P, 2, 4, G * P], BF16)
    bcast = sb("bcast", [P, U, 3, G * P], F16)
    pick = sb("pick", [P, 2, G, P], BF16)
    pick_f = sb("pick_f", [P, 2, G, P], F32)
    near = sb("near", [P, 2, G], F32)
    msg = sb("msg", [P, 2, G, 3 * (D + 1)], BF16)
    msg_f = sb("msg_f", [P, 2, G, D + 1], F32)
    small = sb("small", [P, 2, 4, G], F32)
    wide = sb("wide", [P, 2, BANK], F32)
    biases = sb("biases", [P, 8, D], F32)
    w_sb = sb("w_sb", [P, BANK], F32)
    stat = sb("stat", [P, 2, NCH], F32)
    rel_f = sb("rel_f", [P, 2, D + 2], F32)
    rel_t = sb("rel_t", [P, 2, TD], BF16)
    gath = [work[:, 2 * s * BANK:2 * (s + 1) * BANK].rearrange("p (t w) -> p t w", w=GW) for s in range(2)]
    column = {"src": src_lo, "dst": dst_lo}
    acc_off = {"src": OFF_AS, "dst": OFF_AD}
    table_most = {OFF_GS: (CH - 1) * TW, OFF_GD: (CH - 1) * TD}
    ACC_MAX = (CH - 1) * AW + (CH - 1) // APB * (BANK - APB * AW)

    def offsets(eng, field, tile, regs, most):
        eng.load(regs, offs[0:1, field, bass.ds(tile, len(regs))])
        return [eng.snap(r, min_val=0, max_val=most) for r in regs]

    def clear_acc(pe):
        for b in range(4):
            pe.matmul(acc[:, b * BANK:(b + 1) * BANK], zeros[:, 0:P], zeros[:, :], start=True, stop=True)

    m_loaded = [sem(f"m_loaded{u}") for u in range(U)]
    m_marked, m_gathered, m_msg, m_picked, m_added, m_part, m_near, m_kept, m_sum = (
        [sem(f"m_{what}{s}") for s in range(2)]
        for what in ("marked", "gathered", "msg", "picked", "added", "part", "near", "kept", "sum"))
    m_prod, m_high, m_rest, m_mid = ([sem(f"m_{what}{s}") for s in range(2)] for what in ("prod", "high", "rest", "mid"))
    m_step, m_top = sem("m_step"), sem("m_top")
    o_pair = sb("o_pair", [P, 2, U * G // 2, PAIR], F32)
    o_address = sb("o_address", [P, 2, U * G // 2], U32)
    o_staged, o_back = sem("o_staged"), sem("o_back")
    o_sent = [sem(f"o_sent{s}") for s in range(2)]
    first_ones = m_marked + m_gathered + m_msg + m_picked + m_added + m_kept + m_sum + m_prod
    pass_sems = first_ones + m_loaded + m_part + m_near + m_high + m_rest + m_mid + [m_step, m_top]
    x_in, x_tp, x_out = ([sem(f"x_{what}{s}") for s in range(2)] for what in ("in", "tp", "out"))
    counted = {"pass": 0, "linear": 0, "sent": 0, "load": 0, "row passes": 0, "stored": 0, "ve": 0, "ac": 0}

    def reorder(gp, first, turns):
        half = U * G // 2

        def batch(t, s, again):
            if again:
                gp.wait_ge(o_sent[s], 16 * half * t)
            at = bass.ds(U * G * t + half * s, half) if again else slice(half * s, half * (s + 1))
            gp.tensor_copy(o_pair[:, s, :, :], pair[:, at, :]).then_inc(o_staged, 1)
            gp.tensor_copy(o_address[:, s, :], address2[:, at]).then_inc(o_staged, 1)
            gp.wait_ge(o_staged, 4 * t + 2 * s + 2)
            gp.sem_inc(past, 1)
            for j in range(half):
                gp.indirect_dma_start(out=rec2, out_offset=bass.IndirectOffsetOnAxis(ap=o_address[:, s, j:j + 1], axis=0),
                                      in_=o_pair[:, s, j, :], in_offset=None).then_inc(o_sent[s], 16)

        if first == 0:
            for s in range(2):
                batch(0, s, False)
        with gp.Fori(max(first, 1), first + turns) as t:
            for s in range(2):
                batch(t, s, True)
        for s in range(2):
            gp.wait_ge(o_sent[s], 16 * half * (first + turns))

    def fresh_semaphores(more=()):
        with nc.Block() as block:
            @block.gpsimd
            def _(gp):
                if counted["pass"]:
                    for m in pass_sems:
                        gp.sem_clear(m)
                for m in first_ones + list(more):
                    gp.sem_inc(m, 1)
        counted["pass"] += 1

    def edge_pass(name, fields, into, width, gathers, kind, reordered=None):
        n_rows = 1 + max(f for f, _ in fields)
        high_too = fields[-1][1]
        assert fields == [(f, False) for f in range(n_rows)] + [(n_rows - 1, True)] * high_too
        row_sums = [wide[:, s, 0:G * width].rearrange("p (t w) -> p t w", t=G) for s in range(2)] if width else None
        kinds = sorted({gt[1] for gt in gathers if gt[1] is not None})
        fresh_semaphores()
        with nc.Block() as block:
            if kind == "maximum":
                @block.vector
                def _(ve):
                    ve.memset(cat[:, :, :], FAR)
                    ve.memset(cat2[:, :, :], FAR)
        with nc.Block() as block:
            @block.sync
            def _(sp):
                def load(t, u):
                    sp.dma_start(bcast[:, u, 0:n_rows, :],
                                 rows[0:n_rows, bass.ds(G * (U * t + u), G), :].rearrange("(o f) t e -> o f (t e)", o=1)
                                 .to_broadcast([P, n_rows, G * P])).then_inc(m_loaded[u], 16)

                for u in range(U):
                    load(0, u)
                with sp.Fori(1, TURNS) as t:
                    for u in range(U):
                        sp.wait_ge(m_marked[u % 2], 2 * t + u // 2)
                        load(t, u)
                for u in range(2):
                    sp.wait_ge(m_marked[u], 2 * TURNS)
                    load(TURNS, u)

            @block.vector
            def _(ve):
                def mark(t, u):
                    t, k = t + u // U, 2 * t + u // 2
                    ve.wait_ge(m_loaded[u % U], 16 * t + 16)
                    ve.wait_ge(m_gathered[u % 2], k + 1)
                    op = ve.tensor_scalar(marks[:, u % 2, 0:n_rows, :], bcast[:, u % U, 0:n_rows, :], lane[:, 0:1], None, ALU.is_equal)
                    if high_too:
                        op = ve.tensor_scalar(marks[:, u % 2, n_rows, :], bcast[:, u % U, n_rows - 1, :], lane_hi[:, 0:1], None,
                                              ALU.is_equal)
                    op.then_inc(m_marked[u % 2], 1)

                def choose(g, s, k):
                    ve.wait_ge(m_added[s], k + 1)
                    ve.tensor_tensor(pick[:, s, :, :],
                                     iota_n[:, :].unsqueeze(1).to_broadcast([P, G, P]),
                                     column[into][:, bass.ds(G * g, G)].unsqueeze(2).to_broadcast([P, G, P]),
                                     ALU.is_equal).then_inc(m_picked[s], 1)

                def sum_parts(s):
                    return ve.tensor_reduce(row_sums[s], gath[s][:, :, 0:3 * width].rearrange("p t (q w) -> p t w q", q=3),
                                            AX.X, ALU.add)

                def maxima(g, s, k, u):
                    ve.wait_ge(m_part[s], k + 1)
                    ve.wait_ge(m_picked[s], k + 2)
                    for j in range(G):
                        if j >= 2:
                            ve.wait_ge(m_top, (G - 1) * g + j - 1)
                        elif j == 0:
                            ve.wait_ge(m_msg[1 - s], k + 1 + s)
                        top = cat_f[j % 2][:, bass.ds(top_at[G * u + j], P)]
                        op = ve.scalar_tensor_tensor(out=top, in0=pick[:, s, j, :], scalar=small[:, s, 0, j:j + 1], in1=top,
                                                     op0=ALU.subtract, op1=ALU.min)
                        op.then_inc(m_top if j < G - 1 else m_msg[s], 1)

                def group(t, u):
                    g, s, k = U * t + u, u % 2, 2 * t + u // 2
                    if kind == "plain":
                        choose(g, s, k)
                        mark(t, u + 2)
                        return
                    ve.wait_ge(m_gathered[s], k + 2)
                    if kind == "maximum":
                        ve.wait_ge(m_kept[s], k + 1)
                        ve.tensor_reduce(small[:, s, 1, :], gath[s][:, :, 0:3], AX.X, ALU.add).then_inc(m_step, 1)
                        mark(t, u + 2)
                        ve.wait_ge(m_step, g + 1)
                        ve.sem_inc(m_sum[s], 1)
                        ve.scalar_tensor_tensor(out=small[:, s, 0, :], in0=small[:, s, 1, :], scalar=0.2,
                                                in1=small[:, s, 1, :], op0=ALU.mult, op1=ALU.max).then_inc(m_part[s], 1)
                        if u > 0:
                            maxima(g - 1, 1 - s, 2 * t + (u - 1) // 2, u - 1)
                        if u == U - 1:
                            maxima(g, s, k, u)
                    else:
                        ve.wait_ge(m_prod[s], k + 1)
                        ve.tensor_reduce(small[:, s, 2, :], gath[s][:, :, 3 * width:3 * width + 3], AX.X, ALU.add).then_inc(m_step, 1)
                        mark(t, u + 2)
                        ve.wait_ge(m_step, 2 * g + 1)
                        ve.tensor_tensor(small[:, s, 0, :], edge_a[:, bass.ds(G * g, G)], small[:, s, 2, :],
                                         ALU.subtract).then_inc(m_part[s], 1)
                        sum_parts(s).then_inc(m_sum[s], 1)
                        ve.sem_inc(m_step, 1)
                        choose(g, s, k)

                if kind == "maximum":
                    max_regs = [ve.alloc_register(f"{name}_off{j}") for j in range(U * G)]
                mark(0, 0)
                mark(0, 1)
                with ve.Fori(0, TURNS) as t:
                    for u in range(U):
                        if kind == "maximum" and u == 0:
                            top_at = offsets(ve, OFF_RS, G * U * t, max_regs, (CH - 1) * P)
                        group(t, u)
                if kind == "maximum":
                    for r in max_regs:
                        ve.free_register(r)

            if reordered is not None:
                @block.gpsimd
                def _(gp):
                    reorder(gp, *reordered)

            if kind == "softmax":
                @block.gpsimd
                def _(gp):
                    def product(s, k):
                        gp.wait_ge(m_near[s], k + 1)
                        gp.wait_ge(m_msg[s], k + 1)
                        gp.wait_ge(m_sum[s], k + 2)
                        gp.sem_inc(past, 1)
                        gp.tensor_tensor(msg_f[:, s, :, 0:width], row_sums[s], small[:, s, 1, :].unsqueeze(2).to_broadcast([P, G, width]),
                                         ALU.mult).then_inc(m_prod[s], 1)

                    def rest(s, k):
                        gp.wait_ge(m_high[s], k + 1)
                        gp.tensor_tensor(msg_f[:, s, :, 0:width], msg_f[:, s, :, 0:width], msg[:, s, :, 0:width],
                                         ALU.subtract).then_inc(m_rest[s], 1)

                    def low(s, k):
                        gp.wait_ge(m_mid[s], k + 1)
                        gp.tensor_tensor(msg[:, s, :, 2 * width:3 * width], msg_f[:, s, :, 0:width], msg[:, s, :, width:2 * width],
                                         ALU.subtract).then_inc(m_msg[s], 1)

                    with gp.Fori(0, TURNS) as t:
                        for u in range(U):
                            s, k = u % 2, 2 * t + u // 2
                            product(s, k)
                            if u > 0:
                                low(1 - s, 2 * t + (u - 1) // 2)
                            rest(s, k)
                        low((U - 1) % 2, 2 * t + (U - 1) // 2)

            @block.scalar
            def _(ac):
                def middle(s, k):
                    ac.wait_ge(m_rest[s], k + 1)
                    ac.copy(msg[:, s, :, width:2 * width], msg_f[:, s, :, 0:width]).then_inc(m_mid[s], 1)

                with ac.Fori(0, TURNS) as t:
                    for u in range(U):
                        g, s, k = U * t + u, u % 2, 2 * t + u // 2
                        if kind == "plain":
                            ac.wait_ge(m_gathered[s], k + 2)
                            ac.wait_ge(m_added[s], k + 1)
                            ac.copy(msg[:, s, :, 0:3 * width], gath[s][:, :, 0:3 * width]).then_inc(m_msg[s], 1)
                        elif kind == "maximum":
                            ac.wait_ge(m_msg[s], k + 1)
                            ac.activation(near[:, s, :], column[into][:, bass.ds(G * g, G)], ACT.Copy, scale=-FAR).then_inc(m_near[s], 1)
                            ac.wait_ge(m_near[s], k + 1)
                            for j in range(G):
                                op = ac.activation(pick[:, s, j, :], iota_n[:, :], ACT.Abs, bias=near[:, s, j:j + 1], scale=FAR)
                            op.then_inc(m_picked[s], 1)
                            ac.wait_ge(m_part[s], k + 1)
                            ac.copy(edge_a[:, bass.ds(G * g, G)], small[:, s, 0, :]).then_inc(m_kept[s], 1)
                        else:
                            ac.wait_ge(m_part[s], k + 1)
                            ac.activation(small[:, s, 1, :], small[:, s, 0, :], ACT.Exp).then_inc(m_near[s], 1)
                            if u > 0:
                                middle(1 - s, 2 * t + (u - 1) // 2)
                            ac.wait_ge(m_prod[s], k + 2)
                            ac.wait_ge(m_added[s], k + 1)
                            ac.copy(msg[:, s, :, 0:width], msg_f[:, s, :, 0:width]).then_inc(m_high[s], 1)
                            if u == U - 1:
                                middle(s, k)

            @block.tensor
            def _(pe):
                regs = {f: [pe.alloc_register(f"{name}_{f}_{j}") for j in range(U * G)] for f in kinds + [acc_off[into]]}

                def gather(at, s, k):
                    pe.wait_ge(m_marked[s], k + 2)
                    pe.wait_ge((m_msg if kind == "plain" else m_sum)[s], k + 1)
                    for j in range(G):
                        for mark_n, field, table, first, n, col, start, stop in gathers:
                            if field is None:
                                rhs = table[:, first:first + n]
                            else:
                                most = TW if field == OFF_GS else TD
                                rhs = table[:, bass.ds(at[field][j], most)][:, first:first + n]
                            mm = pe.matmul(gath[s][:, j, col:col + n], marks[:, s, mark_n, j * P:(j + 1) * P], rhs,
                                           start=start, stop=stop)
                    mm.then_inc(m_gathered[s], 1)

                def add(at, s, k):
                    if kind == "maximum":
                        return
                    pe.wait_ge(m_msg[s], k + 2)
                    pe.wait_ge(m_picked[s], k + 2)
                    for j in range(G):
                        sums = acc[:, bass.ds(at[j], width)]
                        for r in range(3):
                            mm = pe.matmul(sums, pick[:, s, j, :], msg[:, s, :, r * width:(r + 1) * width][:, j, :],
                                           start=False, stop=False, skip_group_check=True)
                    mm.then_inc(m_added[s], 1)

                if kind != "maximum":
                    clear_acc(pe)
                first = {f: offsets(pe, f, 0, regs[f][0:2 * G], table_most[f]) for f in kinds}
                for u in range(2):
                    gather({f: first[f][u * G:(u + 1) * G] for f in kinds}, u, 0)
                with pe.Fori(0, TURNS) as t:
                    here = {f: offsets(pe, f, G * (U * t + 2), regs[f], table_most[f]) for f in kinds}
                    to = [0] * U * G
                    if kind != "maximum":
                        to = offsets(pe, acc_off[into], G * U * t, regs[acc_off[into]], ACC_MAX)
                    for u in range(U):
                        gather({f: here[f][u * G:(u + 1) * G] for f in kinds}, u % 2, 2 * t + u // 2 + 1)
                        add(to[u * G:(u + 1) * G], u % 2, 2 * t + u // 2)
                for rs in regs.values():
                    for r in rs:
                        pe.free_register(r)

    l_in, l_tp, l_xt, l_mm, l_out, l_sent, l_back = (
        [sem(f"l_{what}{s}") for s in range(2)] for what in ("in", "tp", "xt", "mm", "out", "sent", "back"))
    s_ld, s_ve, s_ac = sem("s_ld"), sem("s_ve"), sem("s_ac")
    with nc.Block() as block:
        @block.gpsimd
        def _(gp):
            for m in l_tp + l_in + l_xt + l_mm + l_out + l_back:
                gp.sem_inc(m, 1)
            gp.memset(edge_a[:, :], 0.0)
            gp.memset(cat[:, :, :], 0.0)

        @block.vector
        def _(ve):
            ve.memset(edge_b[:, :], 0.0)
            ve.memset(cat2[:, :, :], 0.0)
            ve.memset(t_src[:, :, :], 0.0)
            ve.memset(t_dst[:, :, :], 0.0)

    def linear(name, x, k_dim, m, finish, store=None, chunks=NCH):
        c0 = counted["linear"] + 1
        counted["linear"] += chunks // 2
        sent0 = counted["sent"]
        if store is not None:
            counted["sent"] += chunks // 2
        turned = [work[:, s * BANK:s * BANK + P] for s in range(2)]
        product = [work[:, (2 + s) * BANK:(2 + s) * BANK + m] for s in range(2)]
        with nc.Block() as block:
            @block.scalar
            def _(ac):
                with ac.Fori(0, chunks // 2) as t:
                    for s in range(2):
                        ac.wait_ge(l_tp[s], t + c0)
                        ac.copy(xt[:, s, 0, 0:k_dim], x(2 * t + s)).then_inc(l_in[s], 1)
                    for s in range(2):
                        ac.wait_ge(l_tp[s], t + c0 + 1)
                        ac.wait_ge(l_mm[s], t + c0)
                        ac.copy(xt[0:k_dim, s, 1, :], turned[s][0:k_dim, :]).then_inc(l_xt[s], 1)

            @block.tensor
            def _(pe):
                with pe.Fori(0, chunks // 2) as t:
                    for s in range(2):
                        pe.wait_ge(l_in[s], t + c0 + 1)
                        pe.wait_ge(l_xt[s], t + c0)
                        pe.transpose(turned[s], xt[:, s, 0, :], ident[:, :]).then_inc(l_tp[s], 1)
                    for s in range(2):
                        pe.wait_ge(l_xt[s], t + c0 + 1)
                        pe.wait_ge(l_out[s], t + c0)
                        pe.matmul(product[s], xt[0:k_dim, s, 1, :], w_sb[0:k_dim, 0:m], start=True, stop=True).then_inc(l_mm[s], 1)

            @block.vector
            def _(ve):
                with ve.Fori(0, chunks // 2) as t:
                    for s in range(2):
                        ve.wait_ge(l_mm[s], t + c0 + 1)
                        if store is not None:
                            ve.wait_ge(l_back[s], t + sent0 + 1)
                        finish(ve, 2 * t + s, s, product[s]).then_inc(l_out[s], 1)

            if store is not None:
                @block.sync
                def _(sp):
                    with sp.Fori(0, chunks // 2) as t:
                        for s in range(2):
                            sp.wait_ge(l_out[s], t + c0 + 1)
                            store(sp, 2 * t + s, s).then_inc(l_sent[s], 16)
                        for s in range(2):
                            sp.wait_ge(l_sent[s], 16 * (t + sent0 + 1))
                            sp.sem_inc(l_back[s], 1)

    def flat(ap):
        return ap.rearrange("p a d -> p (a d)")

    def chunk(buf, c, n):
        return flat(buf[:, bass.ds(c, 1), 0:n])

    def stepper(ve):
        def step(op):
            op.then_inc(s_ve, 1)
            counted["ve"] += 1
            ve.wait_ge(s_ve, counted["ve"])
        return step

    def split(ve, step, x, hi, mid, lo, rest):
        step(ve.tensor_copy(hi, x))
        step(ve.tensor_tensor(rest, x, hi, ALU.subtract))
        step(ve.tensor_copy(mid, rest))
        step(ve.tensor_tensor(lo, rest, mid, ALU.subtract))

    def layernorm(before):
        mean, var = stat[:, 0, :], stat[:, 1, :]
        counted["ac"] += 1
        with nc.Block() as block:
            @block.vector
            def _(ve):
                step = stepper(ve)
                before(ve, step)
                step(ve.tensor_reduce(mean, xs[:, :, :], AX.X, ALU.add))
                step(ve.tensor_scalar(mean, mean, 1.0 / D, None, ALU.mult))
                step(ve.tensor_tensor(hs[:, :, :], xs[:, :, :], mean.unsqueeze(2).to_broadcast([P, NCH, D]), ALU.subtract))
                step(ve.tensor_tensor(cat[:, :, 0:D], hs[:, :, :], hs[:, :, :], ALU.mult))
                step(ve.tensor_reduce(var, cat[:, :, 0:D], AX.X, ALU.add))
                step(ve.tensor_scalar(var, var, 1.0 / D, EPS, ALU.mult, ALU.add))
                counted["sqrt"] = counted["ve"]
                ve.wait_ge(s_ac, counted["ac"])
                step(ve.reciprocal(var, mean))
                step(ve.tensor_tensor(hs[:, :, :], hs[:, :, :], var.unsqueeze(2).to_broadcast([P, NCH, D]), ALU.mult))
                step(ve.tensor_scalar(hs[:, :, :], hs[:, :, :], 0.0, None, ALU.max))

            @block.scalar
            def _(ac):
                ac.wait_ge(s_ve, counted["sqrt"])
                ac.activation(mean, var, ACT.Sqrt).then_inc(s_ac, 1)

    def weights(loads):
        counted["load"] += 16 * len(loads)
        with nc.Block() as block:
            @block.sync
            def _(sp):
                for dest, what in loads:
                    sp.dma_start(dest, what).then_inc(s_ld, 16)
                sp.wait_ge(s_ld, counted["load"])

    banks = [b for b in range(4) if b * APB < NCH]

    W0 = D + 1
    FIRST_TURNS = 3 * TURNS // 7
    layernorm(lambda ve, step: None)
    with nc.Block() as block:
        @block.vector
        def _(ve):
            step = stepper(ve)
            step(ve.memset(t_src[:, :, 0:3 * W0], 0.0))
            step(ve.memset(t_src[:, :, D:W0], 1.0))
            split(ve, step, hs[:, :, :], t_src[:, :, 0:D], t_src[:, :, W0:W0 + D], t_src[:, :, 2 * W0:2 * W0 + D], cat[:, :, 0:D])
    edge_pass("l0", [(0, False)], "dst", W0, [(0, OFF_GS, t_src_f, 0, 3 * W0, 0, True, True)], "plain", reordered=(0, FIRST_TURNS))
    weights([(w_sb[0:D, 0:D], i["L0_gnn_W"])])
    counted["ac"] += 1
    with nc.Block() as block:
        @block.vector
        def _(ve):
            step = stepper(ve)
            for b in banks:
                lo, hi, a = bank_chunks(b)
                step(ve.tensor_tensor(hs[:, lo:hi, :], hs[:, lo:hi, :], a[:, :, 0:D], ALU.add))
                step(ve.tensor_scalar(deg[:, lo:hi], a[:, :, D], 1.0, None, ALU.max))
            counted["sqrt"] = counted["ve"]
            ve.wait_ge(s_ac, counted["ac"])
            step(ve.reciprocal(deg[:, :], stat[:, 0, :]))

        @block.scalar
        def _(ac):
            ac.wait_ge(s_ve, counted["sqrt"])
            ac.activation(stat[:, 0, :], deg[:, :], ACT.Sqrt).then_inc(s_ac, 1)
    linear("lin0", lambda c: chunk(hs, c, D), D, D,
           lambda ve, c, s, y: ve.tensor_scalar(chunk(cat, c, D), y, deg[:, bass.ds(c, 1)], None, ALU.mult))
    with nc.Block() as block:
        @block.scalar
        def _(ac):
            ac.activation(hs[:, :, :], cat[:, :, 0:D], ACT.Tanh)

    layernorm(lambda ve, step: step(ve.tensor_tensor(xs[:, :, :], xs[:, :, :], hs[:, :, :], ALU.add)))
    with nc.Block() as block:
        @block.vector
        def _(ve):
            ve.memset(cat2[:, 0:2, 0:D], 0.0)
    weights([(w_sb[0:D, 0:D], i["W_node_T"]), (w_sb[0:D, D:2 * D], i["W_rel_T"]),
             (cat2[:, 0, 0:D], i["L1_gnn_rel_emb"][0:P, :]), (cat2[0:N_REL - P, 1, 0:D], i["L1_gnn_rel_emb"][P:N_REL, :])]
            + [(biases[:, j, :], i["L1_gnn_attvec"][0:1, j * D:(j + 1) * D].to_broadcast([P, D])) for j in range(3)])
    linear("lin1", lambda c: chunk(hs, c, D), D, D, lambda ve, c, s, y: ve.tensor_copy(chunk(cat, c, D), y))
    with nc.Block() as block:
        @block.vector
        def _(ve):
            ve.tensor_copy(w_sb[0:D, 0:D], w_sb[0:D, D:2 * D])
    linear("linr", lambda c: chunk(cat2, c, D), D, D, lambda ve, c, s, y: ve.tensor_copy(chunk(rel_f, c, D), y), chunks=2)

    SP3 = 3 * W0
    with nc.Block() as block:
        @block.vector
        def _(ve):
            step = stepper(ve)
            tmp = cat2[:, :, 0:D]
            step(ve.memset(t_dst[:, :, :], 0.0))
            step(ve.memset(t_dst[:, :, D:W0], 1.0))
            step(ve.memset(rel_t[:, :, :], 0.0))
            split(ve, step, cat[:, :, 0:D], t_dst[:, :, 0:D], t_dst[:, :, W0:W0 + D], t_dst[:, :, 2 * W0:2 * W0 + D], tmp)
            split(ve, step, rel_f[:, :, 0:D], rel_t[:, :, 0:D], rel_t[:, :, W0:W0 + D], rel_t[:, :, 2 * W0:2 * W0 + D], tmp[:, 0:2, :])
            for j, (rows_in, n, table, first) in enumerate(((cat, NCH, t_src, 0), (cat, NCH, t_dst, SP3), (rel_f, 2, rel_t, SP3))):
                step(ve.tensor_tensor(tmp[:, 0:n, :], rows_in[:, 0:n, 0:D], biases[:, j, :].unsqueeze(1).to_broadcast([P, n, D]), ALU.mult))
                step(ve.tensor_reduce(stat[:, 0, 0:n], tmp[:, 0:n, :], AX.X, ALU.add))
                split(ve, step, stat[:, 0, 0:n], table[:, 0:n, first], table[:, 0:n, first + 1], table[:, 0:n, first + 2], stat[:, 1, 0:n])
    rel_tf = flat(rel_t[:, :, :])
    edge_pass("l1max", [(0, False), (1, False), (2, False), (2, True)], "src", 0, [
        (0, OFF_GS, t_src_f, 0, 3, 0, True, False), (1, OFF_GD, t_dst_f, SP3, 3, 0, False, False),
        (2, None, rel_tf, SP3, 3, 0, False, False), (3, None, rel_tf, TD + SP3, 3, 0, False, True)], "maximum",
        reordered=(FIRST_TURNS, TURNS - FIRST_TURNS))

    with nc.Block() as block:
        @block.vector
        def _(ve):
            ve.tensor_tensor(cat[:, :, :], cat[:, :, :], cat2[:, :, :], ALU.min)

        @block.gpsimd
        def _(gp):
            for m in x_tp + x_out:
                gp.sem_inc(m, 1)
    with nc.Block() as block:
        @block.scalar
        def _(ac):
            with ac.Fori(0, NCH // 2) as t:
                for s in range(2):
                    ac.wait_ge(x_tp[s], t + 1)
                    ac.copy(xt[:, s, 0, :], chunk(cat, 2 * t + s, P)).then_inc(x_in[s], 1)

        @block.tensor
        def _(pe):
            with pe.Fori(0, NCH // 2) as t:
                for s in range(2):
                    pe.wait_ge(x_in[s], t + 1)
                    pe.wait_ge(x_out[s], t + 1)
                    pe.transpose(work[:, s * BANK:s * BANK + P], xt[:, s, 0, :], ident[:, :]).then_inc(x_tp[s], 1)

        @block.vector
        def _(ve):
            with ve.Fori(0, NCH // 2) as t:
                for s in range(2):
                    ve.wait_ge(x_tp[s], t + 2)
                    ve.tensor_reduce(stat[:, 0, bass.ds(2 * t + s, 1)], work[:, s * BANK:s * BANK + P], AX.X, ALU.min).then_inc(x_out[s], 1)
    with nc.Block() as block:
        @block.vector
        def _(ve):
            step = stepper(ve)
            step(ve.tensor_scalar(stat[:, 0, :], stat[:, 0, :], -1.0, None, ALU.mult))
            split(ve, step, stat[:, 0, :], t_src[:, :, 0], t_src[:, :, 1], t_src[:, :, 2], stat[:, 1, :])
    edge_pass("l1sum", [(0, False), (1, False), (2, False), (2, True)], "src", W0, [
        (1, OFF_GD, t_dst_f, 0, 3 * W0, 0, True, False),
        (2, None, rel_tf, 0, 3 * W0, 0, False, False), (3, None, rel_tf, TD, 3 * W0, 0, False, True),
        (0, OFF_GS, t_src_f, 0, 3, SP3, True, True)], "softmax")
    with nc.Block() as block:
        @block.vector
        def _(ve):
            step = stepper(ve)
            for b in banks:
                lo, hi, a = bank_chunks(b)
                step(ve.tensor_copy(hs[:, lo:hi, :], a[:, :, 0:D]))
                step(ve.tensor_scalar(deg[:, lo:hi], a[:, :, D], 1e-12, None, ALU.add))
            step(ve.reciprocal(deg[:, :], deg[:, :]))
            step(ve.tensor_tensor(hs[:, :, :], hs[:, :, :], deg[:, :].unsqueeze(2).to_broadcast([P, NCH, D]), ALU.mult))

    layernorm(lambda ve, step: step(ve.tensor_tensor(xs[:, :, :], xs[:, :, :], hs[:, :, :], ALU.add)))
    weights([(w_sb[0:D, :].rearrange("i (r h) -> i r h", r=N_TYPE), i["L2_gnn_W"].rearrange("r i h -> i r h"))])
    xw_rows = xw.rearrange("(r n) d -> n r d", r=N_TYPE)
    linear("lin2", lambda c: chunk(hs, c, D), D, N_TYPE * D, lambda ve, c, s, y: ve.tensor_copy(wide[:, s, :], y),
           store=lambda sp, c, s: sp.dma_start(xw_rows[bass.ds(P * c, P), :, :], wide[:, s, :].rearrange("p (r d) -> p r d", r=N_TYPE)))

    spans2 = [(a, min(a + P, TILES2)) for a in range(0, TILES2, P)]
    v_turned, v_row, v_sent = ([sem(f"v_{what}{s}") for s in range(2)] for what in ("turned", "row", "sent"))
    with nc.Block() as block:
        @block.sync
        def _(sp):
            sp.dma_start(pair2[:, :, :], rec2[0:P * TILES2, :].rearrange("(p t) r -> p t r", p=P)).then_inc(o_back, 16)
            sp.wait_ge(o_back, 16)
    with nc.Block() as block:
        @block.tensor
        def _(pe):
            for n, (a, b) in enumerate(spans2):
                if n >= 2:
                    pe.wait_ge(v_row[n % 2], n // 2)
                pe.transpose(work[0:b - a, (n % 2) * BANK:(n % 2) * BANK + P], pair2[:, a:b, 0], ident[:, :]).then_inc(v_turned[n % 2], 1)

        @block.scalar
        def _(ac):
            for n, (a, b) in enumerate(spans2):
                ac.wait_ge(v_turned[n % 2], n // 2 + 1)
                if n >= 2:
                    ac.wait_ge(v_sent[n % 2], 16 * (n // 2))
                ac.copy(bcast[0:b - a, n % 2, 0, 0:P], work[0:b - a, (n % 2) * BANK:(n % 2) * BANK + P]).then_inc(v_row[n % 2], 1)

        @block.sync
        def _(sp):
            for n, (a, b) in enumerate(spans2):
                sp.wait_ge(v_row[n % 2], n // 2 + 1)
                sp.dma_start(rows2[a:b, :], bcast[0:b - a, n % 2, 0, 0:P]).then_inc(v_sent[n % 2], 16)
            for s in range(2):
                sp.wait_ge(v_sent[s], 16 * ((len(spans2) + 1 - s) // 2))

    ty_idx = sb("ty_idx", [P, 2, G], U32)
    edge_rows = pair[:, 0:U * G * (D + EH) // PAIR, :].rearrange("p t r -> p (t r)").rearrange(
        "p (u g w) -> p u g w", u=U, g=G)
    ty_chosen, ty_rows, ty_picked, ty_added = ([sem(f"ty_{what}{s}") for s in range(2)]
                                               for what in ("chosen", "rows", "picked", "added"))
    with nc.Block() as block:
        @block.gpsimd
        def _(gp):
            for m in ty_added:
                gp.sem_inc(m, 1)
    with nc.Block() as block:
        @block.vector
        def _(ve):
            with ve.Fori(0, 2 * TURNS2) as t:
                for s in range(2):
                    g = 2 * t + s
                    ve.wait_ge(ty_added[s], t + 1)
                    ve.tensor_tensor(pick_f[:, s, :, :], iota_n[:, :].unsqueeze(1).to_broadcast([P, G, P]),
                                     pair2[:, bass.ds(G * g, G), 0].unsqueeze(2).to_broadcast([P, G, P]),
                                     ALU.is_equal).then_inc(ty_picked[s], 1)

        @block.scalar
        def _(ac):
            with ac.Fori(0, 2 * TURNS2) as t:
                for s in range(2):
                    ac.wait_ge(ty_added[s], t + 1)
                    ac.copy(ty_idx[:, s, :], pair2[:, bass.ds(G * (2 * t + s), G), 1]).then_inc(ty_chosen[s], 1)

        @block.gpsimd
        def _(gp):
            with gp.Fori(0, 2 * TURNS2) as t:
                for s in range(2):
                    gp.wait_ge(ty_chosen[s], t + 1)
                    gp.sem_inc(past, 1)
                    for j in range(G):
                        gp.indirect_dma_start(out=edge_rows[:, s, j, 0:D], out_offset=None, in_=xw,
                                              in_offset=bass.IndirectOffsetOnAxis(ap=ty_idx[:, s, j:j + 1], axis=0)).then_inc(ty_rows[s], 16)

        @block.tensor
        def _(pe):
            regs = [pe.alloc_register(f"ty_r{j}") for j in range(G)]
            clear_acc(pe)
            with pe.Fori(0, 2 * TURNS2) as t:
                for s in range(2):
                    at = offsets(pe, OFF_AD2, G * (2 * t + s), regs, ACC_MAX)
                    pe.wait_ge(ty_picked[s], t + 1)
                    pe.wait_ge(ty_rows[s], 16 * G * t + 16 * G)
                    for j in range(G):
                        mm = pe.matmul(acc[:, bass.ds(at[j], D)], pick_f[:, s, j, :], edge_rows[:, s, j, 0:D], start=False, stop=False,
                                       skip_group_check=True)
                    mm.then_inc(ty_added[s], 1)
            for r in regs:
                pe.free_register(r)

    def add_sums(ve, step):
        for b in banks:
            lo, hi, a = bank_chunks(b)
            step(ve.tensor_tensor(xs[:, lo:hi, :], xs[:, lo:hi, :], a[:, :, 0:D], ALU.add))
    layernorm(add_sums)

    def conv_loads(n, k_dim, m):
        return [(w_sb[0:k_dim, 0:m], i[f"L3_gnn_Wrel{n}"]), (w_sb[k_dim:2 * k_dim, 0:m], i[f"L3_gnn_Wroot{n}"]),
                (biases[:, 0, 0:m], i[f"L3_gnn_brel{n}"].rearrange("(o m) -> o m", o=1).to_broadcast([P, m]))]

    def mlp_loads(n, k_dim):
        wf = i[f"L3_gnn_Wf{n}"]
        return [(w_sb[0:k_dim, 0:EH], wf[0:k_dim, :]), (w_sb[0:k_dim, EH:2 * EH], wf[k_dim:2 * k_dim, :]),
                (biases[:, 1, 0:EH], i[f"L3_gnn_bf{n}"].rearrange("(o m) -> o m", o=1).to_broadcast([P, EH])),
                (biases[:, 2, 0:EH], wf[2 * k_dim:2 * k_dim + 1, :].to_broadcast([P, EH])),
                (biases[:, 3, 0:EH], i[f"L3_gnn_Wr{n}"].rearrange("h o -> o h").to_broadcast([P, EH])),
                (biases[:, 3, EH:EH + 1], i[f"L3_gnn_br{n}"].rearrange("(o m) -> o m", o=1).to_broadcast([P, 1]))]

    row_idx = sb("row_idx", [P, U, G], U32)
    row_there = [sem(f"row_there{u}") for u in range(U)]
    s_rows = sem("s_rows")

    def conv_pass(width, w, mlp):
        fresh_semaphores(m_msg)
        rows0 = 16 * G * TURNS2 * counted["row passes"]
        counted["row passes"] += 1
        row_width = width + EH * (mlp is not None)
        hid = [wide[:, s, 0:G * EH].rearrange("p (t h) -> p t h", h=EH) for s in range(2)]
        ends_share = [wide[:, s, G * EH:2 * G * EH].rearrange("p (t h) -> p t h", h=EH) for s in range(2)]
        with nc.Block() as block:
            if mlp is not None:
                @block.sync
                def _(sp):
                    def load(t, u):
                        sp.dma_start(bcast[:, u, 0, :], rows2[bass.ds(G * (U * t + u), G), :].rearrange("(o t) e -> o (t e)", o=1)
                                     .to_broadcast([P, G * P])).then_inc(m_loaded[u], 16)

                    for u in range(U):
                        load(0, u)
                    with sp.Fori(1, TURNS2) as t:
                        for u in range(U):
                            sp.wait_ge(m_marked[u % 2], 2 * t + u // 2)
                            load(t, u)

            @block.scalar
            def _(ac):
                with ac.Fori(0, TURNS2) as t:
                    for u in range(U):
                        s, k = u % 2, 2 * t + u // 2
                        ac.wait_ge(m_msg[s], k + 1)
                        ac.copy(row_idx[:, u, :], pair2[:, bass.ds(G * (U * t + u), G), 2]).then_inc(m_near[s], 1)

            @block.gpsimd
            def _(gp):
                with gp.Fori(0, TURNS2) as t:
                    for u in range(U):
                        s, k = u % 2, 2 * t + u // 2
                        gp.wait_ge(m_near[s], k + 1)
                        gp.sem_inc(past, 1)
                        for j in range(G):
                            gp.indirect_dma_start(out=edge_rows[:, u, j, 0:row_width], out_offset=None,
                                                  in_=node_rows[row_width],
                                                  in_offset=bass.IndirectOffsetOnAxis(ap=row_idx[:, u, j:j + 1], axis=0)).then_inc(row_there[u], 16)

            @block.vector
            def _(ve):
                def mark(t, u):
                    s, k = u % 2, 2 * t + u // 2
                    ve.wait_ge(m_loaded[u], 16 * t + 16)
                    ve.wait_ge(m_gathered[s], k + 1)
                    ve.tensor_scalar(marks[:, s, 0, :], bcast[:, u, 0, :], lane[:, 0:1], None, ALU.is_equal).then_inc(m_marked[s], 1)

                with ve.Fori(0, TURNS2) as t:
                    for u in range(U):
                        g, s, k = U * t + u, u % 2, 2 * t + u // 2
                        tiles = bass.ds(G * g, G)
                        if mlp is not None:
                            w_row, w_out, b_out, dest = mlp
                            if u == 0:
                                mark(t, 0)
                            if u < U - 1:
                                mark(t, u + 1)
                            ve.tensor_tensor(hid[s], w(tiles).unsqueeze(2).to_broadcast([P, G, EH]),
                                             w_row.unsqueeze(1).to_broadcast([P, G, EH]), ALU.mult).then_inc(m_step, 1)
                            ve.wait_ge(m_gathered[s], k + 2)
                            ve.tensor_reduce(ends_share[s], gath[s][:, :, 0:3 * EH].rearrange("p t (q h) -> p t h q", q=3),
                                             AX.X, ALU.add).then_inc(m_sum[s], 1)
                        ve.wait_ge(m_added[s], k + 1)
                        ve.tensor_tensor(pick_f[:, s, :, :], iota_n[:, :].unsqueeze(1).to_broadcast([P, G, P]),
                                         pair2[:, tiles, 0].unsqueeze(2).to_broadcast([P, G, P]), ALU.is_equal).then_inc(m_picked[s], 1)
                        ve.wait_ge(row_there[u], 16 * G * t + (16 * G + rows0))
                        if mlp is not None:
                            ve.wait_ge(m_sum[s], k + 2)
                            ve.tensor_tensor(ends_share[s], ends_share[s], edge_rows[:, u, :, width:row_width], ALU.add).then_inc(m_step, 1)
                        ve.tensor_tensor(msg_f[:, s, :, 0:width], edge_rows[:, u, :, 0:width],
                                         w(tiles).unsqueeze(2).to_broadcast([P, G, width]), ALU.mult).then_inc(m_msg[s], 1)
                        if mlp is not None:
                            ve.wait_ge(m_step, 6 * g + 2)
                            ve.tensor_tensor(hid[s], hid[s], ends_share[s], ALU.add).then_inc(m_step, 1)
                            ve.wait_ge(m_step, 6 * g + 3)
                            ve.scalar_tensor_tensor(out=hid[s], in0=hid[s], scalar=0.0, in1=w_out.unsqueeze(1).to_broadcast([P, G, EH]),
                                                    op0=ALU.max, op1=ALU.mult).then_inc(m_step, 1)
                            ve.wait_ge(m_step, 6 * g + 4)
                            ve.tensor_reduce(small[:, s, 0, :], hid[s], AX.X, ALU.add).then_inc(m_step, 1)
                            ve.wait_ge(m_step, 6 * g + 5)
                            ve.tensor_scalar(dest[:, tiles], small[:, s, 0, :], b_out, None, ALU.add).then_inc(m_step, 1)

            @block.tensor
            def _(pe):
                gd_regs = [pe.alloc_register(f"conv{rows0}_g{j}") for j in range(U * G)]
                ad_regs = [pe.alloc_register(f"conv{rows0}_a{j}") for j in range(U * G)]

                def gather(t, u):
                    s, k = u % 2, 2 * t + u // 2
                    pe.wait_ge(m_marked[s], k + 2)
                    pe.wait_ge(m_sum[s], k + 1)
                    for j in range(G):
                        mm = pe.matmul(gath[s][:, j, 0:3 * EH], marks[:, s, 0, j * P:(j + 1) * P],
                                       t_dst_f[:, bass.ds(share_at[u * G + j], 3 * EH)], start=True, stop=True)
                    mm.then_inc(m_gathered[s], 1)

                clear_acc(pe)
                with pe.Fori(0, TURNS2) as t:
                    if mlp is not None:
                        share_at = offsets(pe, OFF_GD2, U * G * t, gd_regs, table_most[OFF_GD])
                    to = offsets(pe, OFF_AD2, U * G * t, ad_regs, ACC_MAX)
                    for u in range(U):
                        s, k = u % 2, 2 * t + u // 2
                        if mlp is not None:
                            if u == 0:
                                gather(t, 0)
                            if u < U - 1:
                                gather(t, u + 1)
                        pe.wait_ge(m_picked[s], k + 2)
                        pe.wait_ge(m_msg[s], k + 3)
                        for j in range(G):
                            mm = pe.matmul(acc[:, bass.ds(to[u * G + j], width)], pick_f[:, s, j, :], msg_f[:, s, j, 0:width],
                                           start=False, stop=False, skip_group_check=True)
                        mm.then_inc(m_added[s], 1)
                for r in gd_regs + ad_regs:
                    pe.free_register(r)

    def conv_tables(n, k_dim, net):
        if net:
            weights(mlp_loads(n, k_dim))
            linear(f"mlp{n}", lambda c: chunk(hs, c, k_dim), k_dim, 2 * EH,
                   lambda ve, c, s, y: ve.tensor_copy(chunk(cat, c, 2 * EH), y))
        table = node_rows[k_dim + EH * net].rearrange("(c p) d -> p c d", p=P)
        counted["stored"] += 16 * (1 + net)
        with nc.Block() as block:
            @block.sync
            def _(sp):
                sp.dma_start(table[:, :, 0:k_dim], hs[:, :, 0:k_dim]).then_inc(s_rows, 16)
                if net:
                    sp.dma_start(table[:, :, k_dim:k_dim + EH], cat[:, :, 0:EH]).then_inc(s_rows, 16)
                sp.wait_ge(s_rows, counted["stored"])

            if net:
                @block.vector
                def _(ve):
                    step = stepper(ve)
                    step(ve.tensor_tensor(cat[:, :, EH:2 * EH], cat[:, :, EH:2 * EH],
                                          biases[:, 1, 0:EH].unsqueeze(1).to_broadcast([P, NCH, EH]), ALU.add))
                    split(ve, step, cat[:, :, EH:2 * EH], *(t_dst[:, :, q * EH:(q + 1) * EH] for q in range(3)), cat2[:, :, 0:EH])

    def conv(n, k_dim, m):
        weights(conv_loads(n, k_dim, m))
        with nc.Block() as block:
            @block.vector
            def _(ve):
                step = stepper(ve)
                for b in banks:
                    lo, hi, a = bank_chunks(b)
                    step(ve.tensor_copy(cat[:, lo:hi, 0:k_dim], a[:, :, 0:k_dim]))
                step(ve.tensor_copy(cat[:, :, k_dim:2 * k_dim], hs[:, :, 0:k_dim]))
        linear(f"conv{n}", lambda c: chunk(cat, c, 2 * k_dim), 2 * k_dim, m,
               lambda ve, c, s, y: ve.tensor_tensor(chunk(hs, c, m), y, biases[:, 0, 0:m], ALU.add))
        with nc.Block() as block:
            @block.vector
            def _(ve):
                ve.tensor_scalar(hs[:, :, 0:m], hs[:, :, 0:m], 0.0, None, ALU.max)

    for n, k_dim, m, w, dest in ((1, D, H1, lambda tiles: pair2[:, tiles, 3], edge_a),
                                 (2, H1, D, lambda tiles: edge_a[:, tiles], edge_b)):
        conv_tables(n, k_dim, True)
        conv_pass(k_dim, w, (biases[:, 2, 0:EH], biases[:, 3, 0:EH], biases[:, 3, EH:EH + 1], dest))
        conv(n, k_dim, m)
    conv_tables(3, D, False)
    conv_pass(D, lambda tiles: edge_b[:, tiles], None)
    conv(3, D, D)
    with nc.Block() as block:
        @block.vector
        def _(ve):
            ve.tensor_tensor(xs[:, :, :], xs[:, :, :], hs[:, :, :], ALU.add)
    s_out = sem("s_out")
    with nc.Block() as block:
        @block.sync
        def _(sp):
            sp.dma_start(out[0:FULL * P, :].rearrange("(c p) d -> p c d", p=P), xs[:, 0:FULL, :]).then_inc(s_out, 16)
            sp.dma_start(out[FULL * P:N_NODES, :], xs[0:TAIL, FULL, :]).then_inc(s_out, 16)
            sp.wait_ge(s_out, 32)


def kernel(**inputs):
    import numpy as np
    import concourse.bacc as bacc
    from concourse import mybir
    from concourse.bass_utils import run_bass_kernel_spmd

    host = {name: np.ascontiguousarray(a) for name, a in inputs.items()}
    host["W_node_T"] = np.ascontiguousarray(host.pop("L1_gnn_W_node").T)
    host["W_rel_T"] = np.ascontiguousarray(host.pop("L1_gnn_W_rel").T)
    nc = bacc.Bacc("TRN2", target_bir_lowering=False, num_devices=1)
    arrays, aps = {}, {}
    for name, a in host.items():
        arrays[f"in_{name}"] = a
        aps[name] = nc.dram_tensor(f"in_{name}", a.shape, mybir.dt.from_np(a.dtype), kind="ExternalInput").ap()
    out = nc.dram_tensor("out", (N_NODES, D), mybir.dt.float32, kind="ExternalOutput").ap()
    build(nc, aps, out)
    return run_bass_kernel_spmd(nc, [arrays], core_ids=[0]).results[0]["out"]
```
